# Optimizing a Trainium2 kernel written in Bass

```python
import numpy as np
import jax
import jax.numpy as jnp

def _softmax(x, axis=-1):
    return jax.nn.softmax(x, axis=axis)

def _gelu(x):
    return jax.nn.gelu(x, approximate=True)

def _silu(x):
    return jax.nn.silu(x)

def _sigmoid(x):
    return jax.nn.sigmoid(x)

def _layernorm(x, axis=-1, eps=1e-05):
    m = jnp.mean(x, axis=axis, keepdims=True)
    v = jnp.var(x, axis=axis, keepdims=True)
    return (x - m) / jnp.sqrt(v + eps)

def _scatter_add(tgt, idx, src, axis=0):
    return tgt.at[idx].add(src)

def _segment_sum(src, seg, n):
    return jax.ops.segment_sum(src, seg, n)
kernel_name = 'mk_adj_resnorm_d4_adj_r2_da83ca'

def setup_inputs(seed: int=0):
    np.random.seed(seed)
    _w = jnp.asarray

    def _rec_inputs():
        import jax
        import jax.numpy as jnp
        _gk = jax.random.key(seed)
        x = -0.0004039 + 1 * jax.random.normal(jax.random.fold_in(_gk, 1), (64, 128, 384), jnp.float32)
        _a = jax.random.bernoulli(jax.random.fold_in(_gk, 2), 0.015625, (64, 128, 128))
        _af = _a.astype(jnp.float32)
        adj = _af
        return (x, adj)
    x, adj = _rec_inputs()

    def _L0_gnn_setup():
        import jax, jax.numpy as jnp
        import numpy as np
        B, S, H, L = (32, 256, 384, 2)

        def _layer_norm(z, a, b, eps=0.001):
            mu = jnp.mean(z, axis=-1, keepdims=True)
            sigma = jnp.std(z, axis=-1, keepdims=True, ddof=1)
            return (z - mu) / (sigma + eps) * a + b
        key = jax.random.key(seed)
        ks = jax.random.split(key, 6)
        hidden_state = jax.random.normal(ks[0], (B, S, H), dtype=jnp.float32)
        adjacency_matrix = (jax.random.uniform(ks[1], (B, S, S)) < 0.2).astype(jnp.float32)
        W_left = 0.05 * jax.random.normal(ks[2], (L, H, H), dtype=jnp.float32)
        W_right = 0.05 * jax.random.normal(ks[3], (L, H, H), dtype=jnp.float32)
        W_lin = 0.05 * jax.random.normal(ks[4], (L, H, H), dtype=jnp.float32)
        b_lin = jnp.zeros((L, H), dtype=jnp.float32)
        ln_a = jnp.ones((L, H), dtype=jnp.float32)
        ln_b = jnp.zeros((L, H), dtype=jnp.float32)
        return {'hidden_state': hidden_state, 'adjacency_matrix': adjacency_matrix, 'W_left': W_left, 'W_right': W_right, 'W_lin': W_lin, 'b_lin': b_lin, 'ln_a': ln_a, 'ln_b': ln_b}
    _L0_gnn_all = _L0_gnn_setup()
    _L0_gnn_in = {k: v for k, v in _L0_gnn_all.items() if k in ('W_left', 'W_right', 'W_lin', 'b_lin', 'ln_a', 'ln_b')}
    del _L0_gnn_all

    def _L1_gnn_setup():
        import jax, jax.numpy as jnp
        import numpy as np
        LN_EPS = 1e-12

        def _digcn_forward(hidden_state, adjacency_matrix, Wl, bl, Ws, bs, Wr, br, ln_w, ln_b):
            B, S, D = hidden_state.shape
            temper = jnp.asarray(D, jnp.float32) ** 0.5
            i = jnp.arange(S)
            upper = (i[None, :] > i[:, None]).astype(hidden_state.dtype)
            lower = (i[None, :] < i[:, None]).astype(hidden_state.dtype)

            def layer(h, params):
                wl, b_l, ws, b_s, wr, b_r, g, beta = params
                u = jnp.einsum('bid,bjd->bij', h, h) / temper
                a = jax.nn.softmax(u, axis=-1)
                delta = a * adjacency_matrix
                attn = delta / (jnp.sum(delta, axis=-1, keepdims=True) + 1e-10)
                hl = h @ wl.T + b_l
                hs = h @ ws.T + b_s
                hr = h @ wr.T + b_r
                diag_a = jnp.diagonal(attn, axis1=1, axis2=2)
                ctx = jnp.einsum('bij,bjd->bid', attn * upper, hl) + diag_a[..., None] * hs + jnp.einsum('bij,bjd->bid', attn * lower, hr)
                mean = ctx.mean(-1, keepdims=True)
                var = ctx.var(-1, keepdims=True)
                o = (ctx - mean) / jnp.sqrt(var + LN_EPS) * g + beta
                return (jax.nn.relu(o), None)
            out, _ = jax.lax.scan(layer, hidden_state, (Wl, bl, Ws, bs, Wr, br, ln_w, ln_b))
            return out
        key = jax.random.key(seed)
        ks = jax.random.split(key, 6)
        B, S, D, L = (8, 512, 384, 2)
        scale = (1.0 / D) ** 0.5
        hidden_state = jax.random.normal(ks[0], (B, S, D), jnp.float32)
        adjacency_matrix = (jax.random.uniform(ks[1], (B, S, S)) < 0.05).astype(jnp.float32)
        Wl = jax.random.normal(ks[2], (L, D, D), jnp.float32) * scale
        Ws = jax.random.normal(ks[3], (L, D, D), jnp.float32) * scale
        Wr = jax.random.normal(ks[4], (L, D, D), jnp.float32) * scale
        bl = jnp.zeros((L, D), jnp.float32)
        bs = jnp.zeros((L, D), jnp.float32)
        br = jnp.zeros((L, D), jnp.float32)
        ln_w = jnp.ones((L, D), jnp.float32)
        ln_b = jnp.zeros((L, D), jnp.float32)
        return dict(hidden_state=hidden_state, adjacency_matrix=adjacency_matrix, Wl=Wl, bl=bl, Ws=Ws, bs=bs, Wr=Wr, br=br, ln_w=ln_w, ln_b=ln_b)
    _L1_gnn_all = _L1_gnn_setup()
    _L1_gnn_in = {k: v for k, v in _L1_gnn_all.items() if k in ('Wl', 'bl', 'Ws', 'bs', 'Wr', 'br', 'ln_w', 'ln_b')}
    del _L1_gnn_all

    def _L2_gnn_setup():
        import jax, jax.numpy as jnp
        import numpy as np
        NUM_HEADS = 12
        HIDDEN = 384
        HEAD = HIDDEN // NUM_HEADS
        SCALE = HIDDEN ** (-0.5)
        key = jax.random.key(seed)
        ks = jax.random.split(key, 8)
        B, N = (16, 256)
        std = HIDDEN ** (-0.5)
        return {'x': jax.random.normal(ks[0], (B, N, HIDDEN), dtype=jnp.float32), 'encoding_bias': jax.random.normal(ks[1], (B, N, N), dtype=jnp.float32), 'Wq': jax.random.normal(ks[2], (HIDDEN, HIDDEN), dtype=jnp.float32) * std, 'Wk': jax.random.normal(ks[3], (HIDDEN, HIDDEN), dtype=jnp.float32) * std, 'Wv': jax.random.normal(ks[4], (HIDDEN, HIDDEN), dtype=jnp.float32) * std, 'bv': jax.random.normal(ks[5], (HIDDEN,), dtype=jnp.float32) * 0.01, 'Wo': jax.random.normal(ks[6], (HIDDEN, HIDDEN), dtype=jnp.float32) * std, 'bo': jax.random.normal(ks[7], (HIDDEN,), dtype=jnp.float32) * 0.01}
    _L2_gnn_all = _L2_gnn_setup()
    _L2_gnn_in = {k: v for k, v in _L2_gnn_all.items() if k in ('Wq', 'Wk', 'Wv', 'bv', 'Wo', 'bo')}
    del _L2_gnn_all

    def _L3_gnn_setup():
        import jax, jax.numpy as jnp
        import numpy as np
        B, L, H = (8, 1024, 384)
        LN_EPS = 1e-12
        key = jax.random.key(seed)
        ks = jax.random.split(key, 10)
        hidden_state = jax.random.normal(ks[0], (B, L, H), dtype=jnp.float32)
        adjacency = jax.random.randint(ks[1], (B, L, L), 0, 2).astype(jnp.float32)
        bound = 1.0 / np.sqrt(H)
        W_left = jax.random.normal(ks[2], (H, H), dtype=jnp.float32) * np.sqrt(2.0 / (H + H))
        b_left = jax.random.uniform(ks[3], (H,), minval=-bound, maxval=bound, dtype=jnp.float32)
        W_self = jax.random.normal(ks[4], (H, H), dtype=jnp.float32) * np.sqrt(2.0 / (H + H))
        b_self = jax.random.uniform(ks[5], (H,), minval=-bound, maxval=bound, dtype=jnp.float32)
        W_right = jax.random.normal(ks[6], (H, H), dtype=jnp.float32) * np.sqrt(2.0 / (H + H))
        b_right = jax.random.uniform(ks[7], (H,), minval=-bound, maxval=bound, dtype=jnp.float32)
        gamma = jnp.ones((H,), dtype=jnp.float32)
        beta = jnp.zeros((H,), dtype=jnp.float32)
        return {'hidden_state': hidden_state, 'adjacency': adjacency, 'W_left': W_left, 'b_left': b_left, 'W_self': W_self, 'b_self': b_self, 'W_right': W_right, 'b_right': b_right, 'gamma': gamma, 'beta': beta}
    _L3_gnn_all = _L3_gnn_setup()
    _L3_gnn_in = {k: v for k, v in _L3_gnn_all.items() if k in ('W_left', 'b_left', 'W_self', 'b_self', 'W_right', 'b_right', 'gamma', 'beta')}
    del _L3_gnn_all
    return {'x': x, 'adj': adj, 'L0_gnn_W_left': _L0_gnn_in['W_left'], 'L0_gnn_W_right': _L0_gnn_in['W_right'], 'L0_gnn_W_lin': _L0_gnn_in['W_lin'], 'L0_gnn_b_lin': _L0_gnn_in['b_lin'], 'L0_gnn_ln_a': _L0_gnn_in['ln_a'], 'L0_gnn_ln_b': _L0_gnn_in['ln_b'], 'L1_gnn_Wl': _L1_gnn_in['Wl'], 'L1_gnn_bl': _L1_gnn_in['bl'], 'L1_gnn_Ws': _L1_gnn_in['Ws'], 'L1_gnn_bs': _L1_gnn_in['bs'], 'L1_gnn_Wr': _L1_gnn_in['Wr'], 'L1_gnn_br': _L1_gnn_in['br'], 'L1_gnn_ln_w': _L1_gnn_in['ln_w'], 'L1_gnn_ln_b': _L1_gnn_in['ln_b'], 'L2_gnn_Wq': _L2_gnn_in['Wq'], 'L2_gnn_Wk': _L2_gnn_in['Wk'], 'L2_gnn_Wv': _L2_gnn_in['Wv'], 'L2_gnn_bv': _L2_gnn_in['bv'], 'L2_gnn_Wo': _L2_gnn_in['Wo'], 'L2_gnn_bo': _L2_gnn_in['bo'], 'L3_gnn_W_left': _L3_gnn_in['W_left'], 'L3_gnn_b_left': _L3_gnn_in['b_left'], 'L3_gnn_W_self': _L3_gnn_in['W_self'], 'L3_gnn_b_self': _L3_gnn_in['b_self'], 'L3_gnn_W_right': _L3_gnn_in['W_right'], 'L3_gnn_b_right': _L3_gnn_in['b_right'], 'L3_gnn_gamma': _L3_gnn_in['gamma'], 'L3_gnn_beta': _L3_gnn_in['beta']}

def reference(x, adj, L0_gnn_W_left, L0_gnn_W_right, L0_gnn_W_lin, L0_gnn_b_lin, L0_gnn_ln_a, L0_gnn_ln_b, L1_gnn_Wl, L1_gnn_bl, L1_gnn_Ws, L1_gnn_bs, L1_gnn_Wr, L1_gnn_br, L1_gnn_ln_w, L1_gnn_ln_b, L2_gnn_Wq, L2_gnn_Wk, L2_gnn_Wv, L2_gnn_bv, L2_gnn_Wo, L2_gnn_bo, L3_gnn_W_left, L3_gnn_b_left, L3_gnn_W_self, L3_gnn_b_self, L3_gnn_W_right, L3_gnn_b_right, L3_gnn_gamma, L3_gnn_beta):
    import jax
    import jax.numpy as jnp

    def _L0_gnn_ref(hidden_state, adjacency_matrix, W_left, W_right, W_lin, b_lin, ln_a, ln_b):
        import jax, jax.numpy as jnp
        import numpy as np
        B, S, H, L = (32, 256, 384, 2)

        def _layer_norm(z, a, b, eps=0.001):
            mu = jnp.mean(z, axis=-1, keepdims=True)
            sigma = jnp.std(z, axis=-1, keepdims=True, ddof=1)
            return (z - mu) / (sigma + eps) * a + b
        temper = float(np.sqrt(H))
        adj = adjacency_matrix
        adj_tri = jnp.triu(adj, k=1)
        diag_mask = jnp.triu(adj, k=0) - adj_tri
        h = hidden_state
        for l in range(L):
            m_left = jnp.einsum('bsh,oh->bso', h, W_left[l])
            m_right = jnp.einsum('bsh,oh->bso', h, W_right[l])
            u_left = jnp.einsum('bih,bjh->bij', h, m_left) / temper
            u_right = jnp.einsum('bih,bjh->bij', h, m_right) / temper
            u = u_left * adj_tri + u_left * diag_mask + u_right * jnp.swapaxes(adj_tri, 1, 2)
            delta_exp_u = jnp.exp(u) * adj
            attention = delta_exp_u / (jnp.sum(delta_exp_u, axis=2, keepdims=True) + 1e-10)
            h_lin = jnp.einsum('bsh,oh->bso', h, W_lin[l]) + b_lin[l]
            ctx = jnp.matmul(attention, h_lin)
            h = jax.nn.relu(_layer_norm(ctx, ln_a[l], ln_b[l]))
        return h

    def _L1_gnn_ref(hidden_state, adjacency_matrix, Wl, bl, Ws, bs, Wr, br, ln_w, ln_b):
        import jax, jax.numpy as jnp
        import numpy as np
        LN_EPS = 1e-12

        def _digcn_forward(hidden_state, adjacency_matrix, Wl, bl, Ws, bs, Wr, br, ln_w, ln_b):
            B, S, D = hidden_state.shape
            temper = jnp.asarray(D, jnp.float32) ** 0.5
            i = jnp.arange(S)
            upper = (i[None, :] > i[:, None]).astype(hidden_state.dtype)
            lower = (i[None, :] < i[:, None]).astype(hidden_state.dtype)

            def layer(h, params):
                wl, b_l, ws, b_s, wr, b_r, g, beta = params
                u = jnp.einsum('bid,bjd->bij', h, h) / temper
                a = jax.nn.softmax(u, axis=-1)
                delta = a * adjacency_matrix
                attn = delta / (jnp.sum(delta, axis=-1, keepdims=True) + 1e-10)
                hl = h @ wl.T + b_l
                hs = h @ ws.T + b_s
                hr = h @ wr.T + b_r
                diag_a = jnp.diagonal(attn, axis1=1, axis2=2)
                ctx = jnp.einsum('bij,bjd->bid', attn * upper, hl) + diag_a[..., None] * hs + jnp.einsum('bij,bjd->bid', attn * lower, hr)
                mean = ctx.mean(-1, keepdims=True)
                var = ctx.var(-1, keepdims=True)
                o = (ctx - mean) / jnp.sqrt(var + LN_EPS) * g + beta
                return (jax.nn.relu(o), None)
            out, _ = jax.lax.scan(layer, hidden_state, (Wl, bl, Ws, bs, Wr, br, ln_w, ln_b))
            return out
        return _digcn_forward(hidden_state, adjacency_matrix, Wl, bl, Ws, bs, Wr, br, ln_w, ln_b)

    def _L2_gnn_ref(x, encoding_bias, Wq, Wk, Wv, bv, Wo, bo):
        import jax, jax.numpy as jnp
        import numpy as np
        NUM_HEADS = 12
        HIDDEN = 384
        HEAD = HIDDEN // NUM_HEADS
        SCALE = HIDDEN ** (-0.5)
        B, N, _ = x.shape
        q = (x @ Wq.T).reshape(B, N, NUM_HEADS, HEAD)
        k = (x @ Wk.T).reshape(B, N, NUM_HEADS, HEAD)
        v = (x @ Wv.T + bv).reshape(B, N, NUM_HEADS, HEAD)
        a = jnp.einsum('bnhd,bmhd->bhnm', q, k) * SCALE + encoding_bias[:, None, :, :]
        pad_mask = jnp.all(a == 0, axis=-1)
        a = jnp.where(pad_mask[..., None], -jnp.inf, a)
        a = jax.nn.softmax(a, axis=-1)
        a = jnp.nan_to_num(a)
        o = jnp.einsum('bhnm,bmhd->bnhd', a, v).reshape(B, N, HIDDEN)
        return o @ Wo.T + bo

    def _L3_gnn_ref(hidden_state, adjacency, W_left, b_left, W_self, b_self, W_right, b_right, gamma, beta):
        import jax, jax.numpy as jnp
        import numpy as np
        B, L, H = (8, 1024, 384)
        LN_EPS = 1e-12
        h = hidden_state
        d = h.shape[-1]
        n = h.shape[1]
        u = jnp.einsum('bld,bmd->blm', h, h) / jnp.sqrt(jnp.asarray(d, h.dtype))
        p = jax.nn.softmax(u, axis=-1)
        delta = p * adjacency
        attn = delta / (jnp.sum(delta, axis=2, keepdims=True) + 1e-10)
        h_left = jnp.einsum('bld,ed->ble', h, W_left) + b_left
        h_self = jnp.einsum('bld,ed->ble', h, W_self) + b_self
        h_right = jnp.einsum('bld,ed->ble', h, W_right) + b_right
        i = jnp.arange(n)[:, None]
        j = jnp.arange(n)[None, :]
        attn_left = jnp.where(j > i, attn, 0.0)
        attn_right = jnp.where(j < i, attn, 0.0)
        diag_a = jnp.diagonal(attn, axis1=1, axis2=2)
        ctx = jnp.einsum('blm,bmd->bld', attn_left, h_left) + diag_a[..., None] * h_self + jnp.einsum('blm,bmd->bld', attn_right, h_right)
        mu = jnp.mean(ctx, axis=-1, keepdims=True)
        var = jnp.mean(jnp.square(ctx - mu), axis=-1, keepdims=True)
        o = (ctx - mu) / jnp.sqrt(var + LN_EPS) * gamma + beta
        return jax.nn.relu(o)
    x = _layernorm(x + _L0_gnn_ref(x, adj, L0_gnn_W_left, L0_gnn_W_right, L0_gnn_W_lin, L0_gnn_b_lin, L0_gnn_ln_a, L0_gnn_ln_b), axis=-1)
    x = _layernorm(x + _L1_gnn_ref(x, adj, L1_gnn_Wl, L1_gnn_bl, L1_gnn_Ws, L1_gnn_bs, L1_gnn_Wr, L1_gnn_br, L1_gnn_ln_w, L1_gnn_ln_b), axis=-1)
    x = _layernorm(x + _L2_gnn_ref(x, adj, L2_gnn_Wq, L2_gnn_Wk, L2_gnn_Wv, L2_gnn_bv, L2_gnn_Wo, L2_gnn_bo), axis=-1)
    x = _layernorm(x + _L3_gnn_ref(x, adj, L3_gnn_W_left, L3_gnn_b_left, L3_gnn_W_self, L3_gnn_b_self, L3_gnn_W_right, L3_gnn_b_right, L3_gnn_gamma, L3_gnn_beta), axis=-1)
    return x

_drawn_inputs = setup_inputs


def setup_inputs(seed=0):
    import zlib

    import numpy as np

    out = dict(_drawn_inputs(seed))
    spreads = {'L0_gnn_b_lin': (0.0, 0.1),
     'L0_gnn_ln_a': (1.0, 0.2),
     'L0_gnn_ln_b': (0.0, 0.1),
     'L1_gnn_bl': (0.0, 0.1),
     'L1_gnn_bs': (0.0, 0.54),
     'L1_gnn_br': (0.0, 0.1),
     'L1_gnn_ln_w': (1.0, 0.2),
     'L1_gnn_ln_b': (0.0, 0.1),
     'L3_gnn_gamma': (1.0, 0.2),
     'L3_gnn_beta': (0.0, 0.1)}
    factors = {'L2_gnn_bv': 5.147,
     'L2_gnn_bo': 5.469,
     'L3_gnn_b_left': 4.51,
     'L3_gnn_b_self': 23.91,
     'L3_gnn_b_right': 4.305}
    for name, (base, spread) in spreads.items():
        noise = np.random.default_rng([zlib.crc32(name.encode()), seed]).standard_normal(out[name].shape)
        drawn = base * np.exp(spread * noise) if base else spread * noise
        out[name] = jnp.asarray(drawn.astype(out[name].dtype))
    for name, factor in factors.items():
        out[name] = (out[name] * factor).astype(out[name].dtype)
    return out
```

```python
from contextlib import ExitStack

import concourse.bass as bass
from concourse import mybir

F32 = mybir.dt.float32
F32R = mybir.dt.float32r
ALU = mybir.AluOpType
ACT = mybir.ActivationFunctionType
AX_X = mybir.AxisListType.X

B, S, H = 64, 128, 384
P = 128
KC = H // P
GB = 2
NIT = B // (2 * GB)
HE = H + 2
BN = 6


class Memory:

    def __init__(self, nc, ctx, prefix):
        self.nc, self.ctx, self.prefix, self.sems = nc, ctx, prefix, []
        ctx.callback(self.clear)

    def clear(self):
        self.nc.clear_and_free_semaphores(self.sems)
        self.nc.all_engine_barrier()

    def sb(self, name, shape, dt=F32):
        return self.ctx.enter_context(self.nc.sbuf_tensor(self.prefix + name, [P] + shape, dt))

    def ps(self, name, shape):
        return self.ctx.enter_context(self.nc.psum_tensor(self.prefix + name, [P] + shape, F32))

    def sem(self, name):
        self.sems.append(self.nc.alloc_semaphore(self.prefix + name))
        return self.sems[-1]


def halves(eng, layers, half, last):
    n = 2 * layers
    for k in range(n):
        half(0, k, k > 0, True)
    with eng.Fori(1, NIT - 1) as it:
        for k in range(n):
            half(it, k, True, True)
    for k in range(n):
        half(NIT - 1, k, True, k < n - 1)
    last()


def rows(w):
    return w.rearrange("(c p) n -> p c n", p=P)


def split_product(pe, out, his, los, rhis, rlos, first=True, close=True):
    n = len(his)
    for c in range(n):
        pe.matmul(out, his[c], rhis[c], start=(first and c == 0), stop=False)
        pe.matmul(out, his[c], rlos[c], start=False, stop=False)
        last = pe.matmul(out, los[c], rhis[c], start=False, stop=(close and c == n - 1))
    return last


def after(eng, sem, count):
    if not isinstance(count, int) or count > 0:
        eng.wait_ge(sem, count)


def gat_phase(nc, x_in, adj, w_left, w_right, w_lin_t, b_lin, ln_a, ln_b, ln_a_cols, ln_b_cols, x_out):
    L = 2
    n = 2 * L
    TEMPER = float(H) ** 0.5
    with ExitStack() as ctx:
        m = Memory(nc, ctx, "g0_")
        raw = m.sb("raw", [3 * L, KC, H])
        w_hi = m.sb("w_hi", [3 * L, KC, H], F32R)
        w_lo = m.sb("w_lo", [3 * L, KC, H], F32R)
        b_raw = m.sb("b_raw", [L, H])
        b_rnd = m.sb("b_rnd", [L, H], F32R)
        b_parts = m.sb("b_parts", [L, H], F32R)
        ones_f = m.sb("ones_f", [P])
        ones = m.sb("ones", [P], F32R)
        ident = m.sb("ident", [P])
        half_c = m.sb("half_c", [GB])
        mhalf_c = m.sb("mhalf_c", [GB])
        a_cols = m.sb("a_cols", [KC])
        b_cols = m.sb("b_cols", [KC])
        a_row = m.sb("a_row", [H])
        b_row = m.sb("b_row", [H])
        xin = [m.sb(f"xin{p}", [GB, H]) for p in range(2)]
        adjin = [m.sb(f"adjin{p}", [GB, S]) for p in range(2)]
        xres = [m.sb(f"xres{p}", [GB, H]) for p in range(2)]
        adj_t = [m.sb(f"adj_t{p}", [GB, S]) for p in range(2)]
        masks = [m.sb(f"masks{p}", [GB, 2, S]) for p in range(2)]
        h_f = m.sb("h_f", [KC, GB, S])
        h_hi = [m.sb(f"h_hi{p}", [KC, GB, S], F32R) for p in range(2)]
        h_lo = [m.sb(f"h_lo{p}", [KC, GB, S], F32R) for p in range(2)]
        g_hi = m.sb("g_hi", [KC, 2, GB, S], F32R)
        g_lo = m.sb("g_lo", [KC, 2, GB, S], F32R)
        v_hi = m.sb("v_hi", [GB, HE], F32R)
        v_lo = m.sb("v_lo", [GB, HE], F32R)
        um = m.sb("um", [GB, 2, S])
        ua = m.sb("ua", [GB, S])
        e_s = m.sb("e_s", [GB, S])
        ea = m.sb("ea", [GB, S])
        e_hi = m.sb("e_hi", [GB, S], F32R)
        e_lo = m.sb("e_lo", [GB, S], F32R)
        den = m.sb("den", [GB])
        rden = m.sb("rden", [GB])
        cn = m.sb("cn", [GB, H])
        tn = m.sb("tn", [GB, H])
        t2 = m.sb("t2", [GB, H])
        t3 = m.sb("t3", [GB, H])
        y = m.sb("y", [GB, H])
        o = [m.sb(f"o{p}", [GB, H]) for p in range(2)]
        stats = m.sb("stats", [GB, BN])
        mv = m.sb("mv", [GB, 2])
        vs = m.sb("vs", [GB])
        sd = m.sb("sd", [GB])
        se = m.sb("se", [GB])
        rr = m.sb("rr", [GB])
        ystats = m.sb("ystats", [GB, BN])
        ymv = m.sb("ymv", [GB, 2])
        yv = m.sb("yv", [GB])
        yr = m.sb("yr", [GB])

        tp = m.ps("tp", [GB, 512])
        pj = m.ps("pj", [3, 512])
        us = m.ps("us", [GB, 2, S])
        cx = m.ps("cx", [GB, 512])

        w_loaded = m.sem("w_loaded")
        c_loaded = m.sem("c_loaded")
        w_hi_done = m.sem("w_hi_done")
        w_ready = m.sem("w_ready")
        consts = m.sem("consts")
        dconst = m.sem("dconst")
        pool_gate = m.sem("pool_gate")
        dve_gate = m.sem("dve_gate")
        x_loaded = [m.sem(f"x_loaded{p}") for p in range(2)]
        xin_free = [m.sem(f"xin_free{p}") for p in range(2)]
        tp_ready = m.sem("tp_ready")
        f_ready = m.sem("f_ready")
        hh_ready = m.sem("hh_ready")
        h_ready = m.sem("h_ready")
        pj_ready = m.sem("pj_ready")
        hi_ready = m.sem("hi_ready")
        pj_taken = m.sem("pj_taken")
        us_ready = m.sem("us_ready")
        um_ready = m.sem("um_ready")
        ua_ready = m.sem("ua_ready")
        e_ready = m.sem("e_ready")
        ea_ready = m.sem("ea_ready")
        eh_ready = m.sem("eh_ready")
        a_ready = m.sem("a_ready")
        cx_ready = m.sem("cx_ready")
        den_ready = m.sem("den_ready")
        rden_ready = m.sem("rden_ready")
        cn_ready = m.sem("cn_ready")
        st_ready = m.sem("st_ready")
        mv_ready = m.sem("mv_ready")
        vs_ready = m.sem("vs_ready")
        sd_ready = m.sem("sd_ready")
        se_ready = m.sem("se_ready")
        rr_ready = m.sem("rr_ready")
        tn_ready = m.sem("tn_ready")
        mask_ready = m.sem("mask_ready")
        adjt_ready = m.sem("adjt_ready")
        t2_ready = m.sem("t2_ready")
        t3_ready = m.sem("t3_ready")
        y_ready = m.sem("y_ready")
        yst_ready = m.sem("yst_ready")
        ymv_ready = m.sem("ymv_ready")
        yv_ready = m.sem("yv_ready")
        yr_ready = m.sem("yr_ready")
        o_ready = m.sem("o_ready")
        stored = [m.sem(f"stored{p}") for p in range(2)]

        NW = 3 * L
        JOBS = 5
        RING = 3

        block = ctx.enter_context(nc.Block())

        def prev_of(it, k):
            return (it, (k - 1) // 2, (k - 1) % 2) if k else (it - 1, L - 1, 1)

        def next_of(it, k):
            return (it, (k + 1) // 2, (k + 1) % 2) if k < n - 1 else (it + 1, 0, 0)

        @block.sync
        def _(sp):
            for i in range(L):
                sp.dma_start(raw[:, 3 * i], rows(w_left[i])).then_inc(w_loaded, 16)
                sp.dma_start(raw[:, 3 * i + 1], rows(w_right[i])).then_inc(w_loaded, 16)
                sp.dma_start(raw[:, 3 * i + 2], rows(w_lin_t[i])).then_inc(w_loaded, 16)
            sp.wait_ge(dconst, 1)
            sp.dma_start(b_raw[0:1], b_lin.unsqueeze(0)).then_inc(c_loaded, 16)
            sp.dma_start(b_raw[32:33], b_lin.unsqueeze(0)).then_inc(c_loaded, 16)
            sp.dma_start(a_cols[:], ln_a_cols[0]).then_inc(c_loaded, 16)
            sp.dma_start(b_cols[:], ln_b_cols[0]).then_inc(c_loaded, 16)
            sp.dma_start(a_row[:], ln_a[L - 1].partition_broadcast(P)).then_inc(c_loaded, 16)
            sp.dma_start(b_row[:], ln_b[L - 1].partition_broadcast(P)).then_inc(c_loaded, 16)

            def load(it, p):
                after(sp, xin_free[p], it)
                at = (2 * it + p) * GB
                sp.dma_start(xin[p][:], x_in[bass.ds(at, GB)].rearrange("b s h -> s b h")).then_inc(x_loaded[p], 16)
                sp.dma_start(adjin[p][:], adj[bass.ds(at, GB)].rearrange("b s t -> s b t")).then_inc(x_loaded[p], 16)

            def store(it, p):
                sp.wait_ge(o_ready, 2 * it + p + 1)
                at = (2 * it + p) * GB
                sp.dma_start(x_out[bass.ds(at, GB)].rearrange("b s h -> s b h"), o[p][:]).then_inc(stored[p], 16)

            for p in range(2):
                load(0, p)
            with sp.Fori(1, NIT) as it:
                for p in range(2):
                    load(it, p)
                    store(it - 1, p)
            for p in range(2):
                store(NIT - 1, p)
            for p in range(2):
                sp.wait_ge(stored[p], 16 * NIT + 16)

        @block.gpsimd
        def _(pool):
            pool.memset(ones_f[:], 1.0).then_inc(consts, 1)
            pool.memset(half_c[:], 0.5).then_inc(consts, 1)
            pool.memset(mhalf_c[:], -0.5).then_inc(consts, 1)
            pool.memset(ident[:], 0.0).then_inc(consts, 1)
            pool.wait_ge(consts, 4)
            pool.affine_select(out=ident[:], in_=ident[:], compare_op=ALU.not_equal, fill=1.0, base=0,
                               pattern=[[-1, P]], channel_multiplier=1).then_inc(consts, 1)
            pool.wait_ge(c_loaded, 16 * 6)

            def open_visit(it, l, p, v):
                if l == 0:
                    pool.wait_ge(adjt_ready, 2 * it + p + 1)
                    pool.sem_inc(pool_gate, 1)
                    pool.affine_select(out=masks[p][:, :, 0, :], in_=adj_t[p][:], compare_op=ALU.is_ge, fill=0.0,
                                       base=0, pattern=[[0, GB], [-1, S]], channel_multiplier=1)
                    pool.affine_select(out=masks[p][:, :, 1, :], in_=adjin[p][:], compare_op=ALU.is_gt, fill=0.0,
                                       base=0, pattern=[[0, GB], [1, S]], channel_multiplier=-1).then_inc(mask_ready, 1)
                    after(pool, y_ready, 2 * it + p - 1)
                    pool.sem_inc(pool_gate, 1)
                    pool.tensor_copy(xres[p][:], xin[p][:]).then_inc(xin_free[p], 1)

            def half(it, k, has_prev, has_next):
                v = n * it + k
                pi, pl, pp = prev_of(it, k)
                ni, nl, np_ = next_of(it, k)
                if has_prev:
                    pool.wait_ge(vs_ready, v)
                    pool.tensor_tensor(sd[:], vs[:], half_c[:], ALU.pow).then_inc(sd_ready, 1)
                    if pl == L - 1:
                        affine(pi, pp, v - 1)
                        out_norm(pi, pp)
                if has_next:
                    open_visit(ni, nl, np_, v + 1)
                pool.wait_ge(um_ready, v + 1)
                pool.tensor_tensor(ua[:], um[:, :, 0, :], um[:, :, 1, :], ALU.add).then_inc(ua_ready, 1)
                pool.wait_ge(e_ready, v + 1)
                pool.tensor_tensor(ea[:], e_s[:], adj_t[k % 2][:], ALU.mult).then_inc(ea_ready, 1)

            def affine(it, p, v):
                g = 2 * it + p
                pool.wait_ge(tn_ready, v + 1)
                pool.tensor_tensor(t2[:], tn[:], a_row[:].unsqueeze(1).broadcast_to([P, GB, H]), ALU.mult).then_inc(t2_ready, 1)
                pool.wait_ge(t2_ready, g + 1)
                pool.tensor_tensor(t3[:], t2[:], b_row[:].unsqueeze(1).broadcast_to([P, GB, H]), ALU.add).then_inc(t3_ready, 1)

            def out_norm(it, p):
                pool.wait_ge(yv_ready, 2 * it + p + 1)
                pool.tensor_tensor(yr[:], yv[:], mhalf_c[:], ALU.pow).then_inc(yr_ready, 1)

            open_visit(0, 0, 0, 0)

            def last():
                v = n * NIT
                pool.wait_ge(vs_ready, v)
                pool.tensor_tensor(sd[:], vs[:], half_c[:], ALU.pow).then_inc(sd_ready, 1)
                affine(NIT - 1, 1, v - 1)
                out_norm(NIT - 1, 1)

            halves(pool, L, half, last)

        @block.scalar
        def _(act):
            act.wait_ge(w_loaded, 16 * NW)
            for w in range(NW):
                act.activation(w_hi[:, w], raw[:, w], ACT.Copy).then_inc(w_hi_done, 1)
            act.wait_ge(c_loaded, 16 * 6)

            def open_visit(it, l, p, v):
                act.wait_ge(tp_ready, v + 1)
                if l == 0:
                    act.activation(adj_t[p][:], tp[:, :, H:512], ACT.Copy).then_inc(adjt_ready, 1)
                    for b in range(GB):
                        i = act.activation(h_f[:, :, b, :], tp[:, b, 0:H].rearrange("p (c s) -> p c s", c=KC), ACT.Copy)
                else:
                    for c in range(KC):
                        i = act.activation(h_f[:, c], tp[:, :, c * P:(c + 1) * P], ACT.Relu,
                                           bias=b_cols[:, c:c + 1], scale=a_cols[:, c:c + 1])
                i.then_inc(f_ready, 1)

            def take_hi(j, v):
                act.wait_ge(pj_ready, JOBS * v + j + 1)
                if j < KC:
                    i = act.activation(g_hi[:, j], pj[:, j % RING, :].rearrange("p (w b s) -> p w b s", w=2, b=GB), ACT.Copy)
                else:
                    i = act.activation(v_hi[:, j - KC, 0:H], pj[:, j % RING, 0:H], ACT.Copy)
                i.then_inc(hi_ready, 1)

            def close_visit(v):
                act.wait_ge(rden_ready, v + 1)
                for b in range(GB):
                    i = act.activation(cn[:, b], cx[:, b, 0:H], ACT.Copy, scale=rden[:, b:b + 1])
                i.then_inc(cn_ready, 1)

            def half(it, k, has_prev, has_next):
                v = n * it + k
                ni, nl, np_ = next_of(it, k)
                take_hi(0, v)
                if has_prev:
                    close_visit(v - 1)
                for j in range(1, KC + 1):
                    take_hi(j, v)
                if has_next:
                    open_visit(ni, nl, np_, v + 1)
                act.wait_ge(ua_ready, v + 1)
                act.activation(e_s[:], ua[:], ACT.Exp, scale=1.0 / TEMPER).then_inc(e_ready, 1)
                take_hi(KC + 1, v)

            open_visit(0, 0, 0, 0)
            halves(act, L, half, lambda: close_visit(n * NIT - 1))

        @block.vector
        def _(dve):
            dve.memset(b_raw[:], 0.0).then_inc(dconst, 1)
            for w in range(NW):
                dve.wait_ge(w_hi_done, w + 1)
                dve.tensor_tensor(w_lo[:, w], raw[:, w], w_hi[:, w].bitcast(F32), ALU.subtract).then_inc(w_ready, 1)
            dve.wait_ge(consts, 5)
            dve.tensor_copy(ones[:], ones_f[:]).then_inc(dconst, 1)
            dve.memset(v_hi[:, :, H:HE].bitcast(F32), 1.0).then_inc(dconst, 1)
            dve.memset(v_lo[:, :, H:HE].bitcast(F32), 0.0).then_inc(dconst, 1)
            dve.memset(b_parts[:].bitcast(F32), 0.0).then_inc(dconst, 1)
            dve.wait_ge(c_loaded, 16 * 6)
            dve.tensor_copy(b_rnd[:], b_raw[:]).then_inc(dconst, 1)
            dve.wait_ge(dconst, 6)
            dve.tensor_copy(b_parts[0:1], b_raw[0:1]).then_inc(dconst, 1)
            dve.tensor_tensor(b_parts[32:33], b_raw[32:33], b_rnd[32:33].bitcast(F32), ALU.subtract).then_inc(dconst, 1)
            for p in range(2):
                dve.engine_nop().then_inc(stored[p], 16)

            def open_visit(p, v):
                dve.wait_ge(f_ready, v + 1)
                dve.tensor_copy(h_hi[p][:], h_f[:]).then_inc(hh_ready, 1)
                dve.wait_ge(hh_ready, v + 1)
                dve.tensor_tensor(h_lo[p][:], h_f[:], h_hi[p][:].bitcast(F32), ALU.subtract).then_inc(h_ready, 1)

            def take_lo(j, v):
                dve.wait_ge(hi_ready, JOBS * v + j + 1)
                if j < KC:
                    i = dve.tensor_tensor(g_lo[:, j].rearrange("p w b s -> p (w b s)"), pj[:, j % RING, :],
                                          g_hi[:, j].bitcast(F32).rearrange("p w b s -> p (w b s)"), ALU.subtract)
                else:
                    i = dve.tensor_tensor(v_lo[:, j - KC, 0:H], pj[:, j % RING, 0:H],
                                          v_hi[:, j - KC, 0:H].bitcast(F32), ALU.subtract)
                i.then_inc(pj_taken, 1)

            def close_sums(v):
                dve.wait_ge(cx_ready, v + 1)
                dve.tensor_scalar(den[:].unsqueeze(2), cx[:, :, H:H + 1], 1e-10, None, ALU.add).then_inc(den_ready, 1)
                dve.wait_ge(den_ready, v + 1)
                dve.reciprocal(rden[:], den[:]).then_inc(rden_ready, 1)

            def close_stats(v):
                dve.wait_ge(cn_ready, v + 1)
                for b in range(GB):
                    dve.bn_stats(stats[:, b], cn[:, b]).then_inc(st_ready, 1)
                dve.wait_ge(st_ready, GB * (v + 1))
                dve.sem_inc(dve_gate, 1)
                for b in range(GB):
                    dve.bn_aggr(mv[:, b], stats[:, b]).then_inc(mv_ready, 1)
                dve.wait_ge(mv_ready, GB * (v + 1))
                dve.tensor_scalar(vs[:].unsqueeze(2), mv[:, :, 1:2], H / (H - 1.0), 1e-30, ALU.mult, ALU.add).then_inc(vs_ready, 1)

            def close_norm(v):
                dve.wait_ge(sd_ready, v + 1)
                dve.tensor_scalar(se[:], sd[:], 1e-3, None, ALU.add).then_inc(se_ready, 1)
                dve.wait_ge(se_ready, v + 1)
                dve.reciprocal(rr[:], se[:]).then_inc(rr_ready, 1)
                dve.wait_ge(rr_ready, v + 1)
                for b in range(GB):
                    i = dve.tensor_scalar(tn[:, b], cn[:, b], mv[:, b, 0:1], rr[:, b:b + 1], ALU.subtract, ALU.mult)
                i.then_inc(tn_ready, 1)

            def residual(it, p):
                g = 2 * it + p
                dve.wait_ge(t3_ready, g + 1)
                dve.scalar_tensor_tensor(y[:], t3[:], 0.0, xres[p][:], ALU.max, ALU.add).then_inc(y_ready, 1)
                dve.wait_ge(y_ready, g + 1)
                for b in range(GB):
                    dve.bn_stats(ystats[:, b], y[:, b]).then_inc(yst_ready, 1)
                dve.wait_ge(yst_ready, GB * (g + 1))
                dve.sem_inc(dve_gate, 1)
                for b in range(GB):
                    dve.bn_aggr(ymv[:, b], ystats[:, b]).then_inc(ymv_ready, 1)
                dve.wait_ge(ymv_ready, GB * (g + 1))
                dve.tensor_scalar(yv[:].unsqueeze(2), ymv[:, :, 1:2], 1e-5, None, ALU.add).then_inc(yv_ready, 1)

            def output(it, p):
                g = 2 * it + p
                dve.wait_ge(yr_ready, g + 1)
                dve.wait_ge(stored[p], 16 * it + 16)
                for b in range(GB):
                    i = dve.tensor_scalar(o[p][:, b], y[:, b], ymv[:, b, 0:1], yr[:, b:b + 1], ALU.subtract, ALU.mult)
                i.then_inc(o_ready, 1)

            def half(it, k, has_prev, has_next):
                v = n * it + k
                pi, pl, pp = prev_of(it, k)
                ni, nl, np_ = next_of(it, k)
                take_lo(0, v)
                if has_prev:
                    close_sums(v - 1)
                take_lo(1, v)
                if has_prev:
                    close_stats(v - 1)
                take_lo(2, v)
                if has_prev:
                    close_norm(v - 1)
                take_lo(3, v)
                if has_prev and pl == L - 1:
                    residual(pi, pp)
                if has_next:
                    open_visit(np_, v + 1)
                dve.wait_ge(us_ready, v + 1)
                dve.wait_ge(mask_ready, 2 * it + k % 2 + 1)
                dve.tensor_tensor(um[:], us[:], masks[k % 2][:], ALU.mult).then_inc(um_ready, 1)
                if has_prev and pl == L - 1:
                    output(pi, pp)
                dve.wait_ge(ea_ready, v + 1)
                dve.tensor_copy(e_hi[:], ea[:]).then_inc(eh_ready, 1)
                dve.wait_ge(eh_ready, v + 1)
                dve.tensor_tensor(e_lo[:], ea[:], e_hi[:].bitcast(F32), ALU.subtract).then_inc(a_ready, 1)
                take_lo(4, v)

            def last():
                v = n * NIT - 1
                close_sums(v)
                close_stats(v)
                close_norm(v)
                residual(NIT - 1, 1)
                output(NIT - 1, 1)

            open_visit(0, 0)
            halves(dve, L, half, last)

        @block.tensor
        def _(pe):
            def open_visit(it, l, p, v):
                after(pe, f_ready, v)
                if l == 0:
                    pe.wait_ge(x_loaded[p], 32 * it + 32)
                    src = xin[p]
                else:
                    pe.wait_ge(tn_ready, v - 1)
                    src = tn
                for b in range(GB):
                    for c in range(KC):
                        i = pe.transpose(tp[:, b, c * P:(c + 1) * P], src[:, b, c * P:(c + 1) * P], ident[:])
                    if l == 0:
                        i = pe.transpose(tp[:, b, H:512], adjin[p][:, b], ident[:])
                i.then_inc(tp_ready, 1)

            def project(j, l, p, v):
                if j == 0:
                    pe.wait_ge(h_ready, v + 1)
                before = JOBS * v + j - 2 if j >= RING else JOBS * (v - 1) + (j + 4 if j < 2 else 3)
                after(pe, pj_taken, before)
                bank = pj[:, j % RING, :]
                if j < KC:
                    for s in range(2):
                        out = bank[:, s * GB * S:(s + 1) * GB * S]
                        w = 3 * l + s
                        i = split_product(
                            pe, out, [w_hi[:, w, c, j * P:(j + 1) * P] for c in range(KC)],
                            [w_lo[:, w, c, j * P:(j + 1) * P] for c in range(KC)],
                            [h_hi[p][:, c].rearrange("p b s -> p (b s)") for c in range(KC)],
                            [h_lo[p][:, c].rearrange("p b s -> p (b s)") for c in range(KC)])
                else:
                    b, w = j - KC, 3 * l + 2
                    pe.matmul(bank[:, 0:H], ones[:], b_parts[:, l], start=True, stop=False)
                    i = split_product(
                        pe, bank[:, 0:H], [h_hi[p][:, c, b] for c in range(KC)], [h_lo[p][:, c, b] for c in range(KC)],
                        [w_hi[:, w, c] for c in range(KC)], [w_lo[:, w, c] for c in range(KC)], first=False)
                i.then_inc(pj_ready, 1)

            def scores(p, v):
                after(pe, um_ready, v)
                pe.wait_ge(pj_taken, JOBS * v + KC)
                for b in range(GB):
                    i = split_product(
                        pe, us[:, b], [h_hi[p][:, c, b] for c in range(KC)], [h_lo[p][:, c, b] for c in range(KC)],
                        [g_hi[:, c, :, b] for c in range(KC)], [g_lo[:, c, :, b] for c in range(KC)])
                i.then_inc(us_ready, 1)

            def close_visit(v):
                after(pe, cn_ready, v)
                pe.wait_ge(a_ready, v + 1)
                pe.wait_ge(pj_taken, JOBS * (v + 1))
                for b in range(GB):
                    i = split_product(pe, cx[:, b, 0:HE], [e_hi[:, b]], [e_lo[:, b]], [v_hi[:, b]], [v_lo[:, b]])
                i.then_inc(cx_ready, 1)

            def half(it, k, has_prev, has_next):
                v = n * it + k
                l, p = k // 2, k % 2
                ni, nl, np_ = next_of(it, k)
                project(0, l, p, v)
                if has_prev:
                    close_visit(v - 1)
                for j in range(1, KC + 1):
                    project(j, l, p, v)
                if has_next:
                    open_visit(ni, nl, np_, v + 1)
                scores(p, v)
                project(KC + 1, l, p, v)

            pe.wait_ge(consts, 5)
            open_visit(0, 0, 0, 0)
            pe.wait_ge(w_ready, NW)
            pe.wait_ge(dconst, 8)
            halves(pe, L, half, lambda: close_visit(n * NIT - 1))


def digcn_phase(nc, x_in, adj, w_up_t, b_up, w_self_t, b_self, w_low_t, b_low, ln_g, ln_b, ln_g_cols, ln_b_cols,
                x_out):
    L = w_up_t.shape[0]
    n = 2 * L
    TEMPER = float(H) ** 0.5
    prefix = f"g{L}_"
    with ExitStack() as ctx:
        m = Memory(nc, ctx, prefix)
        raw = m.sb("raw", [3 * L, KC, H])
        w_hi = m.sb("w_hi", [3 * L, KC, H], F32R)
        w_lo = m.sb("w_lo", [3 * L, KC, H], F32R)
        b_raw = m.sb("b_raw", [3 * L, H])
        b_rnd = m.sb("b_rnd", [3 * L, H], F32R)
        b_parts = m.sb("b_parts", [3 * L, H], F32R)
        ones_f = m.sb("ones_f", [P])
        ones = m.sb("ones", [P], F32R)
        ident = m.sb("ident", [P])
        mhalf_c = m.sb("mhalf_c", [GB])
        g_cols = m.sb("g_cols", [KC])
        b_cols = m.sb("b_cols", [KC])
        g_row = m.sb("g_row", [H])
        b_row = m.sb("b_row", [H])
        xin = [m.sb(f"xin{p}", [GB, H]) for p in range(2)]
        adjin = [m.sb(f"adjin{p}", [GB, S]) for p in range(2)]
        xres = [m.sb(f"xres{p}", [GB, H]) for p in range(2)]
        adj_d = [m.sb(f"adj_d{p}", [GB]) for p in range(2)]
        masks = [m.sb(f"masks{p}", [GB, 2, S]) for p in range(2)]
        h_f = m.sb("h_f", [KC, GB, S])
        h_hi = [m.sb(f"h_hi{p}", [KC, GB, S], F32R) for p in range(2)]
        h_lo = [m.sb(f"h_lo{p}", [KC, GB, S], F32R) for p in range(2)]
        v_hi = m.sb("v_hi", [GB, 2, HE], F32R)
        v_lo = m.sb("v_lo", [GB, 2, HE], F32R)
        vself = m.sb("vself", [GB, H])
        mx = m.sb("mx", [GB])
        nb = m.sb("nb", [GB])
        e_s = m.sb("e_s", [GB, S])
        esum = [m.sb(f"esum{p}", [GB]) for p in range(2)]
        diag = m.sb("diag", [GB])
        junk = m.sb("junk", [GB, S])
        dself = [m.sb(f"dself{p}", [GB]) for p in range(2)]
        au = m.sb("au", [GB, 2, S])
        a_hi = m.sb("a_hi", [GB, 2, S], F32R)
        a_lo = m.sb("a_lo", [GB, 2, S], F32R)
        part = m.sb("part", [GB])
        den = m.sb("den", [GB])
        dd = m.sb("dd", [GB])
        cn = m.sb("cn", [GB, H])
        tn = m.sb("tn", [GB, H])
        t2 = m.sb("t2", [GB, H])
        t3 = m.sb("t3", [GB, H])
        y = m.sb("y", [GB, H])
        o = [m.sb(f"o{p}", [GB, H]) for p in range(2)]
        stats = m.sb("stats", [GB, BN])
        mv = m.sb("mv", [GB, 2])
        vs = m.sb("vs", [GB])
        rr = m.sb("rr", [GB])
        ystats = m.sb("ystats", [GB, BN])
        ymv = m.sb("ymv", [GB, 2])
        yv = m.sb("yv", [GB])
        yr = m.sb("yr", [GB])

        tp = m.ps("tp", [GB, 512])
        pj = m.ps("pj", [3, 512])
        us = m.ps("us", [512])
        cx = m.ps("cx", [GB, 512])
        us_s = us[:, 0:GB * S].rearrange("p (b s) -> p b s", b=GB)
        us_a = us[:, :].rearrange("p (b w s) -> p b w s", b=GB, w=2)

        w_loaded = m.sem("w_loaded")
        c_loaded = m.sem("c_loaded")
        w_hi_done = m.sem("w_hi_done")
        w_ready = m.sem("w_ready")
        consts = m.sem("consts")
        dconst = m.sem("dconst")
        pool_gate = m.sem("pool_gate")
        dve_gate = m.sem("dve_gate")
        x_loaded = [m.sem(f"x_loaded{p}") for p in range(2)]
        xin_free = [m.sem(f"xin_free{p}") for p in range(2)]
        tp_ready = m.sem("tp_ready")
        f_ready = m.sem("f_ready")
        hh_ready = m.sem("hh_ready")
        h_ready = m.sem("h_ready")
        pj_ready = m.sem("pj_ready")
        hi_ready = m.sem("hi_ready")
        lo_taken = m.sem("lo_taken")
        self_taken = m.sem("self_taken")
        us_ready = m.sem("us_ready")
        mx_ready = m.sem("mx_ready")
        nb_ready = m.sem("nb_ready")
        e_ready = m.sem("e_ready")
        diag_ready = m.sem("diag_ready")
        d_ready = m.sem("d_ready")
        au_ready = m.sem("au_ready")
        at_ready = m.sem("at_ready")
        ah_ready = m.sem("ah_ready")
        a_ready = m.sem("a_ready")
        cx_ready = m.sem("cx_ready")
        part_ready = m.sem("part_ready")
        den_ready = m.sem("den_ready")
        cn_ready = m.sem("cn_ready")
        dd_ready = m.sem("dd_ready")
        st_ready = m.sem("st_ready")
        mv_ready = m.sem("mv_ready")
        vs_ready = m.sem("vs_ready")
        rr_ready = m.sem("rr_ready")
        tn_ready = m.sem("tn_ready")
        mask_ready = m.sem("mask_ready")
        adjd_ready = m.sem("adjd_ready")
        t2_ready = m.sem("t2_ready")
        t3_ready = m.sem("t3_ready")
        y_ready = m.sem("y_ready")
        yst_ready = m.sem("yst_ready")
        ymv_ready = m.sem("ymv_ready")
        yv_ready = m.sem("yv_ready")
        yr_ready = m.sem("yr_ready")
        o_ready = m.sem("o_ready")
        stored = [m.sem(f"stored{p}") for p in range(2)]

        NW = 3 * L
        RING = 3
        LO_JOBS = 2 * GB
        JOBS = 3 * GB
        ML = L - 1

        block = ctx.enter_context(nc.Block())

        def prev_of(it, k):
            return (it, (k - 1) // 2, (k - 1) % 2) if k else (it - 1, L - 1, 1)

        def next_of(it, k):
            return (it, (k + 1) // 2, (k + 1) % 2) if k < n - 1 else (it + 1, 0, 0)

        @block.sync
        def _(sp):
            for i in range(L):
                for w, a in enumerate((w_up_t, w_low_t, w_self_t)):
                    sp.dma_start(raw[:, 3 * i + w], rows(a[i])).then_inc(w_loaded, 16)
            sp.wait_ge(dconst, 1)
            for i in range(L):
                for w, a in enumerate((b_up, b_low, b_self)):
                    for r in (0, 32):
                        sp.dma_start(b_raw[r:r + 1, 3 * i + w], a[i:i + 1]).then_inc(c_loaded, 16)
            sp.dma_start(g_cols[:], ln_g_cols[0]).then_inc(c_loaded, 16)
            sp.dma_start(b_cols[:], ln_b_cols[0]).then_inc(c_loaded, 16)
            sp.dma_start(g_row[:], ln_g[L - 1].partition_broadcast(P)).then_inc(c_loaded, 16)
            sp.dma_start(b_row[:], ln_b[L - 1].partition_broadcast(P)).then_inc(c_loaded, 16)

            def load(it, p):
                after(sp, xin_free[p], it)
                at = (2 * it + p) * GB
                sp.dma_start(xin[p][:], x_in[bass.ds(at, GB)].rearrange("b s h -> s b h")).then_inc(x_loaded[p], 16)
                sp.dma_start(adjin[p][:], adj[bass.ds(at, GB)].rearrange("b s t -> s b t")).then_inc(x_loaded[p], 16)

            def store(it, p):
                sp.wait_ge(o_ready, 2 * it + p + 1)
                at = (2 * it + p) * GB
                sp.dma_start(x_out[bass.ds(at, GB)].rearrange("b s h -> s b h"), o[p][:]).then_inc(stored[p], 16)

            for p in range(2):
                load(0, p)
            with sp.Fori(1, NIT) as it:
                for p in range(2):
                    load(it, p)
                    store(it - 1, p)
            for p in range(2):
                store(NIT - 1, p)
            for p in range(2):
                sp.wait_ge(stored[p], 16 * NIT + 16)

        CONSTS = 2 * 3 * L + 4

        @block.gpsimd
        def _(pool):
            pool.memset(ones_f[:], 1.0).then_inc(consts, 1)
            pool.memset(mhalf_c[:], -0.5).then_inc(consts, 1)
            pool.memset(ident[:], 0.0).then_inc(consts, 1)
            pool.wait_ge(consts, 3)
            pool.affine_select(out=ident[:], in_=ident[:], compare_op=ALU.not_equal, fill=1.0, base=0,
                               pattern=[[-1, P]], channel_multiplier=1).then_inc(consts, 1)
            pool.wait_ge(c_loaded, 16 * CONSTS)

            def open_visit(it, l, p, v):
                if l == 0:
                    pool.wait_ge(tp_ready, v + 1)
                    pool.sem_inc(pool_gate, 1)
                    pool.affine_select(out=masks[p][:, :, 0, :], in_=adjin[p][:], compare_op=ALU.is_gt, fill=0.0,
                                       base=0, pattern=[[0, GB], [1, S]], channel_multiplier=-1)
                    pool.affine_select(out=masks[p][:, :, 1, :], in_=adjin[p][:], compare_op=ALU.is_gt, fill=0.0,
                                       base=0, pattern=[[0, GB], [-1, S]], channel_multiplier=1).then_inc(mask_ready, 1)
                    after(pool, y_ready, 2 * it + p - 1)
                    pool.wait_ge(adjd_ready, GB * (2 * it + p + 1))
                    pool.sem_inc(pool_gate, 1)
                    pool.tensor_copy(xres[p][:], xin[p][:]).then_inc(xin_free[p], 1)

            def half(it, k, has_prev, has_next):
                v = n * it + k
                pi, pl, pp = prev_of(it, k)
                ni, nl, np_ = next_of(it, k)
                pool.wait_ge(e_ready, GB * (v + 1))
                pool.wait_ge(mask_ready, 2 * it + k % 2 + 1)
                for b in range(GB):
                    i = pool.tensor_tensor(au[:, b], e_s[:, b].unsqueeze(1).broadcast_to([P, 2, S]),
                                           masks[k % 2][:, b], ALU.mult)
                i.then_inc(au_ready, 1)
                if has_prev:
                    close(pi, pl, pp, v - 1)
                if has_next:
                    open_visit(ni, nl, np_, v + 1)

            def close(it, l, p, v):
                pool.wait_ge(vs_ready, v + 1)
                pool.tensor_tensor(rr[:], vs[:], mhalf_c[:], ALU.pow).then_inc(rr_ready, 1)
                if l == L - 1:
                    g = 2 * it + p
                    pool.wait_ge(tn_ready, v + 1)
                    pool.tensor_tensor(t2[:], tn[:], g_row[:].unsqueeze(1).broadcast_to([P, GB, H]), ALU.mult).then_inc(t2_ready, 1)
                    pool.wait_ge(t2_ready, g + 1)
                    pool.tensor_tensor(t3[:], t2[:], b_row[:].unsqueeze(1).broadcast_to([P, GB, H]), ALU.add).then_inc(t3_ready, 1)
                    pool.wait_ge(yv_ready, g + 1)
                    pool.tensor_tensor(yr[:], yv[:], mhalf_c[:], ALU.pow).then_inc(yr_ready, 1)

            open_visit(0, 0, 0, 0)
            halves(pool, L, half, lambda: close(NIT - 1, L - 1, 1, n * NIT - 1))

        @block.scalar
        def _(act):
            act.wait_ge(w_loaded, 16 * NW)
            for w in range(NW):
                act.activation(w_hi[:, w], raw[:, w], ACT.Copy).then_inc(w_hi_done, 1)
            act.wait_ge(c_loaded, 16 * CONSTS)

            def open_visit(l, v):
                act.wait_ge(tp_ready, v + 1)
                if l == 0:
                    for b in range(GB):
                        i = act.activation(h_f[:, :, b, :], tp[:, b, 0:H].rearrange("p (c s) -> p c s", c=KC), ACT.Copy)
                else:
                    for c in range(KC):
                        i = act.activation(h_f[:, c], tp[:, :, c * P:(c + 1) * P], ACT.Relu,
                                           bias=b_cols[:, c:c + 1], scale=g_cols[:, c:c + 1])
                i.then_inc(f_ready, 1)

            def take_hi(j, v):
                act.wait_ge(pj_ready, JOBS * v + j + 1)
                after(act, cx_ready, v)
                act.activation(v_hi[:, j // 2, j % 2, 0:H], pj[:, j % RING, 0:H], ACT.Copy).then_inc(hi_ready, 1)

            def take_self(b, p, v):
                act.wait_ge(pj_ready, JOBS * v + LO_JOBS + b + 1)
                act.wait_ge(d_ready, v + 1)
                after(act, cn_ready, v)
                act.activation(vself[:, b], pj[:, (LO_JOBS + b) % RING, 0:H], ACT.Copy,
                               scale=dself[p][:, b:b + 1]).then_inc(self_taken, 1)

            def exps(it, l, p, v):
                act.wait_ge(us_ready, v + 1)
                after(act, au_ready, v)
                if l:
                    act.wait_ge(nb_ready, ML * 2 * it + 2 * (l - 1) + p + 1)
                for b in range(GB):
                    act.activation(e_s[:, b], us_s[:, b], ACT.Exp, scale=1.0 / TEMPER,
                                   bias=nb[:, b:b + 1] if l else 0.0,
                                   accum_out=esum[p][:, b:b + 1]).then_inc(e_ready, 1)

            def take_attention(v):
                act.wait_ge(at_ready, v + 1)
                act.activation(a_hi[:], us_a, ACT.Copy).then_inc(ah_ready, 1)

            def half(it, k, has_prev, has_next):
                v = n * it + k
                ni, nl, np_ = next_of(it, k)
                exps(it, k // 2, k % 2, v)
                for j in range(LO_JOBS):
                    take_hi(j, v)
                take_attention(v)
                if has_next:
                    open_visit(nl, v + 1)
                for b in range(GB):
                    take_self(b, k % 2, v)

            open_visit(0, 0)
            halves(act, L, half, lambda: None)

        @block.vector
        def _(dve):
            dve.memset(b_raw[:], 0.0).then_inc(dconst, 1)
            for w in range(NW):
                dve.wait_ge(w_hi_done, w + 1)
                dve.tensor_tensor(w_lo[:, w], raw[:, w], w_hi[:, w].bitcast(F32), ALU.subtract).then_inc(w_ready, 1)
            dve.wait_ge(consts, 4)
            dve.tensor_copy(ones[:], ones_f[:]).then_inc(dconst, 1)
            dve.memset(v_hi[:, :, :, H:HE].bitcast(F32), 1.0).then_inc(dconst, 1)
            dve.memset(v_lo[:, :, :, H:HE].bitcast(F32), 0.0).then_inc(dconst, 1)
            dve.memset(b_parts[:].bitcast(F32), 0.0).then_inc(dconst, 1)
            dve.wait_ge(c_loaded, 16 * CONSTS)
            dve.tensor_copy(b_rnd[:], b_raw[:]).then_inc(dconst, 1)
            dve.wait_ge(dconst, 6)
            dve.tensor_copy(b_parts[0:1], b_raw[0:1]).then_inc(dconst, 1)
            dve.tensor_tensor(b_parts[32:33], b_raw[32:33], b_rnd[32:33].bitcast(F32), ALU.subtract).then_inc(dconst, 1)
            for p in range(2):
                dve.engine_nop().then_inc(stored[p], 16)

            def open_visit(it, l, p, v):
                if l == 0:
                    dve.wait_ge(x_loaded[p], 32 * it + 32)
                    for b in range(GB):
                        dve.tensor_tensor_reduce(junk[:, b], adjin[p][:, b], ident[:], 1.0, 0.0, ALU.mult, ALU.add,
                                                 adj_d[p][:, b:b + 1]).then_inc(adjd_ready, 1)
                dve.wait_ge(f_ready, v + 1)
                dve.tensor_copy(h_hi[p][:], h_f[:]).then_inc(hh_ready, 1)
                dve.wait_ge(hh_ready, v + 1)
                dve.tensor_tensor(h_lo[p][:], h_f[:], h_hi[p][:].bitcast(F32), ALU.subtract).then_inc(h_ready, 1)

            def row_max(it, l, p, v):
                c = ML * 2 * it + 2 * (l - 1) + p
                dve.wait_ge(us_ready, v + 1)
                dve.tensor_reduce(mx[:], us_s, AX_X, ALU.max).then_inc(mx_ready, 1)
                dve.wait_ge(mx_ready, c + 1)
                dve.tensor_scalar(nb[:], mx[:], -1.0 / TEMPER, None, ALU.mult).then_inc(nb_ready, 1)

            def diagonal(it, p, v):
                dve.wait_ge(e_ready, GB * (v + 1))
                for b in range(GB):
                    dve.tensor_tensor_reduce(junk[:, b], e_s[:, b], ident[:], 1.0, 0.0, ALU.mult, ALU.add,
                                             diag[:, b:b + 1]).then_inc(diag_ready, 1)
                dve.wait_ge(diag_ready, GB * (v + 1))
                dve.wait_ge(adjd_ready, GB * (2 * it + p + 1))
                dve.tensor_tensor(dself[p][:], diag[:], adj_d[p][:], ALU.mult).then_inc(d_ready, 1)

            def take_lo(j, v):
                dve.wait_ge(hi_ready, LO_JOBS * v + j + 1)
                dve.tensor_tensor(v_lo[:, j // 2, j % 2, 0:H], pj[:, j % RING, 0:H],
                                  v_hi[:, j // 2, j % 2, 0:H].bitcast(F32), ALU.subtract).then_inc(lo_taken, 1)

            def take_attention(v):
                dve.wait_ge(ah_ready, v + 1)
                dve.tensor_tensor(a_lo[:], us_a, a_hi[:].bitcast(F32), ALU.subtract).then_inc(a_ready, 1)

            def close_sums(p, v):
                dve.wait_ge(cx_ready, v + 1)
                dve.scalar_tensor_tensor(part[:].unsqueeze(2), esum[p][:].unsqueeze(2), 1e-10, cx[:, :, H:H + 1],
                                         ALU.mult, ALU.add).then_inc(part_ready, 1)
                dve.wait_ge(self_taken, GB * (v + 1))
                dve.tensor_tensor(cn[:], cx[:, :, 0:H], vself[:], ALU.add).then_inc(cn_ready, 1)
                dve.wait_ge(part_ready, v + 1)
                dve.tensor_tensor(den[:], part[:], dself[p][:], ALU.add).then_inc(den_ready, 1)
                dve.wait_ge(den_ready, v + 1)
                dve.scalar_tensor_tensor(dd[:], den[:], 1e-12, den[:], ALU.mult, ALU.mult).then_inc(dd_ready, 1)

            def close_stats(v):
                dve.wait_ge(cn_ready, v + 1)
                for b in range(GB):
                    dve.bn_stats(stats[:, b], cn[:, b]).then_inc(st_ready, 1)
                dve.wait_ge(st_ready, GB * (v + 1))
                dve.sem_inc(dve_gate, 1)
                for b in range(GB):
                    dve.bn_aggr(mv[:, b], stats[:, b]).then_inc(mv_ready, 1)
                dve.wait_ge(mv_ready, GB * (v + 1))
                dve.wait_ge(dd_ready, v + 1)
                dve.tensor_tensor(vs[:].unsqueeze(2), mv[:, :, 1:2], dd[:].unsqueeze(2), ALU.add).then_inc(vs_ready, 1)

            def close_norm(v):
                dve.wait_ge(rr_ready, v + 1)
                for b in range(GB):
                    i = dve.tensor_scalar(tn[:, b], cn[:, b], mv[:, b, 0:1], rr[:, b:b + 1], ALU.subtract, ALU.mult)
                i.then_inc(tn_ready, 1)

            def residual(it, p):
                g = 2 * it + p
                dve.wait_ge(t3_ready, g + 1)
                dve.scalar_tensor_tensor(y[:], t3[:], 0.0, xres[p][:], ALU.max, ALU.add).then_inc(y_ready, 1)
                dve.wait_ge(y_ready, g + 1)
                for b in range(GB):
                    dve.bn_stats(ystats[:, b], y[:, b]).then_inc(yst_ready, 1)
                dve.wait_ge(yst_ready, GB * (g + 1))
                dve.sem_inc(dve_gate, 1)
                for b in range(GB):
                    dve.bn_aggr(ymv[:, b], ystats[:, b]).then_inc(ymv_ready, 1)
                dve.wait_ge(ymv_ready, GB * (g + 1))
                dve.tensor_scalar(yv[:].unsqueeze(2), ymv[:, :, 1:2], 1e-5, None, ALU.add).then_inc(yv_ready, 1)

            def output(it, p):
                g = 2 * it + p
                dve.wait_ge(yr_ready, g + 1)
                dve.wait_ge(stored[p], 16 * it + 16)
                for b in range(GB):
                    i = dve.tensor_scalar(o[p][:, b], y[:, b], ymv[:, b, 0:1], yr[:, b:b + 1], ALU.subtract, ALU.mult)
                i.then_inc(o_ready, 1)

            def half(it, k, has_prev, has_next):
                v = n * it + k
                l, p = k // 2, k % 2
                pi, pl, pp = prev_of(it, k)
                ni, nl, np_ = next_of(it, k)
                if l:
                    row_max(it, l, p, v)
                diagonal(it, p, v)
                take_lo(0, v)
                if has_prev:
                    close_sums(pp, v - 1)
                take_lo(1, v)
                if has_prev:
                    close_stats(v - 1)
                take_lo(2, v)
                if has_prev:
                    close_norm(v - 1)
                take_lo(3, v)
                take_attention(v)
                if has_next:
                    open_visit(ni, nl, np_, v + 1)
                if has_prev and pl == L - 1:
                    residual(pi, pp)
                    output(pi, pp)

            def last():
                v = n * NIT - 1
                close_sums(1, v)
                close_stats(v)
                close_norm(v)
                residual(NIT - 1, 1)
                output(NIT - 1, 1)

            open_visit(0, 0, 0, 0)
            halves(dve, L, half, last)

        @block.tensor
        def _(pe):
            def open_visit(it, l, p, v):
                after(pe, f_ready, v)
                if l == 0:
                    pe.wait_ge(x_loaded[p], 32 * it + 32)
                    src = xin[p]
                else:
                    pe.wait_ge(tn_ready, v - 1)
                    src = tn
                for b in range(GB):
                    for c in range(KC):
                        i = pe.transpose(tp[:, b, c * P:(c + 1) * P], src[:, b, c * P:(c + 1) * P], ident[:])
                i.then_inc(tp_ready, 1)

            def scores(v):
                pe.wait_ge(f_ready, v + 1)
                after(pe, a_ready, v)
                for b in range(GB):
                    for c in range(KC):
                        i = pe.matmul(us_s[:, b], h_f[:, c, b], h_f[:, c, b], start=(c == 0), stop=(c == KC - 1))
                i.then_inc(us_ready, 1)

            def project(j, l, p, v):
                if j == 0:
                    pe.wait_ge(h_ready, v + 1)
                if j in (1, 2):
                    after(pe, self_taken, GB * (v - 1) + j)
                else:
                    after(pe, lo_taken, LO_JOBS * v + (j - RING + 1 if j else 0))
                b, s = (j // 2, j % 2) if j < LO_JOBS else (j - LO_JOBS, 2)
                w = 3 * l + s
                out = pj[:, j % RING, 0:H]
                pe.matmul(out, ones[:], b_parts[:, w], start=True, stop=False)
                split_product(
                    pe, out, [h_hi[p][:, c, b] for c in range(KC)], [h_lo[p][:, c, b] for c in range(KC)],
                    [w_hi[:, w, c] for c in range(KC)], [w_lo[:, w, c] for c in range(KC)], first=False).then_inc(pj_ready, 1)

            def transpose_attention(v):
                pe.wait_ge(e_ready, GB * (v + 1))
                pe.wait_ge(au_ready, v + 1)
                for b in range(GB):
                    for s in range(2):
                        i = pe.transpose(us_a[:, b, s], au[:, b, s], ident[:])
                i.then_inc(at_ready, 1)

            def close_visit(v):
                after(pe, cn_ready, v)
                pe.wait_ge(a_ready, v + 1)
                pe.wait_ge(lo_taken, LO_JOBS * (v + 1))
                for b in range(GB):
                    i = split_product(pe, cx[:, b, 0:HE], [a_hi[:, b, s] for s in range(2)], [a_lo[:, b, s] for s in range(2)],
                                      [v_hi[:, b, s] for s in range(2)], [v_lo[:, b, s] for s in range(2)])
                i.then_inc(cx_ready, 1)

            def half(it, k, has_prev, has_next):
                v = n * it + k
                l, p = k // 2, k % 2
                ni, nl, np_ = next_of(it, k)
                scores(v)
                project(0, l, p, v)
                if has_prev:
                    close_visit(v - 1)
                for j in range(1, LO_JOBS):
                    project(j, l, p, v)
                transpose_attention(v)
                if has_next:
                    open_visit(ni, nl, np_, v + 1)
                for j in range(LO_JOBS, JOBS):
                    project(j, l, p, v)

            pe.wait_ge(consts, 4)
            open_visit(0, 0, 0, 0)
            pe.wait_ge(w_ready, NW)
            pe.wait_ge(dconst, 8)
            halves(pe, L, half, lambda: close_visit(n * NIT - 1))


def mha_phase(nc, x_in, adj, w_q_t, w_k_t, w_v_t, w_o_t, b_v, b_o, x_out):
    n = 2
    HEADS = 12
    D = H // HEADS
    R = P // D
    SCALE = float(H) ** -0.5
    HJ = HEADS // 3
    with ExitStack() as ctx:
        m = Memory(nc, ctx, "mh_")
        raw = m.sb("raw", [4, KC, H])
        w_hi = m.sb("w_hi", [4, KC, H], F32R)
        w_lo = m.sb("w_lo", [4, KC, H], F32R)
        b_raw = m.sb("b_raw", [2, H])
        b_rnd = m.sb("b_rnd", [2, H], F32R)
        b_parts = m.sb("b_parts", [2, H], F32R)
        ones_f = m.sb("ones_f", [P])
        ones = m.sb("ones", [P], F32R)
        ident = m.sb("ident", [P])
        mhalf_c = m.sb("mhalf_c", [GB])
        xin = [m.sb(f"xin{p}", [GB, H]) for p in range(2)]
        adjin = [m.sb(f"adjin{p}", [GB, S]) for p in range(2)]
        xres = [m.sb(f"xres{p}", [GB, H]) for p in range(2)]
        h_f = m.sb("h_f", [KC, GB, S])
        h_hi = m.sb("h_hi", [KC, GB, S], F32R)
        h_lo = m.sb("h_lo", [KC, GB, S], F32R)
        qk = m.sb("qk", [KC, 2, GB, S])
        v_s = [m.sb(f"v_s{p}", [GB, H]) for p in range(2)]
        a_s = [m.sb(f"a_s{b}", [HEADS, S]) for b in range(GB)]
        e_s = [m.sb(f"e_s{b}", [HEADS, S]) for b in range(GB)]
        mx = [m.sb(f"mx{b}", [HEADS]) for b in range(GB)]
        mn = [m.sb(f"mn{b}", [HEADS]) for b in range(GB)]
        nb = [m.sb(f"nb{b}", [HEADS]) for b in range(GB)]
        zero = [m.sb(f"zero{b}", [HEADS]) for b in range(GB)]
        pad = [m.sb(f"pad{b}", [HEADS]) for b in range(GB)]
        keep = [m.sb(f"keep{b}", [HEADS]) for b in range(GB)]
        esum = [m.sb(f"esum{b}", [HEADS]) for b in range(GB)]
        rec = m.sb("rec", [HEADS])
        rd = [m.sb(f"rd{b}", [HEADS]) for b in range(GB)]
        at = m.sb("at", [HEADS, S])
        o_hi = m.sb("o_hi", [KC, S], F32R)
        o_lo = m.sb("o_lo", [KC, S], F32R)
        y = m.sb("y", [GB, H])
        o = [m.sb(f"o{p}", [GB, H]) for p in range(2)]
        ystats = m.sb("ystats", [GB, BN])
        ymv = m.sb("ymv", [GB, 2])
        yv = m.sb("yv", [GB])
        yr = m.sb("yr", [GB])

        ra = m.ps("ra", [2, 512])
        rb = m.ps("rb", [2, 512])
        sc = m.ps("sc", [R, 512])

        w_loaded = m.sem("w_loaded")
        c_loaded = m.sem("c_loaded")
        w_hi_done = m.sem("w_hi_done")
        w_ready = m.sem("w_ready")
        consts = m.sem("consts")
        dconst = m.sem("dconst")
        pool_gate = m.sem("pool_gate")
        dve_gate = m.sem("dve_gate")
        x_loaded = [m.sem(f"x_loaded{p}") for p in range(2)]
        adj_loaded = [m.sem(f"adj_loaded{p}") for p in range(2)]
        xin_free = [m.sem(f"xin_free{p}") for p in range(2)]
        tp_ready = m.sem("tp_ready")
        f_ready = m.sem("f_ready")
        hh_ready = m.sem("hh_ready")
        h_ready = m.sem("h_ready")
        qk_done = m.sem("qk_done")
        qk_taken = m.sem("qk_taken")
        v_done = m.sem("v_done")
        v_taken = m.sem("v_taken")
        sc_ready = m.sem("sc_ready")
        a_ready = m.sem("a_ready")
        mx_ready = m.sem("mx_ready")
        nb_ready = m.sem("nb_ready")
        mn_ready = m.sem("mn_ready")
        zero_ready = m.sem("zero_ready")
        pad_ready = m.sem("pad_ready")
        keep_ready = m.sem("keep_ready")
        e_ready = m.sem("e_ready")
        rec_ready = m.sem("rec_ready")
        rd_ready = m.sem("rd_ready")
        p_ready = m.sem("p_ready")
        et_done = m.sem("et_done")
        et_taken = m.sem("et_taken")
        av_done = m.sem("av_done")
        oh_ready = m.sem("oh_ready")
        av_taken = m.sem("av_taken")
        wo_done = m.sem("wo_done")
        wo_taken = m.sem("wo_taken")
        yst_ready = m.sem("yst_ready")
        ymv_ready = m.sem("ymv_ready")
        yv_ready = m.sem("yv_ready")
        yr_ready = m.sem("yr_ready")
        o_ready = m.sem("o_ready")
        stored = [m.sem(f"stored{p}") for p in range(2)]

        CONSTS = 4

        block = ctx.enter_context(nc.Block())

        def a_bank(job, k):
            return ra[:, (job + k) % 2, :]

        def e_bank(i):
            return rb[:, (i if i < 3 else i + 1) % 2, :]

        def v_bank():
            return rb[:, 1, :]

        def prev_of(it, k):
            return (it, 0) if k else (it - 1, 1)

        def next_of(it, k):
            return (it, 1) if k == 0 else (it + 1, 0)

        @block.sync
        def _(sp):
            for w, a in enumerate((w_q_t, w_k_t, w_v_t, w_o_t)):
                sp.dma_start(raw[:, w], rows(a)).then_inc(w_loaded, 16)
            sp.wait_ge(dconst, 1)
            for w, a in enumerate((b_v, b_o)):
                for r in (0, 32):
                    sp.dma_start(b_raw[r:r + 1, w], a.unsqueeze(0)).then_inc(c_loaded, 16)

            def load(it, p):
                g = 2 * it + p
                after(sp, xin_free[p], it)
                sp.dma_start(xin[p][:], x_in[bass.ds(g * GB, GB)].rearrange("b s h -> s b h")).then_inc(x_loaded[p], 16)
                after(sp, a_ready, GB * R * (g - 1))
                sp.dma_start(adjin[p][:], adj[bass.ds(g * GB, GB)].rearrange("b s t -> s b t")).then_inc(adj_loaded[p], 16)

            def store(it, p):
                sp.wait_ge(o_ready, 2 * it + p + 1)
                g = (2 * it + p) * GB
                sp.dma_start(x_out[bass.ds(g, GB)].rearrange("b s h -> s b h"), o[p][:]).then_inc(stored[p], 16)

            for p in range(2):
                load(0, p)
            with sp.Fori(1, NIT) as it:
                for p in range(2):
                    load(it, p)
                    store(it - 1, p)
            for p in range(2):
                store(NIT - 1, p)
            for p in range(2):
                sp.wait_ge(stored[p], 16 * NIT + 16)

        @block.gpsimd
        def _(pool):
            pool.memset(ones_f[:], 1.0).then_inc(consts, 1)
            pool.memset(mhalf_c[:], -0.5).then_inc(consts, 1)
            pool.memset(ident[:], 0.0).then_inc(consts, 1)
            pool.wait_ge(consts, 3)
            pool.affine_select(out=ident[:], in_=ident[:], compare_op=ALU.not_equal, fill=1.0, base=0,
                               pattern=[[-1, P]], channel_multiplier=1).then_inc(consts, 1)

            def open_visit(it, p, v):
                pool.wait_ge(tp_ready, GB * (v + 1))
                after(pool, wo_taken, GB * (v - 1))
                pool.sem_inc(pool_gate, 1)
                pool.tensor_copy(xres[p][:], xin[p][:]).then_inc(xin_free[p], 1)

            def normalise(b, v):
                pool.wait_ge(rd_ready, GB * v + b + 1)
                pool.tensor_tensor(a_s[b][:], e_s[b][:], rd[b][:].unsqueeze(2).broadcast_to([P, HEADS, S]),
                                   ALU.mult).then_inc(p_ready, 1)

            def out_norm(v):
                pool.wait_ge(yv_ready, v + 1)
                pool.tensor_tensor(yr[:], yv[:], mhalf_c[:], ALU.pow).then_inc(yr_ready, 1)

            def half(it, k, has_prev, has_next):
                v = n * it + k
                ni, np_ = next_of(it, k)
                if has_prev:
                    for b in range(GB):
                        normalise(b, v - 1)
                if has_next:
                    open_visit(ni, np_, v + 1)
                if has_prev:
                    out_norm(v - 1)

            def last():
                for b in range(GB):
                    normalise(b, n * NIT - 1)
                out_norm(n * NIT - 1)

            open_visit(0, 0, 0)
            halves(pool, 1, half, last)

        @block.scalar
        def _(act):
            act.wait_ge(w_loaded, 16 * 4)
            for w in range(4):
                act.activation(w_hi[:, w], raw[:, w], ACT.Copy).then_inc(w_hi_done, 1)

            def open_visit(v, k):
                for b in range(GB):
                    act.wait_ge(tp_ready, GB * v + b + 1)
                    act.activation(h_f[:, :, b, :], a_bank(6 + b, k)[:, 0:H].rearrange("p (c s) -> p c s", c=KC),
                                   ACT.Copy).then_inc(f_ready, 1)

            def take_qk(c, k, v):
                act.wait_ge(qk_done, KC * v + c + 1)
                act.activation(qk[:, c], a_bank(c, k).rearrange("p (w b s) -> p w b s", w=2, b=GB),
                               ACT.Copy).then_inc(qk_taken, 1)

            def take_v(b, p, v):
                act.wait_ge(v_done, GB * v + b + 1)
                act.activation(v_s[p][:, b], v_bank()[:, 0:H], ACT.Copy).then_inc(v_taken, 1)

            def take_e(b, v):
                for i in range(3):
                    act.wait_ge(et_done, 3 * (GB * v + b) + i + 1)
                    act.activation(at[:, HJ * i:HJ * (i + 1)], e_bank(3 * b + i).rearrange("p (h s) -> p h s", h=HJ),
                                   ACT.Copy).then_inc(et_taken, 1)

            def take_o(b, k, v):
                act.wait_ge(av_done, GB * v + b + 1)
                act.activation(o_hi[:], a_bank(3 + 2 * b, k)[:, 0:H].rearrange("p (c s) -> p c s", c=KC),
                               ACT.Copy).then_inc(oh_ready, 1)

            def exps(part, b, v):
                if part == 0:
                    act.wait_ge(nb_ready, GB * v + b + 1)
                for h in range(HJ * part, HJ * (part + 1)):
                    act.activation(e_s[b][:, h], a_s[b][:, h], ACT.Exp, bias=nb[b][:, h:h + 1],
                                   accum_out=esum[b][:, h:h + 1]).then_inc(e_ready, 1)

            def half(it, k, has_prev, has_next):
                v = n * it + k
                take_qk(0, k, v)
                take_qk(1, k, v)
                if has_prev:
                    exps(0, 1, v - 1)
                    take_e(0, v - 1)
                    exps(1, 1, v - 1)
                take_qk(2, k, v)
                if has_prev:
                    take_o(0, k, v - 1)
                    exps(2, 1, v - 1)
                take_v(0, k, v)
                if has_prev:
                    take_e(1, v - 1)
                take_v(1, k, v)
                exps(0, 0, v)
                if has_prev:
                    take_o(1, k, v - 1)
                exps(1, 0, v)
                if has_next:
                    open_visit(v + 1, k)
                exps(2, 0, v)

            def last():
                v = n * NIT - 1
                exps(0, 1, v)
                take_e(0, v)
                exps(1, 1, v)
                take_o(0, 0, v)
                exps(2, 1, v)
                take_e(1, v)
                take_o(1, 0, v)

            open_visit(0, -1)
            halves(act, 1, half, last)

        @block.vector
        def _(dve):
            dve.memset(b_raw[:], 0.0).then_inc(dconst, 1)
            for w in range(4):
                dve.wait_ge(w_hi_done, w + 1)
                dve.tensor_tensor(w_lo[:, w], raw[:, w], w_hi[:, w].bitcast(F32), ALU.subtract).then_inc(w_ready, 1)
            dve.wait_ge(consts, 4)
            dve.tensor_copy(ones[:], ones_f[:]).then_inc(dconst, 1)
            dve.memset(b_parts[:].bitcast(F32), 0.0).then_inc(dconst, 1)
            dve.wait_ge(c_loaded, 16 * CONSTS)
            dve.tensor_copy(b_rnd[:], b_raw[:]).then_inc(dconst, 1)
            dve.wait_ge(dconst, 4)
            dve.tensor_copy(b_parts[0:1], b_raw[0:1]).then_inc(dconst, 1)
            dve.tensor_tensor(b_parts[32:33], b_raw[32:33], b_rnd[32:33].bitcast(F32), ALU.subtract).then_inc(dconst, 1)
            for p in range(2):
                dve.engine_nop().then_inc(stored[p], 16)

            def open_visit(v):
                dve.wait_ge(f_ready, GB * (v + 1))
                dve.tensor_copy(h_hi[:], h_f[:]).then_inc(hh_ready, 1)
                dve.wait_ge(hh_ready, v + 1)
                dve.tensor_tensor(h_lo[:], h_f[:], h_hi[:].bitcast(F32), ALU.subtract).then_inc(h_ready, 1)

            def take_scores(it, b, p, v):
                dve.wait_ge(adj_loaded[p], 16 * it + 16)
                dve.wait_ge(sc_ready, GB * v + b + 1)
                for r in range(R):
                    dve.scalar_tensor_tensor(a_s[b][:, KC * r:KC * (r + 1)], sc[:, r, 0:KC * S].rearrange("p (c s) -> p c s", c=KC),
                                             SCALE, adjin[p][:, b].unsqueeze(1).broadcast_to([P, KC, S]),
                                             ALU.mult, ALU.add).then_inc(a_ready, 1)
                dve.wait_ge(a_ready, R * (GB * v + b + 1))
                dve.tensor_reduce(mx[b][:], a_s[b][:], AX_X, ALU.max).then_inc(mx_ready, 1)
                dve.wait_ge(mx_ready, GB * v + b + 1)
                dve.tensor_scalar(nb[b][:], mx[b][:], -1.0, None, ALU.mult).then_inc(nb_ready, 1)

            def find_pads(b, v):
                u = GB * v + b
                dve.tensor_reduce(mn[b][:], a_s[b][:], AX_X, ALU.min).then_inc(mn_ready, 1)
                dve.wait_ge(mn_ready, u + 1)
                dve.tensor_scalar(zero[b][:], mn[b][:], 0.0, None, ALU.is_equal).then_inc(zero_ready, 1)
                dve.wait_ge(zero_ready, u + 1)
                dve.scalar_tensor_tensor(pad[b][:], mx[b][:], 0.0, zero[b][:], ALU.is_equal, ALU.mult).then_inc(pad_ready, 1)
                dve.wait_ge(pad_ready, u + 1)
                dve.tensor_scalar(keep[b][:], pad[b][:], -1.0, 1.0, ALU.mult, ALU.add).then_inc(keep_ready, 1)

            def sums(b, v):
                u = GB * v + b
                dve.wait_ge(e_ready, HEADS * (u + 1))
                dve.reciprocal(rec[:], esum[b][:]).then_inc(rec_ready, 1)
                dve.wait_ge(rec_ready, u + 1)
                dve.wait_ge(keep_ready, u + 1)
                dve.tensor_tensor(rd[b][:], rec[:], keep[b][:], ALU.mult).then_inc(rd_ready, 1)

            def take_o(b, k, v):
                dve.wait_ge(oh_ready, GB * v + b + 1)
                dve.tensor_tensor(o_lo[:], a_bank(3 + 2 * b, k)[:, 0:H].rearrange("p (c s) -> p c s", c=KC),
                                  o_hi[:].bitcast(F32), ALU.subtract).then_inc(av_taken, 1)

            def residual(b, p, k, v):
                u = GB * v + b
                dve.wait_ge(wo_done, u + 1)
                dve.tensor_tensor(y[:, b], a_bank(4 + 4 * b, k)[:, 0:H], xres[p][:, b], ALU.add).then_inc(wo_taken, 1)
                dve.wait_ge(wo_taken, u + 1)
                dve.bn_stats(ystats[:, b], y[:, b]).then_inc(yst_ready, 1)
                dve.wait_ge(yst_ready, u + 1)
                dve.sem_inc(dve_gate, 1)
                dve.bn_aggr(ymv[:, b], ystats[:, b]).then_inc(ymv_ready, 1)

            def variance(v):
                dve.wait_ge(ymv_ready, GB * (v + 1))
                dve.tensor_scalar(yv[:].unsqueeze(2), ymv[:, :, 1:2], 1e-5, None, ALU.add).then_inc(yv_ready, 1)

            def output(it, p):
                g = 2 * it + p
                dve.wait_ge(yr_ready, g + 1)
                dve.wait_ge(stored[p], 16 * it + 16)
                for b in range(GB):
                    i = dve.tensor_scalar(o[p][:, b], y[:, b], ymv[:, b, 0:1], yr[:, b:b + 1], ALU.subtract, ALU.mult)
                i.then_inc(o_ready, 1)

            def half(it, k, has_prev, has_next):
                v = n * it + k
                pi, pp = prev_of(it, k)
                if has_prev:
                    sums(0, v - 1)
                    take_scores(pi, 1, pp, v - 1)
                    find_pads(1, v - 1)
                    take_o(0, k, v - 1)
                    residual(0, pp, k, v - 1)
                    sums(1, v - 1)
                take_scores(it, 0, k, v)
                if has_prev:
                    take_o(1, k, v - 1)
                if has_next:
                    open_visit(v + 1)
                if has_prev:
                    residual(1, pp, k, v - 1)
                    variance(v - 1)
                find_pads(0, v)
                if has_prev:
                    output(pi, pp)

            def last():
                v = n * NIT - 1
                sums(0, v)
                take_scores(NIT - 1, 1, 1, v)
                find_pads(1, v)
                take_o(0, 0, v)
                residual(0, 1, 0, v)
                sums(1, v)
                take_o(1, 0, v)
                residual(1, 1, 0, v)
                variance(v)
                output(NIT - 1, 1)

            open_visit(0)
            halves(dve, 1, half, last)

        @block.tensor
        def _(pe):
            def open_visit(it, p, v, k, has_prev):
                pe.wait_ge(x_loaded[p], 16 * it + 16)
                for b in range(GB):
                    if has_prev:
                        if b == 0:
                            after(pe, wo_taken, GB * (v - 2) + 1)
                        else:
                            after(pe, av_taken, GB * (v - 2) + 2)
                    else:
                        after(pe, qk_taken, KC * v)
                    for c in range(KC):
                        i = pe.transpose(a_bank(6 + b, k)[:, c * P:(c + 1) * P], xin[p][:, b, c * P:(c + 1) * P], ident[:])
                    i.then_inc(tp_ready, 1)

            def project_qk(c, k, v):
                if c == 0:
                    pe.wait_ge(h_ready, v + 1)
                elif c == 1:
                    after(pe, wo_taken, GB * (v - 1))
                else:
                    pe.wait_ge(qk_taken, KC * v + 1)
                for w in range(2):
                    i = split_product(
                        pe, a_bank(c, k)[:, w * GB * S:(w + 1) * GB * S],
                        [w_hi[:, w, i, c * P:(c + 1) * P] for i in range(KC)],
                        [w_lo[:, w, i, c * P:(c + 1) * P] for i in range(KC)],
                        [h_hi[:, i].rearrange("p b s -> p (b s)") for i in range(KC)],
                        [h_lo[:, i].rearrange("p b s -> p (b s)") for i in range(KC)])
                i.then_inc(qk_done, 1)

            def project_v(b, v, has_prev):
                if has_prev:
                    pe.wait_ge(et_taken, 6 * (v - 1) + 3 * b + 2)
                else:
                    after(pe, v_taken, GB * v + b)
                out = v_bank()[:, 0:H]
                pe.matmul(out, ones[:], b_parts[:, 0], start=True, stop=False)
                split_product(pe, out, [h_hi[:, c, b] for c in range(KC)], [h_lo[:, c, b] for c in range(KC)],
                              [w_hi[:, 2, c] for c in range(KC)], [w_lo[:, 2, c] for c in range(KC)],
                              first=False).then_inc(v_done, 1)

            def scores(b, v):
                pe.wait_ge(qk_taken, KC * (v + 1))
                after(pe, a_ready, R * (GB * v + b))
                for c in range(KC):
                    for r in range(R):
                        q = slice(D * r, D * (r + 1))
                        i = pe.matmul(sc[:, r, c * S:(c + 1) * S], qk[q, c, 0, b], qk[q, c, 1, b], start=True, stop=True)
                i.then_inc(sc_ready, 1)

            def transpose_attention(b, v, projects):
                pe.wait_ge(p_ready, GB * v + b + 1)
                for i in range(3):
                    if (b, i) == (0, 0):
                        after(pe, et_taken, 6 * v)
                    elif (b, i) == (0, 1):
                        pe.wait_ge(v_taken, GB * (v + 1))
                    elif (b, i) == (1, 1) and projects:
                        pe.wait_ge(v_taken, GB * (v + 1) + 1)
                    else:
                        pe.wait_ge(et_taken, 6 * v + 3 * b + i - (1 if b == 0 or i != 0 else 0))
                    for h in range(HJ):
                        t = pe.transpose(e_bank(3 * b + i)[:, h * S:(h + 1) * S], a_s[b][:, HJ * i + h], ident[:])
                    t.then_inc(et_done, 1)

            def attend(b, p, k, v, projects):
                pe.wait_ge(et_taken, 6 * v + 3 * b + 3)
                if b == 0:
                    if projects:
                        pe.wait_ge(qk_taken, KC * (v + 1) + 2)
                    else:
                        after(pe, wo_taken, GB * v)
                        after(pe, av_taken, GB * v)
                else:
                    pe.wait_ge(av_taken, GB * v + 1)
                out = a_bank(3 + 2 * b, k)
                for c in range(KC):
                    for r in range(R):
                        h = R * c + r
                        i = pe.matmul(out[D * r:D * (r + 1), c * S:(c + 1) * S], v_s[p][:, b, h * D:(h + 1) * D],
                                      at[:, KC * r + c], start=True, stop=True)
                i.then_inc(av_done, 1)

            def project_out(b, k, v, projects, opens):
                pe.wait_ge(av_taken, GB * v + b + 1)
                if b == 0:
                    if projects:
                        pe.wait_ge(qk_taken, KC * (v + 2))
                elif opens:
                    pe.wait_ge(f_ready, GB * (v + 2) + 1)
                else:
                    pe.wait_ge(wo_taken, GB * v + 1)
                out = a_bank(4 + 4 * b, k)[:, 0:H]
                pe.matmul(out, ones[:], b_parts[:, 1], start=True, stop=False)
                split_product(pe, out, [o_hi[:, c] for c in range(KC)], [o_lo[:, c] for c in range(KC)],
                              [w_hi[:, 3, c] for c in range(KC)], [w_lo[:, 3, c] for c in range(KC)],
                              first=False).then_inc(wo_done, 1)

            def half(it, k, has_prev, has_next):
                v = n * it + k
                pi, pp = prev_of(it, k)
                ni, np_ = next_of(it, k)
                project_qk(0, k, v)
                project_qk(1, k, v)
                if has_prev:
                    transpose_attention(0, v - 1, True)
                project_qk(2, k, v)
                if has_prev:
                    attend(0, pp, k, v - 1, True)
                scores(0, v)
                if has_prev:
                    project_out(0, k, v - 1, True, has_next)
                project_v(0, v, has_prev)
                if has_prev:
                    transpose_attention(1, v - 1, True)
                project_v(1, v, has_prev)
                if has_prev:
                    attend(1, pp, k, v - 1, True)
                if has_next:
                    open_visit(ni, np_, v + 1, k, has_prev)
                if has_prev:
                    project_out(1, k, v - 1, True, has_next)
                scores(1, v)

            def last():
                v = n * NIT - 1
                transpose_attention(0, v, False)
                attend(0, 1, 0, v, False)
                project_out(0, 0, v, False, False)
                transpose_attention(1, v, False)
                attend(1, 1, 0, v, False)
                project_out(1, 0, v, False, False)

            pe.wait_ge(consts, 4)
            open_visit(0, 0, 0, -1, False)
            pe.wait_ge(w_ready, 4)
            pe.wait_ge(dconst, 6)
            halves(pe, 1, half, last)


def build(nc, a):
    x1, x2, x3 = (nc.dram_tensor(f"x_{i}", (B, S, H), F32).ap() for i in (1, 2, 3))
    gat_phase(nc, a["x"], a["adj"], a["L0_gnn_W_left"], a["L0_gnn_W_right"], a["L0_gnn_W_lin"], a["L0_gnn_b_lin"],
              a["L0_gnn_ln_a"], a["L0_gnn_ln_b"], a["L0_gnn_ln_a_cols"], a["L0_gnn_ln_b_cols"], x1)
    digcn_phase(nc, x1, a["adj"], a["L1_gnn_Wl"], a["L1_gnn_bl"], a["L1_gnn_Ws"], a["L1_gnn_bs"], a["L1_gnn_Wr"],
                a["L1_gnn_br"], a["L1_gnn_ln_w"], a["L1_gnn_ln_b"], a["L1_gnn_ln_w_cols"], a["L1_gnn_ln_b_cols"], x2)
    mha_phase(nc, x2, a["adj"], a["L2_gnn_Wq"], a["L2_gnn_Wk"], a["L2_gnn_Wv"], a["L2_gnn_Wo"], a["L2_gnn_bv"],
              a["L2_gnn_bo"], x3)
    digcn_phase(nc, x3, a["adj"], a["L3_gnn_W_left"], a["L3_gnn_b_left"], a["L3_gnn_W_self"], a["L3_gnn_b_self"],
                a["L3_gnn_W_right"], a["L3_gnn_b_right"], a["L3_gnn_gamma"], a["L3_gnn_beta"],
                a["L3_gnn_gamma_cols"], a["L3_gnn_beta_cols"], a["out"])


_TURNED = ["L0_gnn_W_lin", "L1_gnn_Wl", "L1_gnn_Ws", "L1_gnn_Wr", "L2_gnn_Wq", "L2_gnn_Wk", "L2_gnn_Wv", "L2_gnn_Wo",
           "L3_gnn_W_left", "L3_gnn_W_self", "L3_gnn_W_right"]
_COLUMNS = ["L0_gnn_ln_a", "L0_gnn_ln_b", "L1_gnn_ln_w", "L1_gnn_ln_b", "L3_gnn_gamma", "L3_gnn_beta"]


def kernel(**inputs):
    import numpy as _np
    import concourse.bacc as _bacc
    from concourse import mybir as _mybir
    from concourse.bass_utils import run_bass_kernel_spmd as _run

    nc = _bacc.Bacc("TRN2", target_bir_lowering=False, num_devices=1)
    host = {}
    for name, value in inputs.items():
        value = _np.asarray(value)
        if name in _TURNED:
            value = value.swapaxes(-1, -2)
        if name.startswith("L3_"):
            value = value[None]
        host[name] = value
        if name in _COLUMNS:
            host[name + "_cols"] = value.reshape(-1, KC, P).swapaxes(1, 2)
    arrays, aps = {}, {}
    for name, value in host.items():
        value = _np.ascontiguousarray(value)
        arrays[f"in_{name}"] = value
        aps[name] = nc.dram_tensor(f"in_{name}", value.shape, _mybir.dt.from_np(value.dtype), kind="ExternalInput").ap()
    aps["out"] = nc.dram_tensor("out_x", (B, S, H), F32, kind="ExternalOutput").ap()
    build(nc, aps)
    return _run(nc, [arrays], core_ids=[0]).results[0]["out_x"]
```

```python
from contextlib import ExitStack

import concourse.bass as bass
from concourse import mybir

F32 = mybir.dt.float32
F32R = mybir.dt.float32r
ALU = mybir.AluOpType
ACT = mybir.ActivationFunctionType
AX_X = mybir.AxisListType.X

B, S, H = 64, 128, 384
P = 128
KC = H // P
GB = 2
NIT = B // (2 * GB)
HE = H + 2
BN = 6


class Memory:

    def __init__(self, nc, ctx, prefix):
        self.nc, self.ctx, self.prefix, self.sems = nc, ctx, prefix, []
        ctx.callback(self.clear)

    def clear(self):
        self.nc.clear_and_free_semaphores(self.sems)
        self.nc.all_engine_barrier()

    def sb(self, name, shape, dt=F32):
        return self.ctx.enter_context(self.nc.sbuf_tensor(self.prefix + name, [P] + shape, dt))

    def ps(self, name, shape):
        return self.ctx.enter_context(self.nc.psum_tensor(self.prefix + name, [P] + shape, F32))

    def sem(self, name):
        self.sems.append(self.nc.alloc_semaphore(self.prefix + name))
        return self.sems[-1]


def halves(eng, layers, half, last):
    n = 2 * layers
    for k in range(n):
        half(0, k, k > 0, True)
    with eng.Fori(1, NIT - 1) as it:
        for k in range(n):
            half(it, k, True, True)
    for k in range(n):
        half(NIT - 1, k, True, k < n - 1)
    last()


def rows(w):
    return w.rearrange("(c p) n -> p c n", p=P)


def split_product(pe, out, his, los, rhis, rlos, first=True, close=True):
    n = len(his)
    for c in range(n):
        pe.matmul(out, his[c], rhis[c], start=(first and c == 0), stop=False)
        pe.matmul(out, his[c], rlos[c], start=False, stop=False)
        last = pe.matmul(out, los[c], rhis[c], start=False, stop=(close and c == n - 1))
    return last


def after(eng, sem, count):
    if not isinstance(count, int) or count > 0:
        eng.wait_ge(sem, count)


def gat_phase(nc, x_in, adj, w_left, w_right, w_lin_t, b_lin, ln_a, ln_b, ln_a_cols, ln_b_cols, x_out):
    L = 2
    n = 2 * L
    TEMPER = float(H) ** 0.5
    with ExitStack() as ctx:
        m = Memory(nc, ctx, "g0_")
        raw = m.sb("raw", [3 * L, KC, H])
        w_hi = m.sb("w_hi", [3 * L, KC, H], F32R)
        w_lo = m.sb("w_lo", [3 * L, KC, H], F32R)
        b_raw = m.sb("b_raw", [L, H])
        b_rnd = m.sb("b_rnd", [L, H], F32R)
        b_parts = m.sb("b_parts", [L, H], F32R)
        ones_f = m.sb("ones_f", [P])
        ones = m.sb("ones", [P], F32R)
        ident = m.sb("ident", [P])
        half_c = m.sb("half_c", [GB])
        mhalf_c = m.sb("mhalf_c", [GB])
        a_cols = m.sb("a_cols", [KC])
        b_cols = m.sb("b_cols", [KC])
        a_row = m.sb("a_row", [H])
        b_row = m.sb("b_row", [H])
        xin = [m.sb(f"xin{p}", [GB, H]) for p in range(2)]
        adjin = [m.sb(f"adjin{p}", [GB, S]) for p in range(2)]
        xres = [m.sb(f"xres{p}", [GB, H]) for p in range(2)]
        adj_t = [m.sb(f"adj_t{p}", [GB, S]) for p in range(2)]
        masks = [m.sb(f"masks{p}", [GB, 2, S]) for p in range(2)]
        h_f = m.sb("h_f", [KC, GB, S])
        h_hi = [m.sb(f"h_hi{p}", [KC, GB, S], F32R) for p in range(2)]
        h_lo = [m.sb(f"h_lo{p}", [KC, GB, S], F32R) for p in range(2)]
        g_hi = m.sb("g_hi", [KC, 2, GB, S], F32R)
        g_lo = m.sb("g_lo", [KC, 2, GB, S], F32R)
        v_hi = m.sb("v_hi", [GB, HE], F32R)
        v_lo = m.sb("v_lo", [GB, HE], F32R)
        um = m.sb("um", [GB, 2, S])
        ua = m.sb("ua", [GB, S])
        e_s = m.sb("e_s", [GB, S])
        ea = m.sb("ea", [GB, S])
        e_hi = m.sb("e_hi", [GB, S], F32R)
        e_lo = m.sb("e_lo", [GB, S], F32R)
        den = m.sb("den", [GB])
        rden = m.sb("rden", [GB])
        cn = m.sb("cn", [GB, H])
        tn = m.sb("tn", [GB, H])
        t2 = m.sb("t2", [GB, H])
        t3 = m.sb("t3", [GB, H])
        t4 = m.sb("t4", [GB, H])
        y = [m.sb(f"y{p}", [GB, H]) for p in range(2)]
        o = [m.sb(f"o{p}", [GB, H]) for p in range(2)]
        stats = m.sb("stats", [GB, BN])
        mv = m.sb("mv", [GB, 2])
        vs = m.sb("vs", [GB])
        sd = m.sb("sd", [GB])
        se = m.sb("se", [GB])
        rr = m.sb("rr", [GB])
        ystats = m.sb("ystats", [GB, BN])
        ymv = [m.sb(f"ymv{p}", [GB, 2]) for p in range(2)]
        yv = m.sb("yv", [GB])
        yr = [m.sb(f"yr{p}", [GB]) for p in range(2)]

        tp = m.ps("tp", [GB, 512])
        pj = m.ps("pj", [3, 512])
        us = m.ps("us", [GB, 2, S])
        cx = m.ps("cx", [GB, 512])

        w_loaded = m.sem("w_loaded")
        c_loaded = m.sem("c_loaded")
        w_hi_done = m.sem("w_hi_done")
        w_ready = m.sem("w_ready")
        consts = m.sem("consts")
        dconst = m.sem("dconst")
        pool_gate = m.sem("pool_gate")
        dve_gate = m.sem("dve_gate")
        x_loaded = [m.sem(f"x_loaded{p}") for p in range(2)]
        xin_free = [m.sem(f"xin_free{p}") for p in range(2)]
        tp_ready = m.sem("tp_ready")
        f_ready = m.sem("f_ready")
        hh_ready = m.sem("hh_ready")
        h_ready = m.sem("h_ready")
        pj_ready = m.sem("pj_ready")
        hi_ready = m.sem("hi_ready")
        pj_taken = m.sem("pj_taken")
        us_ready = m.sem("us_ready")
        um_ready = m.sem("um_ready")
        ua_ready = m.sem("ua_ready")
        e_ready = m.sem("e_ready")
        ea_ready = m.sem("ea_ready")
        eh_ready = m.sem("eh_ready")
        a_ready = m.sem("a_ready")
        cx_ready = m.sem("cx_ready")
        den_ready = m.sem("den_ready")
        rden_ready = m.sem("rden_ready")
        cn_ready = m.sem("cn_ready")
        st_ready = m.sem("st_ready")
        mv_ready = m.sem("mv_ready")
        vs_ready = m.sem("vs_ready")
        sd_ready = m.sem("sd_ready")
        se_ready = m.sem("se_ready")
        rr_ready = m.sem("rr_ready")
        tn_ready = m.sem("tn_ready")
        mask_ready = m.sem("mask_ready")
        adjt_ready = m.sem("adjt_ready")
        t2_ready = m.sem("t2_ready")
        t3_ready = m.sem("t3_ready")
        t4_ready = m.sem("t4_ready")
        y_ready = m.sem("y_ready")
        yst_ready = m.sem("yst_ready")
        ymv_ready = m.sem("ymv_ready")
        yv_ready = m.sem("yv_ready")
        yr_ready = m.sem("yr_ready")
        o_ready = m.sem("o_ready")
        stored = [m.sem(f"stored{p}") for p in range(2)]

        NW = 3 * L
        JOBS = 5
        RING = 3

        block = ctx.enter_context(nc.Block())

        def prev_of(it, k):
            return (it, (k - 1) // 2, (k - 1) % 2) if k else (it - 1, L - 1, 1)

        def first(it):
            return isinstance(it, int) and it == 0

        def next_of(it, k):
            return (it, (k + 1) // 2, (k + 1) % 2) if k < n - 1 else (it + 1, 0, 0)

        @block.sync
        def _(sp):
            for i in range(L):
                sp.dma_start(raw[:, 3 * i], rows(w_left[i])).then_inc(w_loaded, 16)
                sp.dma_start(raw[:, 3 * i + 1], rows(w_right[i])).then_inc(w_loaded, 16)
                sp.dma_start(raw[:, 3 * i + 2], rows(w_lin_t[i])).then_inc(w_loaded, 16)
            sp.wait_ge(dconst, 1)
            sp.dma_start(b_raw[0:1], b_lin.unsqueeze(0)).then_inc(c_loaded, 16)
            sp.dma_start(b_raw[32:33], b_lin.unsqueeze(0)).then_inc(c_loaded, 16)
            sp.dma_start(a_cols[:], ln_a_cols[0]).then_inc(c_loaded, 16)
            sp.dma_start(b_cols[:], ln_b_cols[0]).then_inc(c_loaded, 16)
            sp.dma_start(a_row[:], ln_a[L - 1].partition_broadcast(P)).then_inc(c_loaded, 16)
            sp.dma_start(b_row[:], ln_b[L - 1].partition_broadcast(P)).then_inc(c_loaded, 16)

            def load(it, p):
                after(sp, xin_free[p], it)
                at = (2 * it + p) * GB
                after(sp, mask_ready, 2 * it + p - 1)
                sp.dma_start(xin[p][:], x_in[bass.ds(at, GB)].rearrange("b s h -> s b h")).then_inc(x_loaded[p], 16)
                sp.dma_start(adjin[p][:], adj[bass.ds(at, GB)].rearrange("b s t -> s b t")).then_inc(x_loaded[p], 16)

            def store(it, p):
                sp.wait_ge(o_ready, 2 * it + p + 1)
                at = (2 * it + p) * GB
                sp.dma_start(x_out[bass.ds(at, GB)].rearrange("b s h -> s b h"), o[p][:]).then_inc(stored[p], 16)

            for it in range(2):
                for p in range(2):
                    load(it, p)
            with sp.Fori(1, NIT - 1) as it:
                for p in range(2):
                    store(it - 1, p)
                    load(it + 1, p)
            for it in (NIT - 2, NIT - 1):
                for p in range(2):
                    store(it, p)
            for p in range(2):
                sp.wait_ge(stored[p], 16 * NIT + 16)

        @block.gpsimd
        def _(pool):
            pool.memset(ones_f[:], 1.0).then_inc(consts, 1)
            pool.memset(half_c[:], 0.5).then_inc(consts, 1)
            pool.memset(mhalf_c[:], -0.5).then_inc(consts, 1)
            pool.memset(ident[:], 0.0).then_inc(consts, 1)
            pool.wait_ge(consts, 4)
            pool.affine_select(out=ident[:], in_=ident[:], compare_op=ALU.not_equal, fill=1.0, base=0,
                               pattern=[[-1, P]], channel_multiplier=1).then_inc(consts, 1)
            pool.wait_ge(c_loaded, 16 * 6)

            def open_visit(it, l, p, v):
                if l == 0:
                    pool.wait_ge(adjt_ready, 2 * it + p + 1)
                    pool.sem_inc(pool_gate, 1)
                    pool.affine_select(out=masks[p][:, :, 0, :], in_=adj_t[p][:], compare_op=ALU.is_ge, fill=0.0,
                                       base=0, pattern=[[0, GB], [-1, S]], channel_multiplier=1)
                    pool.affine_select(out=masks[p][:, :, 1, :], in_=adjin[p][:], compare_op=ALU.is_gt, fill=0.0,
                                       base=0, pattern=[[0, GB], [1, S]], channel_multiplier=-1).then_inc(mask_ready, 1)

            def deviation(v):
                pool.wait_ge(vs_ready, v + 1)
                pool.tensor_tensor(sd[:], vs[:], half_c[:], ALU.pow).then_inc(sd_ready, 1)

            def affine(it, p, v):
                g = 2 * it + p
                pool.wait_ge(tn_ready, v + 1)
                pool.tensor_tensor(t2[:], tn[:], a_row[:].unsqueeze(1).broadcast_to([P, GB, H]), ALU.mult).then_inc(t2_ready, 1)
                pool.wait_ge(t2_ready, g + 1)
                pool.tensor_tensor(t3[:], t2[:], b_row[:].unsqueeze(1).broadcast_to([P, GB, H]), ALU.add).then_inc(t3_ready, 1)

            def residual(it, p):
                pool.wait_ge(xin_free[p], it + 1)
                pool.wait_ge(t4_ready, 2 * it + p + 1)
                pool.tensor_tensor(y[p][:], t4[:], xres[p][:], ALU.add).then_inc(y_ready, 1)

            def out_norm(it, p):
                pool.wait_ge(yv_ready, 2 * it + p + 1)
                pool.tensor_tensor(yr[p][:], yv[:], mhalf_c[:], ALU.pow).then_inc(yr_ready, 1)

            def half(it, k, has_prev, has_next):
                v = n * it + k
                pi, pl, pp = prev_of(it, k)
                ni, nl, np_ = next_of(it, k)
                done = k < 2 and not first(it)
                if done:
                    residual(it - 1, k)
                if has_prev:
                    deviation(v - 1)
                if has_prev and pl == L - 1:
                    affine(pi, pp, v - 1)
                if has_next:
                    open_visit(ni, nl, np_, v + 1)
                if done:
                    out_norm(it - 1, k)

            open_visit(0, 0, 0, 0)

            def last():
                residual(NIT - 1, 0)
                deviation(n * NIT - 1)
                affine(NIT - 1, 1, n * NIT - 1)
                out_norm(NIT - 1, 0)
                residual(NIT - 1, 1)
                out_norm(NIT - 1, 1)

            halves(pool, L, half, last)

        @block.scalar
        def _(act):
            act.wait_ge(w_loaded, 16 * NW)
            for w in range(NW):
                act.activation(w_hi[:, w], raw[:, w], ACT.Copy).then_inc(w_hi_done, 1)
            act.wait_ge(c_loaded, 16 * 6)

            def open_visit(it, l, p, v):
                act.wait_ge(tp_ready, v + 1)
                if l == 0:
                    act.activation(adj_t[p][:], tp[:, :, H:512], ACT.Copy).then_inc(adjt_ready, 1)
                    for b in range(GB):
                        i = act.activation(h_f[:, :, b, :], tp[:, b, 0:H].rearrange("p (c s) -> p c s", c=KC), ACT.Copy)
                else:
                    for c in range(KC):
                        i = act.activation(h_f[:, c], tp[:, :, c * P:(c + 1) * P], ACT.Relu,
                                           bias=b_cols[:, c:c + 1], scale=a_cols[:, c:c + 1])
                i.then_inc(f_ready, 1)

            def take_hi(j, v):
                act.wait_ge(pj_ready, JOBS * v + j + 1)
                if j < KC:
                    i = act.activation(g_hi[:, j], pj[:, j % RING, :].rearrange("p (w b s) -> p w b s", w=2, b=GB), ACT.Copy)
                else:
                    i = act.activation(v_hi[:, j - KC, 0:H], pj[:, j % RING, 0:H], ACT.Copy)
                i.then_inc(hi_ready, 1)

            def close_visit(v):
                act.wait_ge(rden_ready, v + 1)
                for b in range(GB):
                    act.activation(cn[:, b], cx[:, b, 0:H], ACT.Copy, scale=rden[:, b:b + 1]).then_inc(cn_ready, 1)

            def keep_x(it, p, v):
                act.wait_ge(x_loaded[p], 32 * it + 32)
                act.wait_ge(tp_ready, v + 1)
                after(act, y_ready, 2 * it + p - 1)
                act.activation(xres[p][:], xin[p][:], ACT.Copy).then_inc(xin_free[p], 1)

            def relu(it, p):
                g = 2 * it + p
                act.wait_ge(t3_ready, g + 1)
                after(act, y_ready, g)
                act.activation(t4[:], t3[:], ACT.Relu).then_inc(t4_ready, 1)

            def half(it, k, has_prev, has_next):
                v = n * it + k
                pi, pl, pp = prev_of(it, k)
                ni, nl, np_ = next_of(it, k)
                take_hi(0, v)
                if has_prev:
                    close_visit(v - 1)
                take_hi(1, v)
                take_hi(2, v)
                if k < 2:
                    keep_x(it, k, v)
                take_hi(3, v)
                if has_next:
                    open_visit(ni, nl, np_, v + 1)
                act.wait_ge(ua_ready, v + 1)
                act.activation(e_s[:], ua[:], ACT.Exp, scale=1.0 / TEMPER).then_inc(e_ready, 1)
                take_hi(KC + 1, v)
                if has_prev and pl == L - 1:
                    relu(pi, pp)

            def last():
                close_visit(n * NIT - 1)
                relu(NIT - 1, 1)

            open_visit(0, 0, 0, 0)
            halves(act, L, half, last)

        @block.vector
        def _(dve):
            dve.memset(b_raw[:], 0.0).then_inc(dconst, 1)
            for w in range(NW):
                dve.wait_ge(w_hi_done, w + 1)
                dve.tensor_tensor(w_lo[:, w], raw[:, w], w_hi[:, w].bitcast(F32), ALU.subtract).then_inc(w_ready, 1)
            dve.wait_ge(consts, 5)
            dve.tensor_copy(ones[:], ones_f[:]).then_inc(dconst, 1)
            dve.memset(v_hi[:, :, H:HE].bitcast(F32), 1.0).then_inc(dconst, 1)
            dve.memset(v_lo[:, :, H:HE].bitcast(F32), 0.0).then_inc(dconst, 1)
            dve.memset(b_parts[:].bitcast(F32), 0.0).then_inc(dconst, 1)
            dve.wait_ge(c_loaded, 16 * 6)
            dve.tensor_copy(b_rnd[:], b_raw[:]).then_inc(dconst, 1)
            dve.wait_ge(dconst, 6)
            dve.tensor_copy(b_parts[0:1], b_raw[0:1]).then_inc(dconst, 1)
            dve.tensor_tensor(b_parts[32:33], b_raw[32:33], b_rnd[32:33].bitcast(F32), ALU.subtract).then_inc(dconst, 1)
            for p in range(2):
                dve.engine_nop().then_inc(stored[p], 16)

            def open_hi(p, v):
                dve.wait_ge(f_ready, v + 1)
                dve.tensor_copy(h_hi[p][:], h_f[:]).then_inc(hh_ready, 1)

            def open_lo(p, v):
                dve.wait_ge(hh_ready, v + 1)
                dve.tensor_tensor(h_lo[p][:], h_f[:], h_hi[p][:].bitcast(F32), ALU.subtract).then_inc(h_ready, 1)

            def take_lo(j, v):
                dve.wait_ge(hi_ready, JOBS * v + j + 1)
                if j < KC:
                    i = dve.tensor_tensor(g_lo[:, j].rearrange("p w b s -> p (w b s)"), pj[:, j % RING, :],
                                          g_hi[:, j].bitcast(F32).rearrange("p w b s -> p (w b s)"), ALU.subtract)
                else:
                    i = dve.tensor_tensor(v_lo[:, j - KC, 0:H], pj[:, j % RING, 0:H],
                                          v_hi[:, j - KC, 0:H].bitcast(F32), ALU.subtract)
                i.then_inc(pj_taken, 1)

            def close_sums(v):
                dve.wait_ge(cx_ready, v + 1)
                dve.tensor_scalar(den[:].unsqueeze(2), cx[:, :, H:H + 1], 1e-10, None, ALU.add).then_inc(den_ready, 1)
                dve.wait_ge(den_ready, v + 1)
                dve.reciprocal(rden[:], den[:]).then_inc(rden_ready, 1)

            def close_stats(v):
                for b in range(GB):
                    dve.wait_ge(cn_ready, GB * v + b + 1)
                    dve.bn_stats(stats[:, b], cn[:, b]).then_inc(st_ready, 1)
                dve.wait_ge(st_ready, GB * (v + 1))
                dve.sem_inc(dve_gate, 1)
                for b in range(GB):
                    dve.bn_aggr(mv[:, b], stats[:, b]).then_inc(mv_ready, 1)
                dve.wait_ge(mv_ready, GB * (v + 1))
                dve.tensor_scalar(vs[:].unsqueeze(2), mv[:, :, 1:2], H / (H - 1.0), 1e-30, ALU.mult, ALU.add).then_inc(vs_ready, 1)

            def close_norm(v):
                dve.wait_ge(sd_ready, v + 1)
                dve.tensor_scalar(se[:], sd[:], 1e-3, None, ALU.add).then_inc(se_ready, 1)
                dve.wait_ge(se_ready, v + 1)
                dve.reciprocal(rr[:], se[:]).then_inc(rr_ready, 1)
                dve.wait_ge(rr_ready, v + 1)
                for b in range(GB):
                    i = dve.tensor_scalar(tn[:, b], cn[:, b], mv[:, b, 0:1], rr[:, b:b + 1], ALU.subtract, ALU.mult)
                i.then_inc(tn_ready, 1)

            def out_stats(it, p):
                g = 2 * it + p
                dve.wait_ge(y_ready, g + 1)
                for b in range(GB):
                    dve.bn_stats(ystats[:, b], y[p][:, b]).then_inc(yst_ready, 1)

            def out_variance(it, p):
                g = 2 * it + p
                dve.wait_ge(yst_ready, GB * (g + 1))
                dve.sem_inc(dve_gate, 1)
                for b in range(GB):
                    dve.bn_aggr(ymv[p][:, b], ystats[:, b]).then_inc(ymv_ready, 1)
                dve.wait_ge(ymv_ready, GB * (g + 1))
                dve.tensor_scalar(yv[:].unsqueeze(2), ymv[p][:, :, 1:2], 1e-5, None, ALU.add).then_inc(yv_ready, 1)

            def output(it, p):
                g = 2 * it + p
                dve.wait_ge(yr_ready, g + 1)
                dve.wait_ge(stored[p], 16 * it + 16)
                for b in range(GB):
                    i = dve.tensor_scalar(o[p][:, b], y[p][:, b], ymv[p][:, b, 0:1], yr[p][:, b:b + 1],
                                          ALU.subtract, ALU.mult)
                i.then_inc(o_ready, 1)

            def half(it, k, has_prev, has_next):
                v = n * it + k
                pi, pl, pp = prev_of(it, k)
                ni, nl, np_ = next_of(it, k)
                done = k < 2 and not first(it)
                take_lo(0, v)
                if has_prev:
                    close_sums(v - 1)
                    close_stats(v - 1)
                take_lo(1, v)
                if has_prev:
                    close_norm(v - 1)
                take_lo(2, v)
                if done:
                    out_stats(it - 1, k)
                take_lo(3, v)
                if 0 < k < 3 and not first(it):
                    output(it - 1, k - 1)
                if done:
                    out_variance(it - 1, k)
                if has_next:
                    open_hi(np_, v + 1)
                dve.wait_ge(us_ready, v + 1)
                dve.wait_ge(mask_ready, 2 * it + k % 2 + 1)
                dve.tensor_tensor(um[:], us[:], masks[k % 2][:], ALU.mult).then_inc(um_ready, 1)
                if has_next:
                    open_lo(np_, v + 1)
                dve.wait_ge(um_ready, v + 1)
                dve.tensor_tensor(ua[:], um[:, :, 0, :], um[:, :, 1, :], ALU.add).then_inc(ua_ready, 1)
                dve.wait_ge(e_ready, v + 1)
                dve.tensor_tensor(ea[:], e_s[:], adj_t[k % 2][:], ALU.mult).then_inc(ea_ready, 1)
                dve.wait_ge(ea_ready, v + 1)
                dve.tensor_copy(e_hi[:], ea[:]).then_inc(eh_ready, 1)
                dve.wait_ge(eh_ready, v + 1)
                dve.tensor_tensor(e_lo[:], ea[:], e_hi[:].bitcast(F32), ALU.subtract).then_inc(a_ready, 1)
                take_lo(4, v)

            def last():
                close_sums(n * NIT - 1)
                close_stats(n * NIT - 1)
                close_norm(n * NIT - 1)
                out_stats(NIT - 1, 0)
                out_variance(NIT - 1, 0)
                output(NIT - 1, 0)
                out_stats(NIT - 1, 1)
                out_variance(NIT - 1, 1)
                output(NIT - 1, 1)

            open_hi(0, 0)
            open_lo(0, 0)
            halves(dve, L, half, last)

        @block.tensor
        def _(pe):
            def open_visit(it, l, p, v):
                after(pe, f_ready, v)
                if l == 0:
                    pe.wait_ge(x_loaded[p], 32 * it + 32)
                    src = xin[p]
                else:
                    pe.wait_ge(tn_ready, v - 1)
                    src = tn
                for b in range(GB):
                    for c in range(KC):
                        i = pe.transpose(tp[:, b, c * P:(c + 1) * P], src[:, b, c * P:(c + 1) * P], ident[:])
                    if l == 0:
                        i = pe.transpose(tp[:, b, H:512], adjin[p][:, b], ident[:])
                i.then_inc(tp_ready, 1)

            def project(j, l, p, v):
                if j == 0:
                    pe.wait_ge(h_ready, v + 1)
                before = JOBS * v + j - 2 if j >= RING else JOBS * (v - 1) + (j + 4 if j < 2 else 3)
                after(pe, pj_taken, before)
                bank = pj[:, j % RING, :]
                if j < KC:
                    for s in range(2):
                        out = bank[:, s * GB * S:(s + 1) * GB * S]
                        w = 3 * l + s
                        i = split_product(
                            pe, out, [w_hi[:, w, c, j * P:(j + 1) * P] for c in range(KC)],
                            [w_lo[:, w, c, j * P:(j + 1) * P] for c in range(KC)],
                            [h_hi[p][:, c].rearrange("p b s -> p (b s)") for c in range(KC)],
                            [h_lo[p][:, c].rearrange("p b s -> p (b s)") for c in range(KC)])
                else:
                    b, w = j - KC, 3 * l + 2
                    pe.matmul(bank[:, 0:H], ones[:], b_parts[:, l], start=True, stop=False)
                    i = split_product(
                        pe, bank[:, 0:H], [h_hi[p][:, c, b] for c in range(KC)], [h_lo[p][:, c, b] for c in range(KC)],
                        [w_hi[:, w, c] for c in range(KC)], [w_lo[:, w, c] for c in range(KC)], first=False)
                i.then_inc(pj_ready, 1)

            def scores(p, v):
                after(pe, um_ready, v)
                pe.wait_ge(pj_taken, JOBS * v + KC)
                for b in range(GB):
                    i = split_product(
                        pe, us[:, b], [h_hi[p][:, c, b] for c in range(KC)], [h_lo[p][:, c, b] for c in range(KC)],
                        [g_hi[:, c, :, b] for c in range(KC)], [g_lo[:, c, :, b] for c in range(KC)])
                i.then_inc(us_ready, 1)

            def close_visit(v):
                after(pe, cn_ready, GB * v)
                pe.wait_ge(a_ready, v + 1)
                pe.wait_ge(pj_taken, JOBS * (v + 1))
                for b in range(GB):
                    i = split_product(pe, cx[:, b, 0:HE], [e_hi[:, b]], [e_lo[:, b]], [v_hi[:, b]], [v_lo[:, b]])
                i.then_inc(cx_ready, 1)

            def half(it, k, has_prev, has_next):
                v = n * it + k
                l, p = k // 2, k % 2
                ni, nl, np_ = next_of(it, k)
                project(0, l, p, v)
                if has_prev:
                    close_visit(v - 1)
                for j in range(1, KC + 1):
                    project(j, l, p, v)
                if has_next:
                    open_visit(ni, nl, np_, v + 1)
                scores(p, v)
                project(KC + 1, l, p, v)

            pe.wait_ge(consts, 5)
            open_visit(0, 0, 0, 0)
            pe.wait_ge(w_ready, NW)
            pe.wait_ge(dconst, 8)
            halves(pe, L, half, lambda: close_visit(n * NIT - 1))


def digcn_phase(nc, x_in, adj, w_up_t, b_up, w_self_t, b_self, w_low_t, b_low, ln_g, ln_b, ln_g_cols, ln_b_cols,
                x_out):
    L = w_up_t.shape[0]
    n = 2 * L
    TEMPER = float(H) ** 0.5
    prefix = f"g{L}_"
    with ExitStack() as ctx:
        m = Memory(nc, ctx, prefix)
        raw = m.sb("raw", [3 * L, KC, H])
        w_hi = m.sb("w_hi", [3 * L, KC, H], F32R)
        w_lo = m.sb("w_lo", [3 * L, KC, H], F32R)
        b_raw = m.sb("b_raw", [3 * L, H])
        b_rnd = m.sb("b_rnd", [3 * L, H], F32R)
        b_parts = m.sb("b_parts", [3 * L, H], F32R)
        ones_f = m.sb("ones_f", [P])
        ones = m.sb("ones", [P], F32R)
        ident = m.sb("ident", [P])
        mhalf_c = m.sb("mhalf_c", [GB])
        g_cols = m.sb("g_cols", [KC])
        b_cols = m.sb("b_cols", [KC])
        g_row = m.sb("g_row", [H])
        b_row = m.sb("b_row", [H])
        xin = [m.sb(f"xin{p}", [GB, H]) for p in range(2)]
        adjin = [m.sb(f"adjin{p}", [GB, S]) for p in range(2)]
        xres = [m.sb(f"xres{p}", [GB, H]) for p in range(2)]
        adj_d = [m.sb(f"adj_d{p}", [GB]) for p in range(2)]
        masks = [m.sb(f"masks{p}", [GB, 2, S]) for p in range(2)]
        h_f = m.sb("h_f", [KC, GB, S])
        h_hi = [m.sb(f"h_hi{p}", [KC, GB, S], F32R) for p in range(2)]
        h_lo = [m.sb(f"h_lo{p}", [KC, GB, S], F32R) for p in range(2)]
        v_hi = m.sb("v_hi", [GB, 2, HE], F32R)
        v_lo = m.sb("v_lo", [GB, 2, HE], F32R)
        vself = m.sb("vself", [GB, H])
        mx = m.sb("mx", [GB])
        nb = m.sb("nb", [GB])
        e_s = m.sb("e_s", [GB, S])
        esum = [m.sb(f"esum{p}", [GB]) for p in range(2)]
        diag = m.sb("diag", [GB])
        junk = m.sb("junk", [GB, S])
        dself = [m.sb(f"dself{p}", [GB]) for p in range(2)]
        au = m.sb("au", [GB, 2, S])
        a_hi = m.sb("a_hi", [GB, 2, S], F32R)
        a_lo = m.sb("a_lo", [GB, 2, S], F32R)
        part = m.sb("part", [GB])
        den = m.sb("den", [GB])
        dd = m.sb("dd", [GB])
        cn = m.sb("cn", [GB, H])
        tn = m.sb("tn", [GB, H])
        t2 = m.sb("t2", [GB, H])
        t3 = m.sb("t3", [GB, H])
        y = m.sb("y", [GB, H])
        o = [m.sb(f"o{p}", [GB, H]) for p in range(2)]
        stats = m.sb("stats", [GB, BN])
        mv = m.sb("mv", [GB, 2])
        vs = m.sb("vs", [GB])
        rr = m.sb("rr", [GB])
        ystats = m.sb("ystats", [GB, BN])
        ymv = m.sb("ymv", [GB, 2])
        yv = m.sb("yv", [GB])
        yr = m.sb("yr", [GB])

        tp = m.ps("tp", [GB, 512])
        pj = m.ps("pj", [3, 512])
        us = m.ps("us", [512])
        cx = m.ps("cx", [GB, 512])
        us_s = us[:, 0:GB * S].rearrange("p (b s) -> p b s", b=GB)
        us_a = us[:, :].rearrange("p (b w s) -> p b w s", b=GB, w=2)

        w_loaded = m.sem("w_loaded")
        c_loaded = m.sem("c_loaded")
        w_hi_done = m.sem("w_hi_done")
        w_ready = m.sem("w_ready")
        consts = m.sem("consts")
        dconst = m.sem("dconst")
        pool_gate = m.sem("pool_gate")
        dve_gate = m.sem("dve_gate")
        x_loaded = [m.sem(f"x_loaded{p}") for p in range(2)]
        xin_free = [m.sem(f"xin_free{p}") for p in range(2)]
        tp_ready = m.sem("tp_ready")
        f_ready = m.sem("f_ready")
        hh_ready = m.sem("hh_ready")
        h_ready = m.sem("h_ready")
        pj_ready = m.sem("pj_ready")
        hi_ready = m.sem("hi_ready")
        lo_taken = m.sem("lo_taken")
        self_taken = m.sem("self_taken")
        us_ready = m.sem("us_ready")
        mx_ready = m.sem("mx_ready")
        nb_ready = m.sem("nb_ready")
        e_ready = m.sem("e_ready")
        diag_ready = m.sem("diag_ready")
        d_ready = m.sem("d_ready")
        au_ready = m.sem("au_ready")
        at_ready = m.sem("at_ready")
        ah_ready = m.sem("ah_ready")
        a_ready = m.sem("a_ready")
        cx_ready = m.sem("cx_ready")
        part_ready = m.sem("part_ready")
        den_ready = m.sem("den_ready")
        cn_ready = m.sem("cn_ready")
        dd_ready = m.sem("dd_ready")
        st_ready = m.sem("st_ready")
        mv_ready = m.sem("mv_ready")
        vs_ready = m.sem("vs_ready")
        rr_ready = m.sem("rr_ready")
        tn_ready = m.sem("tn_ready")
        mask_ready = m.sem("mask_ready")
        adjd_ready = m.sem("adjd_ready")
        t2_ready = m.sem("t2_ready")
        t3_ready = m.sem("t3_ready")
        y_ready = m.sem("y_ready")
        yst_ready = m.sem("yst_ready")
        ymv_ready = m.sem("ymv_ready")
        yv_ready = m.sem("yv_ready")
        yr_ready = m.sem("yr_ready")
        o_ready = m.sem("o_ready")
        stored = [m.sem(f"stored{p}") for p in range(2)]

        NW = 3 * L
        RING = 3
        LO_JOBS = 2 * GB
        JOBS = 3 * GB
        ML = L - 1

        block = ctx.enter_context(nc.Block())

        def prev_of(it, k):
            return (it, (k - 1) // 2, (k - 1) % 2) if k else (it - 1, L - 1, 1)

        def next_of(it, k):
            return (it, (k + 1) // 2, (k + 1) % 2) if k < n - 1 else (it + 1, 0, 0)

        @block.sync
        def _(sp):
            for i in range(L):
                for w, a in enumerate((w_up_t, w_low_t, w_self_t)):
                    sp.dma_start(raw[:, 3 * i + w], rows(a[i])).then_inc(w_loaded, 16)
            sp.wait_ge(dconst, 1)
            for i in range(L):
                for w, a in enumerate((b_up, b_low, b_self)):
                    for r in (0, 32):
                        sp.dma_start(b_raw[r:r + 1, 3 * i + w], a[i:i + 1]).then_inc(c_loaded, 16)
            sp.dma_start(g_cols[:], ln_g_cols[0]).then_inc(c_loaded, 16)
            sp.dma_start(b_cols[:], ln_b_cols[0]).then_inc(c_loaded, 16)
            sp.dma_start(g_row[:], ln_g[L - 1].partition_broadcast(P)).then_inc(c_loaded, 16)
            sp.dma_start(b_row[:], ln_b[L - 1].partition_broadcast(P)).then_inc(c_loaded, 16)

            def load(it, p):
                after(sp, xin_free[p], it)
                at = (2 * it + p) * GB
                sp.dma_start(xin[p][:], x_in[bass.ds(at, GB)].rearrange("b s h -> s b h")).then_inc(x_loaded[p], 16)
                sp.dma_start(adjin[p][:], adj[bass.ds(at, GB)].rearrange("b s t -> s b t")).then_inc(x_loaded[p], 16)

            def store(it, p):
                sp.wait_ge(o_ready, 2 * it + p + 1)
                at = (2 * it + p) * GB
                sp.dma_start(x_out[bass.ds(at, GB)].rearrange("b s h -> s b h"), o[p][:]).then_inc(stored[p], 16)

            for p in range(2):
                load(0, p)
            with sp.Fori(1, NIT) as it:
                for p in range(2):
                    load(it, p)
                    store(it - 1, p)
            for p in range(2):
                store(NIT - 1, p)
            for p in range(2):
                sp.wait_ge(stored[p], 16 * NIT + 16)

        CONSTS = 2 * 3 * L + 4

        @block.gpsimd
        def _(pool):
            pool.memset(ones_f[:], 1.0).then_inc(consts, 1)
            pool.memset(mhalf_c[:], -0.5).then_inc(consts, 1)
            pool.memset(ident[:], 0.0).then_inc(consts, 1)
            pool.wait_ge(consts, 3)
            pool.affine_select(out=ident[:], in_=ident[:], compare_op=ALU.not_equal, fill=1.0, base=0,
                               pattern=[[-1, P]], channel_multiplier=1).then_inc(consts, 1)
            pool.wait_ge(c_loaded, 16 * CONSTS)

            def open_visit(it, l, p, v):
                if l == 0:
                    pool.wait_ge(tp_ready, v + 1)
                    pool.sem_inc(pool_gate, 1)
                    pool.affine_select(out=masks[p][:, :, 0, :], in_=adjin[p][:], compare_op=ALU.is_gt, fill=0.0,
                                       base=0, pattern=[[0, GB], [1, S]], channel_multiplier=-1)
                    pool.affine_select(out=masks[p][:, :, 1, :], in_=adjin[p][:], compare_op=ALU.is_gt, fill=0.0,
                                       base=0, pattern=[[0, GB], [-1, S]], channel_multiplier=1).then_inc(mask_ready, 1)
                    after(pool, y_ready, 2 * it + p - 1)
                    pool.wait_ge(adjd_ready, GB * (2 * it + p + 1))
                    pool.sem_inc(pool_gate, 1)
                    pool.tensor_copy(xres[p][:], xin[p][:]).then_inc(xin_free[p], 1)

            def half(it, k, has_prev, has_next):
                v = n * it + k
                pi, pl, pp = prev_of(it, k)
                ni, nl, np_ = next_of(it, k)
                pool.wait_ge(e_ready, GB * (v + 1))
                pool.wait_ge(mask_ready, 2 * it + k % 2 + 1)
                for b in range(GB):
                    i = pool.tensor_tensor(au[:, b], e_s[:, b].unsqueeze(1).broadcast_to([P, 2, S]),
                                           masks[k % 2][:, b], ALU.mult)
                i.then_inc(au_ready, 1)
                if has_prev:
                    close(pi, pl, pp, v - 1)
                if has_next:
                    open_visit(ni, nl, np_, v + 1)

            def close(it, l, p, v):
                pool.wait_ge(vs_ready, v + 1)
                pool.tensor_tensor(rr[:], vs[:], mhalf_c[:], ALU.pow).then_inc(rr_ready, 1)
                if l == L - 1:
                    g = 2 * it + p
                    pool.wait_ge(tn_ready, v + 1)
                    pool.tensor_tensor(t2[:], tn[:], g_row[:].unsqueeze(1).broadcast_to([P, GB, H]), ALU.mult).then_inc(t2_ready, 1)
                    pool.wait_ge(t2_ready, g + 1)
                    pool.tensor_tensor(t3[:], t2[:], b_row[:].unsqueeze(1).broadcast_to([P, GB, H]), ALU.add).then_inc(t3_ready, 1)
                    pool.wait_ge(yv_ready, g + 1)
                    pool.tensor_tensor(yr[:], yv[:], mhalf_c[:], ALU.pow).then_inc(yr_ready, 1)

            open_visit(0, 0, 0, 0)
            halves(pool, L, half, lambda: close(NIT - 1, L - 1, 1, n * NIT - 1))

        @block.scalar
        def _(act):
            act.wait_ge(w_loaded, 16 * NW)
            for w in range(NW):
                act.activation(w_hi[:, w], raw[:, w], ACT.Copy).then_inc(w_hi_done, 1)
            act.wait_ge(c_loaded, 16 * CONSTS)

            def open_visit(l, v):
                act.wait_ge(tp_ready, v + 1)
                if l == 0:
                    for b in range(GB):
                        i = act.activation(h_f[:, :, b, :], tp[:, b, 0:H].rearrange("p (c s) -> p c s", c=KC), ACT.Copy)
                else:
                    for c in range(KC):
                        i = act.activation(h_f[:, c], tp[:, :, c * P:(c + 1) * P], ACT.Relu,
                                           bias=b_cols[:, c:c + 1], scale=g_cols[:, c:c + 1])
                i.then_inc(f_ready, 1)

            def take_hi(j, v):
                act.wait_ge(pj_ready, JOBS * v + j + 1)
                after(act, cx_ready, v)
                act.activation(v_hi[:, j // 2, j % 2, 0:H], pj[:, j % RING, 0:H], ACT.Copy).then_inc(hi_ready, 1)

            def take_self(b, p, v):
                act.wait_ge(pj_ready, JOBS * v + LO_JOBS + b + 1)
                act.wait_ge(d_ready, v + 1)
                after(act, cn_ready, v)
                act.activation(vself[:, b], pj[:, (LO_JOBS + b) % RING, 0:H], ACT.Copy,
                               scale=dself[p][:, b:b + 1]).then_inc(self_taken, 1)

            def exps(it, l, p, v):
                act.wait_ge(us_ready, v + 1)
                after(act, au_ready, v)
                if l:
                    act.wait_ge(nb_ready, ML * 2 * it + 2 * (l - 1) + p + 1)
                for b in range(GB):
                    act.activation(e_s[:, b], us_s[:, b], ACT.Exp, scale=1.0 / TEMPER,
                                   bias=nb[:, b:b + 1] if l else 0.0,
                                   accum_out=esum[p][:, b:b + 1]).then_inc(e_ready, 1)

            def take_attention(v):
                act.wait_ge(at_ready, v + 1)
                act.activation(a_hi[:], us_a, ACT.Copy).then_inc(ah_ready, 1)

            def half(it, k, has_prev, has_next):
                v = n * it + k
                ni, nl, np_ = next_of(it, k)
                exps(it, k // 2, k % 2, v)
                for j in range(LO_JOBS):
                    take_hi(j, v)
                take_attention(v)
                if has_next:
                    open_visit(nl, v + 1)
                for b in range(GB):
                    take_self(b, k % 2, v)

            open_visit(0, 0)
            halves(act, L, half, lambda: None)

        @block.vector
        def _(dve):
            dve.memset(b_raw[:], 0.0).then_inc(dconst, 1)
            for w in range(NW):
                dve.wait_ge(w_hi_done, w + 1)
                dve.tensor_tensor(w_lo[:, w], raw[:, w], w_hi[:, w].bitcast(F32), ALU.subtract).then_inc(w_ready, 1)
            dve.wait_ge(consts, 4)
            dve.tensor_copy(ones[:], ones_f[:]).then_inc(dconst, 1)
            dve.memset(v_hi[:, :, :, H:HE].bitcast(F32), 1.0).then_inc(dconst, 1)
            dve.memset(v_lo[:, :, :, H:HE].bitcast(F32), 0.0).then_inc(dconst, 1)
            dve.memset(b_parts[:].bitcast(F32), 0.0).then_inc(dconst, 1)
            dve.wait_ge(c_loaded, 16 * CONSTS)
            dve.tensor_copy(b_rnd[:], b_raw[:]).then_inc(dconst, 1)
            dve.wait_ge(dconst, 6)
            dve.tensor_copy(b_parts[0:1], b_raw[0:1]).then_inc(dconst, 1)
            dve.tensor_tensor(b_parts[32:33], b_raw[32:33], b_rnd[32:33].bitcast(F32), ALU.subtract).then_inc(dconst, 1)
            for p in range(2):
                dve.engine_nop().then_inc(stored[p], 16)

            def open_visit(it, l, p, v):
                if l == 0:
                    dve.wait_ge(x_loaded[p], 32 * it + 32)
                    for b in range(GB):
                        dve.tensor_tensor_reduce(junk[:, b], adjin[p][:, b], ident[:], 1.0, 0.0, ALU.mult, ALU.add,
                                                 adj_d[p][:, b:b + 1]).then_inc(adjd_ready, 1)
                dve.wait_ge(f_ready, v + 1)
                dve.tensor_copy(h_hi[p][:], h_f[:]).then_inc(hh_ready, 1)
                dve.wait_ge(hh_ready, v + 1)
                dve.tensor_tensor(h_lo[p][:], h_f[:], h_hi[p][:].bitcast(F32), ALU.subtract).then_inc(h_ready, 1)

            def row_max(it, l, p, v):
                c = ML * 2 * it + 2 * (l - 1) + p
                dve.wait_ge(us_ready, v + 1)
                dve.tensor_reduce(mx[:], us_s, AX_X, ALU.max).then_inc(mx_ready, 1)
                dve.wait_ge(mx_ready, c + 1)
                dve.tensor_scalar(nb[:], mx[:], -1.0 / TEMPER, None, ALU.mult).then_inc(nb_ready, 1)

            def diagonal(it, p, v):
                dve.wait_ge(e_ready, GB * (v + 1))
                for b in range(GB):
                    dve.tensor_tensor_reduce(junk[:, b], e_s[:, b], ident[:], 1.0, 0.0, ALU.mult, ALU.add,
                                             diag[:, b:b + 1]).then_inc(diag_ready, 1)
                dve.wait_ge(diag_ready, GB * (v + 1))
                dve.wait_ge(adjd_ready, GB * (2 * it + p + 1))
                dve.tensor_tensor(dself[p][:], diag[:], adj_d[p][:], ALU.mult).then_inc(d_ready, 1)

            def take_lo(j, v):
                dve.wait_ge(hi_ready, LO_JOBS * v + j + 1)
                dve.tensor_tensor(v_lo[:, j // 2, j % 2, 0:H], pj[:, j % RING, 0:H],
                                  v_hi[:, j // 2, j % 2, 0:H].bitcast(F32), ALU.subtract).then_inc(lo_taken, 1)

            def take_attention(v):
                dve.wait_ge(ah_ready, v + 1)
                dve.tensor_tensor(a_lo[:], us_a, a_hi[:].bitcast(F32), ALU.subtract).then_inc(a_ready, 1)

            def close_sums(p, v):
                dve.wait_ge(cx_ready, v + 1)
                dve.scalar_tensor_tensor(part[:].unsqueeze(2), esum[p][:].unsqueeze(2), 1e-10, cx[:, :, H:H + 1],
                                         ALU.mult, ALU.add).then_inc(part_ready, 1)
                dve.wait_ge(self_taken, GB * (v + 1))
                dve.tensor_tensor(cn[:], cx[:, :, 0:H], vself[:], ALU.add).then_inc(cn_ready, 1)
                dve.wait_ge(part_ready, v + 1)
                dve.tensor_tensor(den[:], part[:], dself[p][:], ALU.add).then_inc(den_ready, 1)
                dve.wait_ge(den_ready, v + 1)
                dve.scalar_tensor_tensor(dd[:], den[:], 1e-12, den[:], ALU.mult, ALU.mult).then_inc(dd_ready, 1)

            def close_stats(v):
                dve.wait_ge(cn_ready, v + 1)
                for b in range(GB):
                    dve.bn_stats(stats[:, b], cn[:, b]).then_inc(st_ready, 1)
                dve.wait_ge(st_ready, GB * (v + 1))
                dve.sem_inc(dve_gate, 1)
                for b in range(GB):
                    dve.bn_aggr(mv[:, b], stats[:, b]).then_inc(mv_ready, 1)
                dve.wait_ge(mv_ready, GB * (v + 1))
                dve.wait_ge(dd_ready, v + 1)
                dve.tensor_tensor(vs[:].unsqueeze(2), mv[:, :, 1:2], dd[:].unsqueeze(2), ALU.add).then_inc(vs_ready, 1)

            def close_norm(v):
                dve.wait_ge(rr_ready, v + 1)
                for b in range(GB):
                    i = dve.tensor_scalar(tn[:, b], cn[:, b], mv[:, b, 0:1], rr[:, b:b + 1], ALU.subtract, ALU.mult)
                i.then_inc(tn_ready, 1)

            def residual(it, p):
                g = 2 * it + p
                dve.wait_ge(t3_ready, g + 1)
                dve.scalar_tensor_tensor(y[:], t3[:], 0.0, xres[p][:], ALU.max, ALU.add).then_inc(y_ready, 1)
                dve.wait_ge(y_ready, g + 1)
                for b in range(GB):
                    dve.bn_stats(ystats[:, b], y[:, b]).then_inc(yst_ready, 1)
                dve.wait_ge(yst_ready, GB * (g + 1))
                dve.sem_inc(dve_gate, 1)
                for b in range(GB):
                    dve.bn_aggr(ymv[:, b], ystats[:, b]).then_inc(ymv_ready, 1)
                dve.wait_ge(ymv_ready, GB * (g + 1))
                dve.tensor_scalar(yv[:].unsqueeze(2), ymv[:, :, 1:2], 1e-5, None, ALU.add).then_inc(yv_ready, 1)

            def output(it, p):
                g = 2 * it + p
                dve.wait_ge(yr_ready, g + 1)
                dve.wait_ge(stored[p], 16 * it + 16)
                for b in range(GB):
                    i = dve.tensor_scalar(o[p][:, b], y[:, b], ymv[:, b, 0:1], yr[:, b:b + 1], ALU.subtract, ALU.mult)
                i.then_inc(o_ready, 1)

            def half(it, k, has_prev, has_next):
                v = n * it + k
                l, p = k // 2, k % 2
                pi, pl, pp = prev_of(it, k)
                ni, nl, np_ = next_of(it, k)
                if l:
                    row_max(it, l, p, v)
                diagonal(it, p, v)
                take_lo(0, v)
                if has_prev:
                    close_sums(pp, v - 1)
                take_lo(1, v)
                if has_prev:
                    close_stats(v - 1)
                take_lo(2, v)
                if has_prev:
                    close_norm(v - 1)
                take_lo(3, v)
                take_attention(v)
                if has_next:
                    open_visit(ni, nl, np_, v + 1)
                if has_prev and pl == L - 1:
                    residual(pi, pp)
                    output(pi, pp)

            def last():
                v = n * NIT - 1
                close_sums(1, v)
                close_stats(v)
                close_norm(v)
                residual(NIT - 1, 1)
                output(NIT - 1, 1)

            open_visit(0, 0, 0, 0)
            halves(dve, L, half, last)

        @block.tensor
        def _(pe):
            def open_visit(it, l, p, v):
                after(pe, f_ready, v)
                if l == 0:
                    pe.wait_ge(x_loaded[p], 32 * it + 32)
                    src = xin[p]
                else:
                    pe.wait_ge(tn_ready, v - 1)
                    src = tn
                for b in range(GB):
                    for c in range(KC):
                        i = pe.transpose(tp[:, b, c * P:(c + 1) * P], src[:, b, c * P:(c + 1) * P], ident[:])
                i.then_inc(tp_ready, 1)

            def scores(v):
                pe.wait_ge(f_ready, v + 1)
                after(pe, a_ready, v)
                for b in range(GB):
                    for c in range(KC):
                        i = pe.matmul(us_s[:, b], h_f[:, c, b], h_f[:, c, b], start=(c == 0), stop=(c == KC - 1))
                i.then_inc(us_ready, 1)

            def project(j, l, p, v):
                if j == 0:
                    pe.wait_ge(h_ready, v + 1)
                if j in (1, 2):
                    after(pe, self_taken, GB * (v - 1) + j)
                else:
                    after(pe, lo_taken, LO_JOBS * v + (j - RING + 1 if j else 0))
                b, s = (j // 2, j % 2) if j < LO_JOBS else (j - LO_JOBS, 2)
                w = 3 * l + s
                out = pj[:, j % RING, 0:H]
                pe.matmul(out, ones[:], b_parts[:, w], start=True, stop=False)
                split_product(
                    pe, out, [h_hi[p][:, c, b] for c in range(KC)], [h_lo[p][:, c, b] for c in range(KC)],
                    [w_hi[:, w, c] for c in range(KC)], [w_lo[:, w, c] for c in range(KC)], first=False).then_inc(pj_ready, 1)

            def transpose_attention(v):
                pe.wait_ge(e_ready, GB * (v + 1))
                pe.wait_ge(au_ready, v + 1)
                for b in range(GB):
                    for s in range(2):
                        i = pe.transpose(us_a[:, b, s], au[:, b, s], ident[:])
                i.then_inc(at_ready, 1)

            def close_visit(v):
                after(pe, cn_ready, v)
                pe.wait_ge(a_ready, v + 1)
                pe.wait_ge(lo_taken, LO_JOBS * (v + 1))
                for b in range(GB):
                    i = split_product(pe, cx[:, b, 0:HE], [a_hi[:, b, s] for s in range(2)], [a_lo[:, b, s] for s in range(2)],
                                      [v_hi[:, b, s] for s in range(2)], [v_lo[:, b, s] for s in range(2)])
                i.then_inc(cx_ready, 1)

            def half(it, k, has_prev, has_next):
                v = n * it + k
                l, p = k // 2, k % 2
                ni, nl, np_ = next_of(it, k)
                scores(v)
                project(0, l, p, v)
                if has_prev:
                    close_visit(v - 1)
                for j in range(1, LO_JOBS):
                    project(j, l, p, v)
                transpose_attention(v)
                if has_next:
                    open_visit(ni, nl, np_, v + 1)
                for j in range(LO_JOBS, JOBS):
                    project(j, l, p, v)

            pe.wait_ge(consts, 4)
            open_visit(0, 0, 0, 0)
            pe.wait_ge(w_ready, NW)
            pe.wait_ge(dconst, 8)
            halves(pe, L, half, lambda: close_visit(n * NIT - 1))


def mha_phase(nc, x_in, adj, w_q_t, w_k_t, w_v_t, w_o_t, b_v, b_o, x_out):
    n = 2
    HEADS = 12
    D = H // HEADS
    R = P // D
    SCALE = float(H) ** -0.5
    HJ = HEADS // 3
    with ExitStack() as ctx:
        m = Memory(nc, ctx, "mh_")
        raw = m.sb("raw", [4, KC, H])
        w_hi = m.sb("w_hi", [4, KC, H], F32R)
        w_lo = m.sb("w_lo", [4, KC, H], F32R)
        bv_row = m.sb("bv_row", [H])
        bo_row = m.sb("bo_row", [H])
        ident = m.sb("ident", [P])
        mhalf_c = m.sb("mhalf_c", [GB])
        xin = [m.sb(f"xin{p}", [GB, H]) for p in range(2)]
        adjin = [m.sb(f"adjin{p}", [GB, S]) for p in range(2)]
        xres = [m.sb(f"xres{p}", [GB, H]) for p in range(2)]
        h_f = m.sb("h_f", [KC, GB, S])
        h_hi = m.sb("h_hi", [KC, GB, S], F32R)
        h_lo = m.sb("h_lo", [KC, GB, S], F32R)
        qk = m.sb("qk", [KC, 2, GB, S])
        v_s = [m.sb(f"v_s{p}", [GB, H]) for p in range(2)]
        a_s = [m.sb(f"a_s{b}", [HEADS, S]) for b in range(GB)]
        e_s = [m.sb(f"e_s{b}", [HEADS, S]) for b in range(GB)]
        mx = [m.sb(f"mx{b}", [HEADS]) for b in range(GB)]
        mn = [m.sb(f"mn{b}", [HEADS]) for b in range(GB)]
        nb = [m.sb(f"nb{b}", [HEADS]) for b in range(GB)]
        zero = [m.sb(f"zero{b}", [HEADS]) for b in range(GB)]
        pad = [m.sb(f"pad{b}", [HEADS]) for b in range(GB)]
        keep = [m.sb(f"keep{b}", [HEADS]) for b in range(GB)]
        esum = [m.sb(f"esum{b}", [HEADS]) for b in range(GB)]
        rec = m.sb("rec", [HEADS])
        rd = [m.sb(f"rd{b}", [HEADS]) for b in range(GB)]
        at = m.sb("at", [HEADS, S])
        o_hi = m.sb("o_hi", [KC, S], F32R)
        o_lo = m.sb("o_lo", [KC, S], F32R)
        y = m.sb("y", [GB, H])
        o = [m.sb(f"o{p}", [GB, H]) for p in range(2)]
        ystats = m.sb("ystats", [GB, BN])
        ymv = m.sb("ymv", [GB, 2])
        yv = m.sb("yv", [GB])
        yr = m.sb("yr", [GB])

        ra = m.ps("ra", [2, 512])
        rb = m.ps("rb", [2, 512])
        sc = m.ps("sc", [R, 512])

        w_loaded = m.sem("w_loaded")
        c_loaded = m.sem("c_loaded")
        w_hi_done = m.sem("w_hi_done")
        w_ready = m.sem("w_ready")
        consts = m.sem("consts")
        dve_gate = m.sem("dve_gate")
        x_loaded = [m.sem(f"x_loaded{p}") for p in range(2)]
        adj_loaded = [m.sem(f"adj_loaded{p}") for p in range(2)]
        xin_free = [m.sem(f"xin_free{p}") for p in range(2)]
        tp_ready = m.sem("tp_ready")
        f_ready = m.sem("f_ready")
        hh_ready = m.sem("hh_ready")
        h_ready = m.sem("h_ready")
        qk_done = m.sem("qk_done")
        qk_taken = m.sem("qk_taken")
        v_done = m.sem("v_done")
        v_taken = m.sem("v_taken")
        sc_ready = m.sem("sc_ready")
        a_ready = m.sem("a_ready")
        mx_ready = m.sem("mx_ready")
        nb_ready = m.sem("nb_ready")
        mn_ready = m.sem("mn_ready")
        zero_ready = m.sem("zero_ready")
        pad_ready = m.sem("pad_ready")
        keep_ready = m.sem("keep_ready")
        e_ready = m.sem("e_ready")
        rec_ready = m.sem("rec_ready")
        rd_ready = m.sem("rd_ready")
        p_ready = m.sem("p_ready")
        et_done = m.sem("et_done")
        et_taken = m.sem("et_taken")
        av_done = m.sem("av_done")
        oh_ready = m.sem("oh_ready")
        av_taken = m.sem("av_taken")
        wo_done = m.sem("wo_done")
        wo_taken = m.sem("wo_taken")
        yst_ready = m.sem("yst_ready")
        ymv_ready = m.sem("ymv_ready")
        yv_ready = m.sem("yv_ready")
        yr_ready = m.sem("yr_ready")
        o_ready = m.sem("o_ready")
        stored = [m.sem(f"stored{p}") for p in range(2)]

        block = ctx.enter_context(nc.Block())

        def a_bank(job, k):
            return ra[:, (job + k) % 2, :]

        def e_bank(i):
            return rb[:, (i if i < 3 else i + 1) % 2, :]

        def v_bank():
            return rb[:, 1, :]

        def first(it):
            return isinstance(it, int) and it == 0

        def prev_of(it, k):
            return (it, 0) if k else (it - 1, 1)

        def next_of(it, k):
            return (it, 1) if k == 0 else (it + 1, 0)

        @block.sync
        def _(sp):
            for w, a in enumerate((w_q_t, w_k_t, w_v_t, w_o_t)):
                sp.dma_start(raw[:, w], rows(a)).then_inc(w_loaded, 16)
            sp.dma_start(bv_row[:], b_v.partition_broadcast(P)).then_inc(c_loaded, 16)
            sp.dma_start(bo_row[:], b_o.partition_broadcast(P)).then_inc(c_loaded, 16)

            def load_x(it, p):
                g = 2 * it + p
                after(sp, xin_free[p], it)
                sp.dma_start(xin[p][:], x_in[bass.ds(g * GB, GB)].rearrange("b s h -> s b h")).then_inc(x_loaded[p], 16)

            def load_adj(it, p):
                g = 2 * it + p
                after(sp, a_ready, GB * R * (g - 1))
                sp.dma_start(adjin[p][:], adj[bass.ds(g * GB, GB)].rearrange("b s t -> s b t")).then_inc(adj_loaded[p], 16)

            def store(it, p):
                sp.wait_ge(o_ready, 2 * it + p + 1)
                g = (2 * it + p) * GB
                sp.dma_start(x_out[bass.ds(g, GB)].rearrange("b s h -> s b h"), o[p][:]).then_inc(stored[p], 16)

            for it in range(2):
                for p in range(2):
                    load_x(it, p)
                    load_adj(it, p)
            with sp.Fori(1, NIT - 1) as it:
                for p in range(2):
                    load_x(it + 1, p)
                    store(it - 1, p)
                    load_adj(it + 1, p)
            for it in (NIT - 2, NIT - 1):
                for p in range(2):
                    store(it, p)
            for p in range(2):
                sp.wait_ge(stored[p], 16 * NIT + 16)

        @block.gpsimd
        def _(pool):
            pool.memset(mhalf_c[:], -0.5).then_inc(consts, 1)
            pool.memset(ident[:], 0.0).then_inc(consts, 1)
            pool.wait_ge(consts, 2)
            pool.affine_select(out=ident[:], in_=ident[:], compare_op=ALU.not_equal, fill=1.0, base=0,
                               pattern=[[-1, P]], channel_multiplier=1).then_inc(consts, 1)

            def normalise(b, v):
                pool.wait_ge(rd_ready, GB * v + b + 1)
                for i in range(3):
                    heads = slice(HJ * i, HJ * (i + 1))
                    pool.tensor_tensor(a_s[b][:, heads], e_s[b][:, heads],
                                       rd[b][:, heads].unsqueeze(2).broadcast_to([P, HJ, S]), ALU.mult).then_inc(p_ready, 1)

            def out_norm(v):
                pool.wait_ge(yv_ready, v + 1)
                pool.tensor_tensor(yr[:], yv[:], mhalf_c[:], ALU.pow).then_inc(yr_ready, 1)

            def half(it, k, has_prev, has_next):
                v = n * it + k
                if has_prev:
                    normalise(0, v - 1)
                if not first(it):
                    out_norm(v - 2)
                if has_prev:
                    normalise(1, v - 1)

            def last():
                v = n * NIT - 1
                normalise(0, v)
                out_norm(v - 1)
                normalise(1, v)
                out_norm(v)

            halves(pool, 1, half, last)

        @block.scalar
        def _(act):
            act.wait_ge(w_loaded, 16 * 4)
            for w in range(4):
                act.activation(w_hi[:, w], raw[:, w], ACT.Copy).then_inc(w_hi_done, 1)

            def open_visit(b, v, k):
                act.wait_ge(tp_ready, GB * v + b + 1)
                after(act, h_ready, GB * (v - 1) + b + 1)
                act.activation(h_f[:, :, b, :], a_bank(5 + 2 * b, k)[:, 0:H].rearrange("p (c s) -> p c s", c=KC),
                               ACT.Copy).then_inc(f_ready, 1)

            def take_qk(c, k, v):
                act.wait_ge(qk_done, KC * v + c + 1)
                act.activation(qk[:, c], a_bank(c, k).rearrange("p (w b s) -> p w b s", w=2, b=GB),
                               ACT.Copy).then_inc(qk_taken, 1)

            def take_e(b, parts, v):
                for i in parts:
                    act.wait_ge(et_done, 3 * (GB * v + b) + i + 1)
                    act.activation(at[:, HJ * i:HJ * (i + 1)], e_bank(3 * b + i).rearrange("p (h s) -> p h s", h=HJ),
                                   ACT.Copy).then_inc(et_taken, 1)

            def take_o(b, k, v):
                act.wait_ge(av_done, GB * v + b + 1)
                act.activation(o_hi[:], a_bank(3 + 3 * b, k)[:, 0:H].rearrange("p (c s) -> p c s", c=KC),
                               ACT.Copy).then_inc(oh_ready, 1)

            def exps(part, b, v):
                if part == 0:
                    act.wait_ge(nb_ready, GB * v + b + 1)
                for h in range(HJ * part, HJ * (part + 1)):
                    act.activation(e_s[b][:, h], a_s[b][:, h], ACT.Exp, bias=nb[b][:, h:h + 1],
                                   accum_out=esum[b][:, h:h + 1]).then_inc(e_ready, 1)

            def half(it, k, has_prev, has_next):
                v = n * it + k
                take_qk(0, k, v)
                if has_prev:
                    exps(0, 1, v - 1)
                take_qk(1, k, v)
                if has_prev:
                    take_e(0, (0, 1), v - 1)
                    exps(1, 1, v - 1)
                take_qk(2, k, v)
                if has_prev:
                    take_e(0, (2,), v - 1)
                    exps(2, 1, v - 1)
                    take_o(0, k, v - 1)
                    take_e(1, (0, 1, 2), v - 1)
                exps(0, 0, v)
                if has_next:
                    open_visit(0, v + 1, k)
                if has_prev:
                    take_o(1, k, v - 1)
                if has_next:
                    open_visit(1, v + 1, k)
                exps(1, 0, v)
                exps(2, 0, v)

            def last():
                v = n * NIT - 1
                exps(0, 1, v)
                take_e(0, (0, 1, 2), v)
                exps(1, 1, v)
                exps(2, 1, v)
                take_o(0, 0, v)
                take_e(1, (0, 1, 2), v)
                take_o(1, 0, v)

            for b in range(GB):
                open_visit(b, 0, -1)
            halves(act, 1, half, last)

        @block.vector
        def _(dve):
            for w in range(4):
                dve.wait_ge(w_hi_done, w + 1)
                dve.tensor_tensor(w_lo[:, w], raw[:, w], w_hi[:, w].bitcast(F32), ALU.subtract).then_inc(w_ready, 1)
            dve.wait_ge(c_loaded, 16 * 2)
            for p in range(2):
                dve.engine_nop().then_inc(stored[p], 16)

            def open_visit(b, v):
                dve.wait_ge(f_ready, GB * v + b + 1)
                dve.tensor_copy(h_hi[:, :, b], h_f[:, :, b]).then_inc(hh_ready, 1)
                dve.wait_ge(hh_ready, GB * v + b + 1)
                dve.tensor_tensor(h_lo[:, :, b], h_f[:, :, b], h_hi[:, :, b].bitcast(F32), ALU.subtract).then_inc(h_ready, 1)

            def keep_x(it, p, v):
                dve.wait_ge(x_loaded[p], 16 * it + 16)
                dve.wait_ge(tp_ready, GB * (v + 1))
                dve.tensor_tensor(xres[p][:], xin[p][:], bo_row[:].unsqueeze(1).broadcast_to([P, GB, H]),
                                  ALU.add).then_inc(xin_free[p], 1)

            def take_v(b, p, v):
                dve.wait_ge(v_done, GB * v + b + 1)
                dve.tensor_tensor(v_s[p][:, b], v_bank()[:, 0:H], bv_row[:], ALU.add).then_inc(v_taken, 1)

            def scale_scores(it, b, p, v):
                dve.wait_ge(adj_loaded[p], 16 * it + 16)
                dve.wait_ge(sc_ready, GB * v + b + 1)
                for r in range(R):
                    dve.scalar_tensor_tensor(a_s[b][:, KC * r:KC * (r + 1)], sc[:, r, 0:KC * S].rearrange("p (c s) -> p c s", c=KC),
                                             SCALE, adjin[p][:, b].unsqueeze(1).broadcast_to([P, KC, S]),
                                             ALU.mult, ALU.add).then_inc(a_ready, 1)

            def find_max(b, v):
                dve.wait_ge(a_ready, R * (GB * v + b + 1))
                dve.tensor_reduce(mx[b][:], a_s[b][:], AX_X, ALU.max).then_inc(mx_ready, 1)
                dve.wait_ge(mx_ready, GB * v + b + 1)
                dve.tensor_scalar(nb[b][:], mx[b][:], -1.0, None, ALU.mult).then_inc(nb_ready, 1)

            def find_pads(b, v):
                u = GB * v + b
                dve.tensor_reduce(mn[b][:], a_s[b][:], AX_X, ALU.min).then_inc(mn_ready, 1)
                dve.wait_ge(mn_ready, u + 1)
                dve.tensor_scalar(zero[b][:], mn[b][:], 0.0, None, ALU.is_equal).then_inc(zero_ready, 1)
                dve.wait_ge(zero_ready, u + 1)
                dve.scalar_tensor_tensor(pad[b][:], mx[b][:], 0.0, zero[b][:], ALU.is_equal, ALU.mult).then_inc(pad_ready, 1)
                dve.wait_ge(pad_ready, u + 1)
                dve.tensor_scalar(keep[b][:], pad[b][:], -1.0, 1.0, ALU.mult, ALU.add).then_inc(keep_ready, 1)

            def sums(b, v):
                u = GB * v + b
                dve.wait_ge(e_ready, HEADS * (u + 1))
                dve.reciprocal(rec[:], esum[b][:]).then_inc(rec_ready, 1)
                dve.wait_ge(rec_ready, u + 1)
                dve.wait_ge(keep_ready, u + 1)
                dve.tensor_tensor(rd[b][:], rec[:], keep[b][:], ALU.mult).then_inc(rd_ready, 1)

            def take_o(b, k, v):
                dve.wait_ge(oh_ready, GB * v + b + 1)
                dve.tensor_tensor(o_lo[:], a_bank(3 + 3 * b, k)[:, 0:H].rearrange("p (c s) -> p c s", c=KC),
                                  o_hi[:].bitcast(F32), ALU.subtract).then_inc(av_taken, 1)

            def add_x(it, b, p, k, v):
                u = GB * v + b
                dve.wait_ge(wo_done, u + 1)
                dve.wait_ge(xin_free[p], it + 1)
                dve.tensor_tensor(y[:, b], a_bank(4 + 4 * b, k)[:, 0:H], xres[p][:, b], ALU.add).then_inc(wo_taken, 1)

            def out_stats(b, v):
                u = GB * v + b
                dve.wait_ge(wo_taken, u + 1)
                dve.bn_stats(ystats[:, b], y[:, b]).then_inc(yst_ready, 1)
                dve.wait_ge(yst_ready, u + 1)
                dve.sem_inc(dve_gate, 1)
                dve.bn_aggr(ymv[:, b], ystats[:, b]).then_inc(ymv_ready, 1)

            def variance(v):
                dve.wait_ge(ymv_ready, GB * (v + 1))
                dve.tensor_scalar(yv[:].unsqueeze(2), ymv[:, :, 1:2], 1e-5, None, ALU.add).then_inc(yv_ready, 1)

            def output(it, p):
                g = 2 * it + p
                dve.wait_ge(yr_ready, g + 1)
                dve.wait_ge(stored[p], 16 * it + 16)
                for b in range(GB):
                    i = dve.tensor_scalar(o[p][:, b], y[:, b], ymv[:, b, 0:1], yr[:, b:b + 1], ALU.subtract, ALU.mult)
                i.then_inc(o_ready, 1)

            def half(it, k, has_prev, has_next):
                v = n * it + k
                pi, pp = prev_of(it, k)
                ni, np_ = next_of(it, k)
                if has_prev:
                    find_pads(1, v - 1)
                if not first(it):
                    output(it - 1, k)
                take_v(0, k, v)
                if has_prev:
                    sums(1, v - 1)
                    take_o(0, k, v - 1)
                scale_scores(it, 0, k, v)
                find_max(0, v)
                if has_prev:
                    add_x(pi, 0, pp, k, v - 1)
                    out_stats(0, v - 1)
                take_v(1, k, v)
                if has_next:
                    open_visit(0, v + 1)
                if has_prev:
                    take_o(1, k, v - 1)
                if has_next:
                    open_visit(1, v + 1)
                find_pads(0, v)
                scale_scores(it, 1, k, v)
                sums(0, v)
                if has_prev:
                    add_x(pi, 1, pp, k, v - 1)
                find_max(1, v)
                if has_prev:
                    out_stats(1, v - 1)
                    variance(v - 1)
                if has_next:
                    keep_x(ni, np_, v + 1)

            def last():
                v = n * NIT - 1
                find_pads(1, v)
                output(NIT - 1, 0)
                sums(1, v)
                take_o(0, 0, v)
                add_x(NIT - 1, 0, 1, 0, v)
                out_stats(0, v)
                take_o(1, 0, v)
                add_x(NIT - 1, 1, 1, 0, v)
                out_stats(1, v)
                variance(v)
                output(NIT - 1, 1)

            for b in range(GB):
                open_visit(b, 0)
            keep_x(0, 0, 0)
            halves(dve, 1, half, last)

        @block.tensor
        def _(pe):
            def open_visit(it, b, p, v, k):
                if b == 0:
                    pe.wait_ge(x_loaded[p], 16 * it + 16)
                    after(pe, qk_taken, KC * v)
                    after(pe, av_taken, GB * (v - 2) + 1)
                else:
                    pe.wait_ge(f_ready, GB * v + 1)
                for c in range(KC):
                    i = pe.transpose(a_bank(5 + 2 * b, k)[:, c * P:(c + 1) * P], xin[p][:, b, c * P:(c + 1) * P], ident[:])
                i.then_inc(tp_ready, 1)

            def project_qk(c, k, v):
                if c == 0:
                    pe.wait_ge(h_ready, GB * (v + 1))
                elif c == 1:
                    after(pe, wo_taken, GB * (v - 1))
                else:
                    pe.wait_ge(qk_taken, KC * v + 1)
                for w in range(2):
                    i = split_product(
                        pe, a_bank(c, k)[:, w * GB * S:(w + 1) * GB * S],
                        [w_hi[:, w, i, c * P:(c + 1) * P] for i in range(KC)],
                        [w_lo[:, w, i, c * P:(c + 1) * P] for i in range(KC)],
                        [h_hi[:, i].rearrange("p b s -> p (b s)") for i in range(KC)],
                        [h_lo[:, i].rearrange("p b s -> p (b s)") for i in range(KC)])
                i.then_inc(qk_done, 1)

            def project_v(b, v, has_prev):
                if has_prev:
                    pe.wait_ge(et_taken, 6 * (v - 1) + 3 * b + 2)
                else:
                    after(pe, v_taken, GB * v + b)
                split_product(pe, v_bank()[:, 0:H], [h_hi[:, c, b] for c in range(KC)], [h_lo[:, c, b] for c in range(KC)],
                              [w_hi[:, 2, c] for c in range(KC)], [w_lo[:, 2, c] for c in range(KC)]).then_inc(v_done, 1)

            def scores(b, v):
                pe.wait_ge(qk_taken, KC * (v + 1))
                after(pe, a_ready, R * (GB * v + b))
                for c in range(KC):
                    for r in range(R):
                        q = slice(D * r, D * (r + 1))
                        i = pe.matmul(sc[:, r, c * S:(c + 1) * S], qk[q, c, 0, b], qk[q, c, 1, b], start=True, stop=True)
                i.then_inc(sc_ready, 1)

            def transpose_attention(b, parts, v, projects):
                for i in parts:
                    pe.wait_ge(p_ready, 3 * (GB * v + b) + i + 1)
                    if (b, i) == (0, 0):
                        after(pe, et_taken, 6 * v)
                    elif (b, i) == (0, 1):
                        pe.wait_ge(v_taken, GB * (v + 1))
                    elif (b, i) == (1, 1) and projects:
                        pe.wait_ge(v_taken, GB * (v + 1) + 1)
                    else:
                        pe.wait_ge(et_taken, 6 * v + 3 * b + i - (1 if b == 0 or i != 0 else 0))
                    for h in range(HJ):
                        t = pe.transpose(e_bank(3 * b + i)[:, h * S:(h + 1) * S], a_s[b][:, HJ * i + h], ident[:])
                    t.then_inc(et_done, 1)

            def attend(b, p, k, v, projects):
                pe.wait_ge(et_taken, 6 * v + 3 * b + 3)
                if b == 0:
                    if projects:
                        pe.wait_ge(qk_taken, KC * (v + 1) + 2)
                    else:
                        after(pe, wo_taken, GB * v)
                        after(pe, av_taken, GB * v)
                else:
                    pe.wait_ge(wo_taken, GB * v + 1)
                out = a_bank(3 + 3 * b, k)
                for c in range(KC):
                    for r in range(R):
                        h = R * c + r
                        i = pe.matmul(out[D * r:D * (r + 1), c * S:(c + 1) * S], v_s[p][:, b, h * D:(h + 1) * D],
                                      at[:, KC * r + c], start=True, stop=True)
                i.then_inc(av_done, 1)

            def project_out(b, k, v, projects):
                pe.wait_ge(av_taken, GB * v + b + 1)
                if b == 0 and projects:
                    pe.wait_ge(qk_taken, KC * (v + 2))
                split_product(pe, a_bank(4 + 4 * b, k)[:, 0:H], [o_hi[:, c] for c in range(KC)], [o_lo[:, c] for c in range(KC)],
                              [w_hi[:, 3, c] for c in range(KC)], [w_lo[:, 3, c] for c in range(KC)]).then_inc(wo_done, 1)

            def half(it, k, has_prev, has_next):
                v = n * it + k
                pi, pp = prev_of(it, k)
                ni, np_ = next_of(it, k)
                project_qk(0, k, v)
                project_qk(1, k, v)
                if has_prev:
                    transpose_attention(0, (0, 1), v - 1, True)
                project_qk(2, k, v)
                if has_prev:
                    transpose_attention(0, (2,), v - 1, True)
                project_v(0, v, has_prev)
                if has_prev:
                    attend(0, pp, k, v - 1, True)
                scores(0, v)
                if has_prev:
                    project_out(0, k, v - 1, True)
                    transpose_attention(1, (0, 1), v - 1, True)
                if has_next:
                    open_visit(ni, 0, np_, v + 1, k)
                if has_prev:
                    transpose_attention(1, (2,), v - 1, True)
                project_v(1, v, has_prev)
                if has_prev:
                    attend(1, pp, k, v - 1, True)
                if has_next:
                    open_visit(ni, 1, np_, v + 1, k)
                scores(1, v)
                if has_prev:
                    project_out(1, k, v - 1, True)

            def last():
                v = n * NIT - 1
                transpose_attention(0, (0, 1, 2), v, False)
                attend(0, 1, 0, v, False)
                project_out(0, 0, v, False)
                transpose_attention(1, (0, 1, 2), v, False)
                attend(1, 1, 0, v, False)
                project_out(1, 0, v, False)

            pe.wait_ge(consts, 3)
            for b in range(GB):
                open_visit(0, b, 0, 0, -1)
            pe.wait_ge(w_ready, 4)
            halves(pe, 1, half, last)


def build(nc, a):
    x1, x2, x3 = (nc.dram_tensor(f"x_{i}", (B, S, H), F32).ap() for i in (1, 2, 3))
    gat_phase(nc, a["x"], a["adj"], a["L0_gnn_W_left"], a["L0_gnn_W_right"], a["L0_gnn_W_lin"], a["L0_gnn_b_lin"],
              a["L0_gnn_ln_a"], a["L0_gnn_ln_b"], a["L0_gnn_ln_a_cols"], a["L0_gnn_ln_b_cols"], x1)
    digcn_phase(nc, x1, a["adj"], a["L1_gnn_Wl"], a["L1_gnn_bl"], a["L1_gnn_Ws"], a["L1_gnn_bs"], a["L1_gnn_Wr"],
                a["L1_gnn_br"], a["L1_gnn_ln_w"], a["L1_gnn_ln_b"], a["L1_gnn_ln_w_cols"], a["L1_gnn_ln_b_cols"], x2)
    mha_phase(nc, x2, a["adj"], a["L2_gnn_Wq"], a["L2_gnn_Wk"], a["L2_gnn_Wv"], a["L2_gnn_Wo"], a["L2_gnn_bv"],
              a["L2_gnn_bo"], x3)
    digcn_phase(nc, x3, a["adj"], a["L3_gnn_W_left"], a["L3_gnn_b_left"], a["L3_gnn_W_self"], a["L3_gnn_b_self"],
                a["L3_gnn_W_right"], a["L3_gnn_b_right"], a["L3_gnn_gamma"], a["L3_gnn_beta"],
                a["L3_gnn_gamma_cols"], a["L3_gnn_beta_cols"], a["out"])


_TURNED = ["L0_gnn_W_lin", "L1_gnn_Wl", "L1_gnn_Ws", "L1_gnn_Wr", "L2_gnn_Wq", "L2_gnn_Wk", "L2_gnn_Wv", "L2_gnn_Wo",
           "L3_gnn_W_left", "L3_gnn_W_self", "L3_gnn_W_right"]
_COLUMNS = ["L0_gnn_ln_a", "L0_gnn_ln_b", "L1_gnn_ln_w", "L1_gnn_ln_b", "L3_gnn_gamma", "L3_gnn_beta"]


def kernel(**inputs):
    import numpy as _np
    import concourse.bacc as _bacc
    from concourse import mybir as _mybir
    from concourse.bass_utils import run_bass_kernel_spmd as _run

    nc = _bacc.Bacc("TRN2", target_bir_lowering=False, num_devices=1)
    host = {}
    for name, value in inputs.items():
        value = _np.asarray(value)
        if name in _TURNED:
            value = value.swapaxes(-1, -2)
        if name.startswith("L3_"):
            value = value[None]
        host[name] = value
        if name in _COLUMNS:
            host[name + "_cols"] = value.reshape(-1, KC, P).swapaxes(1, 2)
    arrays, aps = {}, {}
    for name, value in host.items():
        value = _np.ascontiguousarray(value)
        arrays[f"in_{name}"] = value
        aps[name] = nc.dram_tensor(f"in_{name}", value.shape, _mybir.dt.from_np(value.dtype), kind="ExternalInput").ap()
    aps["out"] = nc.dram_tensor("out_x", (B, S, H), F32, kind="ExternalOutput").ap()
    build(nc, aps)
    return _run(nc, [arrays], core_ids=[0]).results[0]["out_x"]
```

```python
from contextlib import ExitStack

import concourse.bass as bass
from concourse import mybir

F32 = mybir.dt.float32
F32R = mybir.dt.float32r
ALU = mybir.AluOpType
ACT = mybir.ActivationFunctionType
AX_X = mybir.AxisListType.X

B, S, H = 64, 128, 384
P = 128
KC = H // P
GB = 2
NIT = B // (2 * GB)
HE = H + 2
BN = 6


class Memory:

    def __init__(self, nc, ctx, prefix):
        self.nc, self.ctx, self.prefix, self.sems = nc, ctx, prefix, []
        ctx.callback(self.clear)

    def clear(self):
        self.nc.clear_and_free_semaphores(self.sems)
        self.nc.all_engine_barrier()

    def sb(self, name, shape, dt=F32):
        return self.ctx.enter_context(self.nc.sbuf_tensor(self.prefix + name, [P] + shape, dt))

    def ps(self, name, shape):
        return self.ctx.enter_context(self.nc.psum_tensor(self.prefix + name, [P] + shape, F32))

    def sem(self, name):
        self.sems.append(self.nc.alloc_semaphore(self.prefix + name))
        return self.sems[-1]


class Shared:

    SLOTS = 6

    def __init__(self, nc, ctx):
        sb = lambda name, shape: ctx.enter_context(nc.sbuf_tensor(name, [P] + shape, F32))
        self.ident = sb("ident", [P])
        self.ones_f = sb("ones_f", [P])
        self.half_c = sb("half_c", [GB])
        self.mhalf_c = sb("mhalf_c", [GB])
        self.raw = sb("raw", [self.SLOTS, KC, H])
        self.loaded = [nc.alloc_semaphore(f"raw_loaded{w}") for w in range(self.SLOTS)]
        self.loads = [0] * self.SLOTS
        self.xin = [sb(f"xin{p}", [GB, H]) for p in range(2)]
        self.adjin = [sb(f"adjin{p}", [GB, S]) for p in range(2)]
        self.o = [sb(f"o{p}", [GB, H]) for p in range(2)]
        self.x_loaded = [nc.alloc_semaphore(f"x_loaded{p}") for p in range(2)]
        self.adj_loaded = [nc.alloc_semaphore(f"adj_loaded{p}") for p in range(2)]
        self.stored = [nc.alloc_semaphore(f"stored{p}") for p in range(2)]
        self.phase = 0

    def enter(self):
        self.phase += 1
        return 16 * NIT * (self.phase - 1)

    def load(self, sp, weights, start=0):
        for w, a in enumerate(weights, start):
            self.loads[w] += 1
            sp.dma_start(self.raw[:, w], rows(a)).then_inc(self.loaded[w], 16)


def set_up(nc, ctx):
    shared = Shared(nc, ctx)
    consts = nc.alloc_semaphore("consts")
    with nc.Block() as block:

        @block.vector
        def _(dve):
            for p in range(2):
                dve.engine_nop().then_inc(shared.stored[p], 16)

        @block.gpsimd
        def _(pool):
            pool.memset(shared.ident[:], 0.0).then_inc(consts, 1)
            pool.memset(shared.ones_f[:], 1.0).then_inc(consts, 1)
            pool.memset(shared.half_c[:], 0.5).then_inc(consts, 1)
            pool.memset(shared.mhalf_c[:], -0.5).then_inc(consts, 1)
            pool.wait_ge(consts, 1)
            pool.affine_select(out=shared.ident[:], in_=shared.ident[:], compare_op=ALU.not_equal, fill=1.0, base=0,
                               pattern=[[-1, P]], channel_multiplier=1).then_inc(consts, 1)
            pool.wait_ge(consts, 5)

    return shared


def first(it):
    return isinstance(it, int) and it == 0


def halves(eng, layers, half, last):
    n = 2 * layers
    for k in range(n):
        half(0, k, k > 0, True)
    with eng.Fori(1, NIT - 1) as it:
        for k in range(n):
            half(it, k, True, True)
    for k in range(n):
        half(NIT - 1, k, True, k < n - 1)
    last()


def rows(w):
    return w.rearrange("(c p) n -> p c n", p=P)


def split_product(pe, out, his, los, rhis, rlos, first=True, close=True, late=None):
    products, with_rlos = [], []
    for hi, lo, rhi, rlo in zip(his, los, rhis, rlos):
        products += [(hi, rhi), (lo, rhi)]
        with_rlos.append((hi, rlo))
    early = len(products)
    products += with_rlos
    for i, (a, b) in enumerate(products):
        if late and i == early:
            pe.wait_ge(*late)
        last = pe.matmul(out, a, b, start=(first and i == 0), stop=(close and i == len(products) - 1))
    return last


def after(eng, sem, count):
    if not isinstance(count, int) or count > 0:
        eng.wait_ge(sem, count)


def gat_phase(nc, x_in, adj, b_lin, ln_a, ln_b, ln_a_cols, ln_b_cols, shared, weights, next_weights, next_adj, x_out, adj_t_out):
    L = 2
    n = 2 * L
    TEMPER = float(H) ** 0.5
    with ExitStack() as ctx:
        m = Memory(nc, ctx, "g0_")
        raw, ident, half_c, mhalf_c = shared.raw, shared.ident, shared.half_c, shared.mhalf_c
        w_count = [count + 1 for count in shared.loads]
        w_hi = m.sb("w_hi", [3 * L, KC, H], F32R)
        w_lo = m.sb("w_lo", [3 * L, KC, H], F32R)
        b_raw = m.sb("b_raw", [L, H])
        b_rnd = m.sb("b_rnd", [L, H], F32R)
        b_parts = m.sb("b_parts", [L, H], F32R)
        ones = m.sb("ones", [P], F32R)
        a_cols = m.sb("a_cols", [KC])
        b_cols = m.sb("b_cols", [KC])
        a_row = m.sb("a_row", [H])
        b_row = m.sb("b_row", [H])
        xin, adjin, o = shared.xin, shared.adjin, shared.o
        x_loaded, adj_loaded, stored = shared.x_loaded, shared.adj_loaded, shared.stored
        base = shared.enter()
        xres = [m.sb(f"xres{p}", [GB, H]) for p in range(2)]
        adj_t = [m.sb(f"adj_t{p}", [GB, S]) for p in range(2)]
        masks = [m.sb(f"masks{p}", [GB, 2, S]) for p in range(2)]
        h_f = m.sb("h_f", [KC, GB, S])
        h_hi = [m.sb(f"h_hi{p}", [KC, GB, S], F32R) for p in range(2)]
        h_lo = [m.sb(f"h_lo{p}", [KC, GB, S], F32R) for p in range(2)]
        g_hi = m.sb("g_hi", [KC, 2, GB, S], F32R)
        g_lo = m.sb("g_lo", [KC, 2, GB, S], F32R)
        v_hi = m.sb("v_hi", [GB, HE], F32R)
        v_lo = m.sb("v_lo", [GB, HE], F32R)
        um = m.sb("um", [GB, 2, S])
        ua = m.sb("ua", [GB, S])
        e_s = m.sb("e_s", [GB, S])
        ea = m.sb("ea", [GB, S])
        e_hi = m.sb("e_hi", [GB, S], F32R)
        e_lo = m.sb("e_lo", [GB, S], F32R)
        den = m.sb("den", [GB])
        rden = m.sb("rden", [GB])
        cn = m.sb("cn", [GB, H])
        tn = m.sb("tn", [GB, H])
        t2 = m.sb("t2", [GB, H])
        t3 = m.sb("t3", [GB, H])
        t4 = m.sb("t4", [GB, H])
        y = [m.sb(f"y{p}", [GB, H]) for p in range(2)]
        stats = m.sb("stats", [GB, BN])
        mv = m.sb("mv", [GB, 2])
        vs = m.sb("vs", [GB])
        sd = m.sb("sd", [GB])
        se = m.sb("se", [GB])
        rr = m.sb("rr", [GB])
        ystats = m.sb("ystats", [GB, BN])
        ymv = [m.sb(f"ymv{p}", [GB, 2]) for p in range(2)]
        yv = m.sb("yv", [GB])
        yr = [m.sb(f"yr{p}", [GB]) for p in range(2)]

        tp = m.ps("tp", [GB, 512])
        pj = m.ps("pj", [3, 512])
        us = m.ps("us", [GB, 2, S])
        cx = m.ps("cx", [GB, 512])

        c_loaded = m.sem("c_loaded")
        w_hi_done = m.sem("w_hi_done")
        w_ready = m.sem("w_ready")
        dconst = m.sem("dconst")
        pool_gate = m.sem("pool_gate")
        dve_gate = m.sem("dve_gate")
        xin_free = [m.sem(f"xin_free{p}") for p in range(2)]
        tp_ready = m.sem("tp_ready")
        f_ready = m.sem("f_ready")
        hh_ready = m.sem("hh_ready")
        h_ready = m.sem("h_ready")
        pj_ready = m.sem("pj_ready")
        hi_ready = m.sem("hi_ready")
        pj_taken = m.sem("pj_taken")
        us_ready = m.sem("us_ready")
        um_ready = m.sem("um_ready")
        ua_ready = m.sem("ua_ready")
        e_ready = m.sem("e_ready")
        ea_ready = m.sem("ea_ready")
        eh_ready = m.sem("eh_ready")
        a_ready = m.sem("a_ready")
        cx_ready = m.sem("cx_ready")
        den_ready = m.sem("den_ready")
        rden_ready = m.sem("rden_ready")
        cn_ready = m.sem("cn_ready")
        st_ready = m.sem("st_ready")
        mv_ready = m.sem("mv_ready")
        vs_ready = m.sem("vs_ready")
        sd_ready = m.sem("sd_ready")
        se_ready = m.sem("se_ready")
        rr_ready = m.sem("rr_ready")
        tn_ready = m.sem("tn_ready")
        mask_ready = m.sem("mask_ready")
        adjt_ready = m.sem("adjt_ready")
        t2_ready = m.sem("t2_ready")
        t3_ready = m.sem("t3_ready")
        t4_ready = m.sem("t4_ready")
        y_ready = m.sem("y_ready")
        yst_ready = m.sem("yst_ready")
        ymv_ready = m.sem("ymv_ready")
        yv_ready = m.sem("yv_ready")
        yr_ready = m.sem("yr_ready")
        o_ready = m.sem("o_ready")
        adjt_stored = [m.sem(f"adjt_stored{p}") for p in range(2)]

        NW = 3 * L
        JOBS = 5
        RING = 3

        block = ctx.enter_context(nc.Block())

        def prev_of(it, k):
            return (it, (k - 1) // 2, (k - 1) % 2) if k else (it - 1, L - 1, 1)

        def next_of(it, k):
            return (it, (k + 1) // 2, (k + 1) % 2) if k < n - 1 else (it + 1, 0, 0)

        @block.sync
        def _(sp):
            def constants():
                sp.wait_ge(dconst, 1)
                sp.dma_start(b_raw[0:1], b_lin.unsqueeze(0)).then_inc(c_loaded, 16)
                sp.dma_start(b_raw[32:33], b_lin.unsqueeze(0)).then_inc(c_loaded, 16)
                sp.dma_start(a_cols[:], ln_a_cols[0]).then_inc(c_loaded, 16)
                sp.dma_start(b_cols[:], ln_b_cols[0]).then_inc(c_loaded, 16)
                sp.dma_start(a_row[:], ln_a[L - 1].partition_broadcast(P)).then_inc(c_loaded, 16)
                sp.dma_start(b_row[:], ln_b[L - 1].partition_broadcast(P)).then_inc(c_loaded, 16)

            def load(it, p, x=x_in, a=adj, at=None):
                after(sp, xin_free[p], it)
                after(sp, mask_ready, 2 * it + p - 1)
                at = (2 * it + p) * GB if at is None else at
                sp.dma_start(xin[p][:], x[bass.ds(at, GB)].rearrange("b s h -> s b h")).then_inc(x_loaded[p], 16)
                sp.dma_start(adjin[p][:], a[bass.ds(at, GB)].rearrange("b s t -> s b t")).then_inc(adj_loaded[p], 16)

            def store(it, p):
                sp.wait_ge(o_ready, 2 * it + p + 1)
                at = (2 * it + p) * GB
                sp.dma_start(x_out[bass.ds(at, GB)].rearrange("b s h -> s b h"), o[p][:]).then_inc(stored[p], 16)

            def store_adj_t(it, p):
                sp.wait_ge(adjt_ready, 2 * it + p + 1)
                at = (2 * it + p) * GB
                sp.dma_start(adj_t_out[bass.ds(at, GB)].rearrange("b s t -> s b t"), adj_t[p][:]).then_inc(adjt_stored[p], 16)

            shared.load(sp, weights[:2])
            load(0, 0)
            shared.load(sp, weights[2:3], 2)
            load(0, 1)
            constants()
            shared.load(sp, weights[3:], 3)
            for p in range(2):
                store_adj_t(0, p)
            for p in range(2):
                load(1, p)
            sp.wait_ge(w_ready, NW)
            shared.load(sp, next_weights)
            with sp.Fori(1, NIT - 1) as it:
                for p in range(2):
                    store_adj_t(it, p)
                    store(it - 1, p)
                    load(it + 1, p)
            for p in range(2):
                store_adj_t(NIT - 1, p)
            for p in range(2):
                store(NIT - 2, p)
                sp.wait_ge(stored[p], base + 32)
                load(NIT, p, x_out, next_adj, GB * p)
            for p in range(2):
                store(NIT - 1, p)
            for p in range(2):
                sp.wait_ge(adjt_stored[p], 16 * NIT + 16)

        @block.gpsimd
        def _(pool):
            pool.wait_ge(c_loaded, 16 * 6)

            def open_visit(it, l, p, v):
                if l == 0:
                    pool.wait_ge(adjt_ready, 2 * it + p + 1)
                    pool.sem_inc(pool_gate, 1)
                    pool.affine_select(out=masks[p][:, :, 0, :], in_=adj_t[p][:], compare_op=ALU.is_ge, fill=0.0,
                                       base=0, pattern=[[0, GB], [-1, S]], channel_multiplier=1)
                    pool.affine_select(out=masks[p][:, :, 1, :], in_=adjin[p][:], compare_op=ALU.is_gt, fill=0.0,
                                       base=0, pattern=[[0, GB], [1, S]], channel_multiplier=-1).then_inc(mask_ready, 1)

            def deviation(v):
                pool.wait_ge(vs_ready, v + 1)
                pool.tensor_tensor(sd[:], vs[:], half_c[:], ALU.pow).then_inc(sd_ready, 1)

            def affine(it, p, v):
                g = 2 * it + p
                pool.wait_ge(tn_ready, v + 1)
                pool.tensor_tensor(t2[:], tn[:], a_row[:].unsqueeze(1).broadcast_to([P, GB, H]), ALU.mult).then_inc(t2_ready, 1)
                pool.wait_ge(t2_ready, g + 1)
                pool.tensor_tensor(t3[:], t2[:], b_row[:].unsqueeze(1).broadcast_to([P, GB, H]), ALU.add).then_inc(t3_ready, 1)

            def residual(it, p):
                pool.wait_ge(xin_free[p], it + 1)
                pool.wait_ge(t4_ready, 2 * it + p + 1)
                pool.tensor_tensor(y[p][:], t4[:], xres[p][:], ALU.add).then_inc(y_ready, 1)

            def out_norm(it, p):
                pool.wait_ge(yv_ready, 2 * it + p + 1)
                pool.tensor_tensor(yr[p][:], yv[:], mhalf_c[:], ALU.pow).then_inc(yr_ready, 1)

            def half(it, k, has_prev, has_next):
                v = n * it + k
                pi, pl, pp = prev_of(it, k)
                ni, nl, np_ = next_of(it, k)
                done = k < 2 and not first(it)
                if done:
                    residual(it - 1, k)
                if has_prev:
                    deviation(v - 1)
                if has_prev and pl == L - 1:
                    affine(pi, pp, v - 1)
                if has_next:
                    open_visit(ni, nl, np_, v + 1)
                if done:
                    out_norm(it - 1, k)

            open_visit(0, 0, 0, 0)

            def last():
                residual(NIT - 1, 0)
                deviation(n * NIT - 1)
                out_norm(NIT - 1, 0)
                out_norm(NIT - 1, 1)

            halves(pool, L, half, last)

        @block.scalar
        def _(act):
            def split_weights(l):
                for w in range(3 * l, 3 * l + 3):
                    act.wait_ge(shared.loaded[w], 16 * w_count[w])
                    act.activation(w_hi[:, w], raw[:, w], ACT.Copy).then_inc(w_hi_done, 1)

            def open_visit(it, l, p, v):
                act.wait_ge(tp_ready, v + 1)
                if l == 0:
                    act.wait_ge(adjt_stored[p], 16 * it + 16)
                    act.activation(adj_t[p][:], tp[:, :, H:512], ACT.Copy).then_inc(adjt_ready, 1)
                    for b in range(GB):
                        i = act.activation(h_f[:, :, b, :], tp[:, b, 0:H].rearrange("p (c s) -> p c s", c=KC), ACT.Copy)
                else:
                    for c in range(KC):
                        i = act.activation(h_f[:, c], tp[:, :, c * P:(c + 1) * P], ACT.Relu,
                                           bias=b_cols[:, c:c + 1], scale=a_cols[:, c:c + 1])
                i.then_inc(f_ready, 1)

            def take_hi(j, v):
                act.wait_ge(pj_ready, JOBS * v + j + 1)
                if j < KC:
                    i = act.activation(g_hi[:, j], pj[:, j % RING, :].rearrange("p (w b s) -> p w b s", w=2, b=GB), ACT.Copy)
                else:
                    i = act.activation(v_hi[:, j - KC, 0:H], pj[:, j % RING, 0:H], ACT.Copy)
                i.then_inc(hi_ready, 1)

            def close_visit(v):
                act.wait_ge(rden_ready, v + 1)
                for b in range(GB):
                    act.activation(cn[:, b], cx[:, b, 0:H], ACT.Copy, scale=rden[:, b:b + 1]).then_inc(cn_ready, 1)

            def keep_x(it, p, v):
                act.wait_ge(x_loaded[p], base + 16 * it + 16)
                act.wait_ge(tp_ready, v + 1)
                after(act, y_ready, 2 * it + p - 1)
                act.activation(xres[p][:], xin[p][:], ACT.Copy).then_inc(xin_free[p], 1)

            def relu(it, p):
                g = 2 * it + p
                act.wait_ge(t3_ready, g + 1)
                after(act, y_ready, g)
                act.activation(t4[:], t3[:], ACT.Relu).then_inc(t4_ready, 1)

            def half(it, k, has_prev, has_next):
                v = n * it + k
                pi, pl, pp = prev_of(it, k)
                ni, nl, np_ = next_of(it, k)
                take_hi(0, v)
                if has_prev:
                    close_visit(v - 1)
                take_hi(1, v)
                take_hi(2, v)
                if k < 2:
                    keep_x(it, k, v)
                take_hi(3, v)
                if has_next:
                    open_visit(ni, nl, np_, v + 1)
                act.wait_ge(ua_ready, v + 1)
                act.activation(e_s[:], ua[:], ACT.Exp, scale=1.0 / TEMPER).then_inc(e_ready, 1)
                take_hi(KC + 1, v)
                if has_prev and pl == L - 1:
                    relu(pi, pp)
                if first(it) and k % 2 == 0 and k // 2 < L - 1:
                    split_weights(k // 2 + 1)

            split_weights(0)
            open_visit(0, 0, 0, 0)
            act.wait_ge(c_loaded, 16 * 6)
            halves(act, L, half, lambda: close_visit(n * NIT - 1))

        @block.vector
        def _(dve):
            for p in range(2):
                dve.engine_nop().then_inc(adjt_stored[p], 16)
            dve.memset(b_raw[:], 0.0).then_inc(dconst, 1)
            dve.tensor_copy(ones[:], shared.ones_f[:]).then_inc(dconst, 1)
            dve.memset(v_hi[:, :, H:HE].bitcast(F32), 1.0).then_inc(dconst, 1)
            dve.memset(v_lo[:, :, H:HE].bitcast(F32), 0.0).then_inc(dconst, 1)
            dve.memset(b_parts[:].bitcast(F32), 0.0).then_inc(dconst, 1)
            def split_weights(slots):
                for w in slots:
                    dve.wait_ge(w_hi_done, w + 1)
                    dve.tensor_tensor(w_lo[:, w], raw[:, w], w_hi[:, w].bitcast(F32), ALU.subtract).then_inc(w_ready, 1)

            def open_hi(p, v):
                dve.wait_ge(f_ready, v + 1)
                dve.tensor_copy(h_hi[p][:], h_f[:]).then_inc(hh_ready, 1)

            def open_lo(p, v):
                dve.wait_ge(hh_ready, v + 1)
                dve.tensor_tensor(h_lo[p][:], h_f[:], h_hi[p][:].bitcast(F32), ALU.subtract).then_inc(h_ready, 1)

            def take_lo(j, v):
                dve.wait_ge(hi_ready, JOBS * v + j + 1)
                if j < KC:
                    i = dve.tensor_tensor(g_lo[:, j].rearrange("p w b s -> p (w b s)"), pj[:, j % RING, :],
                                          g_hi[:, j].bitcast(F32).rearrange("p w b s -> p (w b s)"), ALU.subtract)
                else:
                    i = dve.tensor_tensor(v_lo[:, j - KC, 0:H], pj[:, j % RING, 0:H],
                                          v_hi[:, j - KC, 0:H].bitcast(F32), ALU.subtract)
                i.then_inc(pj_taken, 1)

            def close_sums(v):
                dve.wait_ge(cx_ready, v + 1)
                dve.tensor_scalar(den[:].unsqueeze(2), cx[:, :, H:H + 1], 1e-10, None, ALU.add).then_inc(den_ready, 1)
                dve.wait_ge(den_ready, v + 1)
                dve.reciprocal(rden[:], den[:]).then_inc(rden_ready, 1)

            def close_stats(v):
                for b in range(GB):
                    dve.wait_ge(cn_ready, GB * v + b + 1)
                    dve.bn_stats(stats[:, b], cn[:, b]).then_inc(st_ready, 1)
                dve.wait_ge(st_ready, GB * (v + 1))
                dve.sem_inc(dve_gate, 1)
                for b in range(GB):
                    dve.bn_aggr(mv[:, b], stats[:, b]).then_inc(mv_ready, 1)
                dve.wait_ge(mv_ready, GB * (v + 1))
                dve.tensor_scalar(vs[:].unsqueeze(2), mv[:, :, 1:2], H / (H - 1.0), 1e-30, ALU.mult, ALU.add).then_inc(vs_ready, 1)

            def close_norm(v):
                dve.wait_ge(sd_ready, v + 1)
                dve.tensor_scalar(se[:], sd[:], 1e-3, None, ALU.add).then_inc(se_ready, 1)
                dve.wait_ge(se_ready, v + 1)
                dve.reciprocal(rr[:], se[:]).then_inc(rr_ready, 1)
                dve.wait_ge(rr_ready, v + 1)
                for b in range(GB):
                    i = dve.tensor_scalar(tn[:, b], cn[:, b], mv[:, b, 0:1], rr[:, b:b + 1], ALU.subtract, ALU.mult)
                i.then_inc(tn_ready, 1)

            def out_stats(it, p):
                g = 2 * it + p
                dve.wait_ge(y_ready, g + 1)
                for b in range(GB):
                    dve.bn_stats(ystats[:, b], y[p][:, b]).then_inc(yst_ready, 1)

            def out_variance(it, p):
                g = 2 * it + p
                dve.wait_ge(yst_ready, GB * (g + 1))
                dve.sem_inc(dve_gate, 1)
                for b in range(GB):
                    dve.bn_aggr(ymv[p][:, b], ystats[:, b]).then_inc(ymv_ready, 1)
                dve.wait_ge(ymv_ready, GB * (g + 1))
                dve.tensor_scalar(yv[:].unsqueeze(2), ymv[p][:, :, 1:2], 1e-5, None, ALU.add).then_inc(yv_ready, 1)

            def output(it, p):
                g = 2 * it + p
                dve.wait_ge(yr_ready, g + 1)
                dve.wait_ge(stored[p], base + 16 * it + 16)
                for b in range(GB):
                    i = dve.tensor_scalar(o[p][:, b], y[p][:, b], ymv[p][:, b, 0:1], yr[p][:, b:b + 1],
                                          ALU.subtract, ALU.mult)
                i.then_inc(o_ready, 1)

            def half(it, k, has_prev, has_next):
                v = n * it + k
                pi, pl, pp = prev_of(it, k)
                ni, nl, np_ = next_of(it, k)
                done = k < 2 and not first(it)
                take_lo(0, v)
                if has_prev:
                    close_sums(v - 1)
                    close_stats(v - 1)
                take_lo(1, v)
                if has_prev:
                    close_norm(v - 1)
                take_lo(2, v)
                if done:
                    out_stats(it - 1, k)
                take_lo(3, v)
                if 0 < k < 3 and not first(it):
                    output(it - 1, k - 1)
                if done:
                    out_variance(it - 1, k)
                if has_next:
                    open_hi(np_, v + 1)
                dve.wait_ge(us_ready, v + 1)
                dve.wait_ge(mask_ready, 2 * it + k % 2 + 1)
                dve.tensor_tensor(um[:], us[:], masks[k % 2][:], ALU.mult).then_inc(um_ready, 1)
                dve.wait_ge(um_ready, v + 1)
                dve.tensor_tensor(ua[:], um[:, :, 0, :], um[:, :, 1, :], ALU.add).then_inc(ua_ready, 1)
                if has_next:
                    open_lo(np_, v + 1)
                dve.wait_ge(e_ready, v + 1)
                dve.tensor_tensor(ea[:], e_s[:], adj_t[k % 2][:], ALU.mult).then_inc(ea_ready, 1)
                dve.wait_ge(ea_ready, v + 1)
                dve.tensor_copy(e_hi[:], ea[:]).then_inc(eh_ready, 1)
                dve.wait_ge(eh_ready, v + 1)
                dve.tensor_tensor(e_lo[:], ea[:], e_hi[:].bitcast(F32), ALU.subtract).then_inc(a_ready, 1)
                take_lo(4, v)
                if first(it) and k % 2 == 0 and k // 2 < L - 1:
                    split_weights(range(3 * (k // 2 + 1), 3 * (k // 2 + 2)))

            def last():
                close_sums(n * NIT - 1)
                close_stats(n * NIT - 1)
                close_norm(n * NIT - 1)
                g = 2 * NIT - 1
                dve.wait_ge(tn_ready, n * NIT)
                dve.tensor_tensor(t2[:], tn[:], a_row[:].unsqueeze(1).broadcast_to([P, GB, H]), ALU.mult).then_inc(t2_ready, 1)
                dve.wait_ge(t2_ready, g + 1)
                dve.wait_ge(t4_ready, g)
                dve.tensor_tensor(t3[:], t2[:], b_row[:].unsqueeze(1).broadcast_to([P, GB, H]), ALU.add).then_inc(t3_ready, 1)
                dve.wait_ge(t3_ready, g + 1)
                dve.wait_ge(xin_free[1], NIT)
                dve.wait_ge(y_ready, g)
                dve.scalar_tensor_tensor(y[1][:], t3[:], 0.0, xres[1][:], ALU.max, ALU.add).then_inc(y_ready, 1)
                out_stats(NIT - 1, 0)
                out_variance(NIT - 1, 0)
                output(NIT - 1, 0)
                out_stats(NIT - 1, 1)
                out_variance(NIT - 1, 1)
                output(NIT - 1, 1)

            split_weights((0, 1))
            open_hi(0, 0)
            open_lo(0, 0)
            split_weights((2,))
            dve.wait_ge(c_loaded, 16 * 6)
            dve.tensor_copy(b_rnd[:], b_raw[:]).then_inc(dconst, 1)
            dve.wait_ge(dconst, 6)
            dve.tensor_copy(b_parts[0:1], b_raw[0:1]).then_inc(dconst, 1)
            dve.tensor_tensor(b_parts[32:33], b_raw[32:33], b_rnd[32:33].bitcast(F32), ALU.subtract).then_inc(dconst, 1)
            halves(dve, L, half, last)

        @block.tensor
        def _(pe):
            def open_visit(it, l, p, v):
                after(pe, f_ready, v)
                if l == 0:
                    pe.wait_ge(x_loaded[p], base + 16 * it + 16)
                    pe.wait_ge(adj_loaded[p], base + 16 * it + 16)
                    src = xin[p]
                else:
                    pe.wait_ge(tn_ready, v - 1)
                    src = tn
                for b in range(GB):
                    for c in range(KC):
                        i = pe.transpose(tp[:, b, c * P:(c + 1) * P], src[:, b, c * P:(c + 1) * P], ident[:])
                    if l == 0:
                        i = pe.transpose(tp[:, b, H:512], adjin[p][:, b], ident[:])
                i.then_inc(tp_ready, 1)

            def project(j, it, l, p, v):
                if j == 0:
                    pe.wait_ge(hh_ready, v + 1)
                if first(it):
                    pe.wait_ge(w_ready, 3 * l + (2 if j < KC else 3))
                if first(v) and j == KC:
                    pe.wait_ge(dconst, 8)
                before = JOBS * v + j - 2 if j >= RING else JOBS * (v - 1) + (j + 4 if j < 2 else 3)
                after(pe, pj_taken, before)
                bank = pj[:, j % RING, :]
                if j < KC:
                    for s in range(2):
                        out = bank[:, s * GB * S:(s + 1) * GB * S]
                        w = 3 * l + s
                        i = split_product(
                            pe, out, [w_hi[:, w, c, j * P:(j + 1) * P] for c in range(KC)],
                            [w_lo[:, w, c, j * P:(j + 1) * P] for c in range(KC)],
                            [h_hi[p][:, c].rearrange("p b s -> p (b s)") for c in range(KC)],
                            [h_lo[p][:, c].rearrange("p b s -> p (b s)") for c in range(KC)],
                            late=(h_ready, v + 1) if j == 0 and s == 0 else None)
                else:
                    b, w = j - KC, 3 * l + 2
                    pe.matmul(bank[:, 0:H], ones[:], b_parts[:, l], start=True, stop=False)
                    i = split_product(
                        pe, bank[:, 0:H], [h_hi[p][:, c, b] for c in range(KC)], [h_lo[p][:, c, b] for c in range(KC)],
                        [w_hi[:, w, c] for c in range(KC)], [w_lo[:, w, c] for c in range(KC)], first=False)
                i.then_inc(pj_ready, 1)

            def scores(p, v):
                after(pe, um_ready, v)
                pe.wait_ge(pj_taken, JOBS * v + KC)
                for b in range(GB):
                    i = split_product(
                        pe, us[:, b], [h_hi[p][:, c, b] for c in range(KC)], [h_lo[p][:, c, b] for c in range(KC)],
                        [g_hi[:, c, :, b] for c in range(KC)], [g_lo[:, c, :, b] for c in range(KC)])
                i.then_inc(us_ready, 1)

            def close_visit(v):
                after(pe, cn_ready, GB * v)
                pe.wait_ge(a_ready, v + 1)
                for b in range(GB):
                    pe.wait_ge(pj_taken, JOBS * v + KC + b + 1)
                    i = split_product(pe, cx[:, b, 0:HE], [e_hi[:, b]], [e_lo[:, b]], [v_hi[:, b]], [v_lo[:, b]])
                i.then_inc(cx_ready, 1)

            def half(it, k, has_prev, has_next):
                v = n * it + k
                l, p = k // 2, k % 2
                ni, nl, np_ = next_of(it, k)
                project(0, it, l, p, v)
                if has_prev:
                    close_visit(v - 1)
                for j in range(1, KC + 1):
                    project(j, it, l, p, v)
                if has_next:
                    open_visit(ni, nl, np_, v + 1)
                scores(p, v)
                project(KC + 1, it, l, p, v)

            open_visit(0, 0, 0, 0)
            halves(pe, L, half, lambda: close_visit(n * NIT - 1))


def digcn_phase(nc, x_in, adj_t, b_up, b_self, b_low, ln_g, ln_b, ln_g_cols, ln_b_cols, shared, next_weights, next_adj, x_out):
    L = b_up.shape[0]
    n = 2 * L
    TEMPER = float(H) ** 0.5
    prefix = f"g{L}_"
    with ExitStack() as ctx:
        m = Memory(nc, ctx, prefix)
        raw, ident, mhalf_c = shared.raw, shared.ident, shared.mhalf_c
        w_count = list(shared.loads)
        w_hi = m.sb("w_hi", [3 * L, KC, H], F32R)
        w_lo = m.sb("w_lo", [3 * L, KC, H], F32R)
        v_bias = m.sb("v_bias", [3 * L, H])
        g_cols = m.sb("g_cols", [KC])
        b_cols = m.sb("b_cols", [KC])
        g_row = m.sb("g_row", [H])
        b_row = m.sb("b_row", [H])
        xin, adjin, o = shared.xin, shared.adjin, shared.o
        x_loaded, adj_loaded, stored = shared.x_loaded, shared.adj_loaded, shared.stored
        base = shared.enter()
        xres = [m.sb(f"xres{p}", [GB, H]) for p in range(2)]
        adj_d = [m.sb(f"adj_d{p}", [GB]) for p in range(2)]
        masks = [m.sb(f"masks{p}", [GB, 2, S]) for p in range(2)]
        h_f = m.sb("h_f", [KC, GB, S])
        h_hi = [m.sb(f"h_hi{p}", [KC, GB, S], F32R) for p in range(2)]
        h_lo = [m.sb(f"h_lo{p}", [KC, GB, S], F32R) for p in range(2)]
        v_f = m.sb("v_f", [GB, 2, H])
        v_hi = m.sb("v_hi", [GB, 2, HE], F32R)
        v_lo = m.sb("v_lo", [GB, 2, HE], F32R)
        vself = m.sb("vself", [GB, H])
        bself = m.sb("bself", [GB, H])
        own = m.sb("own", [GB, H])
        e_t = m.sb("e_t", [GB, S])
        mx = m.sb("mx", [GB])
        nb = m.sb("nb", [GB])
        e_s = m.sb("e_s", [GB, S])
        esum = [m.sb(f"esum{p}", [GB]) for p in range(2)]
        diag = m.sb("diag", [GB])
        junk = m.sb("junk", [GB, S])
        junk_adj = m.sb("junk_adj", [GB, S])
        dself = [m.sb(f"dself{p}", [GB]) for p in range(2)]
        au = m.sb("au", [GB, 2, S])
        a_hi = m.sb("a_hi", [GB, 2, S], F32R)
        a_lo = m.sb("a_lo", [GB, 2, S], F32R)
        part = m.sb("part", [GB])
        den = m.sb("den", [GB])
        dd = m.sb("dd", [GB])
        cn = m.sb("cn", [GB, H])
        tn = m.sb("tn", [GB, H])
        t2 = m.sb("t2", [GB, H])
        t3 = m.sb("t3", [GB, H])
        y = [m.sb(f"y{p}", [GB, H]) for p in range(2)]
        stats = m.sb("stats", [GB, BN])
        mv = m.sb("mv", [GB, 2])
        vs = m.sb("vs", [GB])
        rr = m.sb("rr", [GB])
        nm = m.sb("nm", [GB])
        ystats = m.sb("ystats", [GB, BN])
        ymv = m.sb("ymv", [GB, 2])
        yv = m.sb("yv", [GB])
        yr = [m.sb(f"yr{p}", [GB]) for p in range(2)]
        ynm = [m.sb(f"ynm{p}", [GB]) for p in range(2)]

        tp = m.ps("tp", [GB, 512])
        pj = m.ps("pj", [3, 512])
        us = m.ps("us", [2, GB, S])
        cx = m.ps("cx", [GB, 512])

        c_loaded = m.sem("c_loaded")
        w_hi_done = m.sem("w_hi_done")
        w_ready = m.sem("w_ready")
        dconst = m.sem("dconst")
        pool_gate = m.sem("pool_gate")
        dve_gate = m.sem("dve_gate")
        xin_free = [m.sem(f"xin_free{p}") for p in range(2)]
        tp_ready = m.sem("tp_ready")
        f_ready = m.sem("f_ready")
        hh_ready = m.sem("hh_ready")
        h_ready = m.sem("h_ready")
        pj_ready = m.sem("pj_ready")
        f32_taken = m.sem("f32_taken")
        hi_ready = m.sem("hi_ready")
        lo_ready = m.sem("lo_ready")
        self_taken = m.sem("self_taken")
        own_ready = m.sem("own_ready")
        us_ready = m.sem("us_ready")
        mx_ready = m.sem("mx_ready")
        nb_ready = m.sem("nb_ready")
        e_ready = m.sem("e_ready")
        diag_ready = m.sem("diag_ready")
        d_ready = m.sem("d_ready")
        au_ready = m.sem("au_ready")
        et_ready = m.sem("et_ready")
        et_taken = m.sem("et_taken")
        ah_ready = m.sem("ah_ready")
        a_ready = m.sem("a_ready")
        cx_ready = m.sem("cx_ready")
        part_ready = m.sem("part_ready")
        den_ready = m.sem("den_ready")
        cn_ready = m.sem("cn_ready")
        dd_ready = m.sem("dd_ready")
        st_ready = m.sem("st_ready")
        mv_ready = m.sem("mv_ready")
        vs_ready = m.sem("vs_ready")
        rr_ready = m.sem("rr_ready")
        nm_ready = m.sem("nm_ready")
        tn_ready = m.sem("tn_ready")
        mask_ready = m.sem("mask_ready")
        adjd_ready = m.sem("adjd_ready")
        t2_ready = m.sem("t2_ready")
        t3_ready = m.sem("t3_ready")
        y_ready = m.sem("y_ready")
        yst_ready = m.sem("yst_ready")
        ymv_ready = m.sem("ymv_ready")
        yv_ready = m.sem("yv_ready")
        yr_ready = m.sem("yr_ready")
        ynm_ready = m.sem("ynm_ready")
        o_ready = m.sem("o_ready")

        NW = 3 * L
        RING = 3
        LO_JOBS = 2 * GB
        JOBS = 3 * GB
        ML = L - 1

        block = ctx.enter_context(nc.Block())

        def prev_of(it, k):
            return (it, (k - 1) // 2, (k - 1) % 2) if k else (it - 1, L - 1, 1)

        def next_of(it, k):
            return (it, (k + 1) // 2, (k + 1) % 2) if k < n - 1 else (it + 1, 0, 0)

        @block.sync
        def _(sp):
            def load_x(it, p, x=x_in, at=None):
                after(sp, xin_free[p], it)
                at = (2 * it + p) * GB if at is None else at
                sp.dma_start(xin[p][:], x[bass.ds(at, GB)].rearrange("b s h -> s b h")).then_inc(x_loaded[p], 16)

            def load_adj(it, p, a=adj_t, at=None):
                after(sp, adjd_ready, GB * (2 * it + p - 1))
                at = (2 * it + p) * GB if at is None else at
                sp.dma_start(adjin[p][:], a[bass.ds(at, GB)].rearrange("b s t -> s b t")).then_inc(adj_loaded[p], 16)

            def store(it, p):
                sp.wait_ge(o_ready, 2 * it + p + 1)
                at = (2 * it + p) * GB
                sp.dma_start(x_out[bass.ds(at, GB)].rearrange("b s h -> s b h"), o[p][:]).then_inc(stored[p], 16)

            for i in range(L):
                for w, a in enumerate((b_up, b_low, b_self)):
                    sp.dma_start(v_bias[:, 3 * i + w], a[i].partition_broadcast(P)).then_inc(c_loaded, 16)
            sp.dma_start(g_cols[:], ln_g_cols[0]).then_inc(c_loaded, 16)
            sp.dma_start(b_cols[:], ln_b_cols[0]).then_inc(c_loaded, 16)
            sp.dma_start(g_row[:], ln_g[L - 1].partition_broadcast(P)).then_inc(c_loaded, 16)
            sp.dma_start(b_row[:], ln_b[L - 1].partition_broadcast(P)).then_inc(c_loaded, 16)
            for p in range(2):
                load_x(1, p)
                load_adj(1, p)
            sp.wait_ge(w_ready, NW)
            shared.load(sp, next_weights)
            with sp.Fori(1, NIT - 1) as it:
                for p in range(2):
                    load_adj(it + 1, p)
                    store(it - 1, p)
                    load_x(it + 1, p)
            for p in range(2):
                store(NIT - 2, p)
                if next_adj is not None:
                    sp.wait_ge(stored[p], base + 32)
                    load_x(NIT, p, x_out, GB * p)
                    load_adj(NIT, p, next_adj, GB * p)
            for p in range(2):
                store(NIT - 1, p)
            if next_adj is None:
                for p in range(2):
                    sp.wait_ge(stored[p], base + 16 * NIT + 16)

        CONSTS = 3 * L + 4

        @block.gpsimd
        def _(pool):
            def open_visit(it, l, p, v):
                if l == 0:
                    pool.wait_ge(adj_loaded[p], base + 16 * it + 16)
                    after(pool, au_ready, v - 1)
                    pool.sem_inc(pool_gate, 1)
                    pool.affine_select(out=masks[p][:, :, 0, :], in_=adjin[p][:], compare_op=ALU.is_gt, fill=0.0,
                                       base=0, pattern=[[0, GB], [-1, S]], channel_multiplier=1)
                    pool.affine_select(out=masks[p][:, :, 1, :], in_=adjin[p][:], compare_op=ALU.is_gt, fill=0.0,
                                       base=0, pattern=[[0, GB], [1, S]], channel_multiplier=-1).then_inc(mask_ready, 1)

            def deviation(v):
                pool.wait_ge(vs_ready, v + 1)
                pool.tensor_tensor(rr[:], vs[:], mhalf_c[:], ALU.pow).then_inc(rr_ready, 1)

            def attention(it, l, p, v):
                if l:
                    pool.wait_ge(et_taken, ML * 2 * it + 2 * (l - 1) + p + 1)
                else:
                    pool.wait_ge(e_ready, GB * (v + 1))
                pool.wait_ge(mask_ready, 2 * it + p + 1)
                after(pool, a_ready, v)
                for b in range(GB):
                    i = pool.tensor_tensor(au[:, b], (e_t if l else e_s)[:, b].unsqueeze(1).broadcast_to([P, 2, S]),
                                           masks[p][:, b], ALU.mult)
                i.then_inc(au_ready, 1)

            def scale_rows(it, p, v):
                g = 2 * it + p
                pool.wait_ge(tn_ready, v + 1)
                after(pool, t3_ready, g)
                pool.tensor_tensor(t2[:], tn[:], g_row[:].unsqueeze(1).broadcast_to([P, GB, H]), ALU.mult).then_inc(t2_ready, 1)

            def shift_rows(it, p):
                g = 2 * it + p
                after(pool, y_ready, g)
                pool.wait_ge(t2_ready, g + 1)
                pool.tensor_tensor(t3[:], t2[:], b_row[:].unsqueeze(1).broadcast_to([P, GB, H]), ALU.add).then_inc(t3_ready, 1)

            def add_own(v):
                for b in range(GB):
                    after(pool, cn_ready, GB * (v - 1) + b + 1)
                    pool.wait_ge(self_taken, GB * v + b + 1)
                    pool.tensor_tensor(own[:, b], vself[:, b], bself[:, b], ALU.add).then_inc(own_ready, 1)

            def out_norm(it, p):
                pool.wait_ge(yv_ready, 2 * it + p + 1)
                pool.tensor_tensor(yr[p][:], yv[:], mhalf_c[:], ALU.pow).then_inc(yr_ready, 1)

            def half(it, k, has_prev, has_next):
                v = n * it + k
                pi, pl, pp = prev_of(it, k)
                ni, nl, np_ = next_of(it, k)
                if has_prev:
                    deviation(v - 1)
                if has_next:
                    open_visit(ni, nl, np_, v + 1)
                attention(it, k // 2, k % 2, v)
                if has_prev and pl == L - 1:
                    scale_rows(pi, pp, v - 1)
                if k < 2 and not first(it):
                    out_norm(it - 1, k)
                if has_prev and pl == L - 1:
                    shift_rows(pi, pp)
                add_own(v)

            def last():
                deviation(n * NIT - 1)
                out_norm(NIT - 1, 0)
                out_norm(NIT - 1, 1)

            open_visit(0, 0, 0, 0)
            pool.wait_ge(c_loaded, 16 * CONSTS)
            halves(pool, L, half, last)

        @block.scalar
        def _(act):
            def split_weights(l):
                for w in range(3 * l, 3 * l + 3):
                    act.wait_ge(shared.loaded[w], 16 * w_count[w])
                    act.activation(w_hi[:, w], raw[:, w], ACT.Copy).then_inc(w_hi_done, 1)

            def open_visit(l, v):
                act.wait_ge(tp_ready, v + 1)
                if l == 0:
                    for b in range(GB):
                        i = act.activation(h_f[:, :, b, :], tp[:, b, 0:H].rearrange("p (c s) -> p c s", c=KC), ACT.Copy)
                else:
                    for c in range(KC):
                        i = act.activation(h_f[:, c], tp[:, :, c * P:(c + 1) * P], ACT.Relu,
                                           bias=b_cols[:, c:c + 1], scale=g_cols[:, c:c + 1])
                i.then_inc(f_ready, 1)

            def open_hi(p, v):
                act.wait_ge(f_ready, v + 1)
                act.activation(h_hi[p][:], h_f[:], ACT.Copy).then_inc(hh_ready, 1)

            def take_hi(j, v):
                act.wait_ge(f32_taken, LO_JOBS * v + j + 1)
                after(act, cx_ready, v)
                act.activation(v_hi[:, j // 2, j % 2, 0:H], v_f[:, j // 2, j % 2], ACT.Copy).then_inc(hi_ready, 1)

            def scale_bias(l, p, v):
                act.wait_ge(d_ready, v + 1)
                after(act, own_ready, GB * v)
                for b in range(GB):
                    act.activation(bself[:, b], v_bias[:, 3 * l + 2], ACT.Copy, scale=dself[p][:, b:b + 1])

            def take_self(b, p, v):
                act.wait_ge(pj_ready, JOBS * v + LO_JOBS + b + 1)
                act.activation(vself[:, b], pj[:, (LO_JOBS + b) % RING, 0:H], ACT.Copy,
                               scale=dself[p][:, b:b + 1]).then_inc(self_taken, 1)

            def exps(it, l, p, v):
                act.wait_ge(us_ready, v + 1)
                after(act, au_ready, v)
                after(act, d_ready, v)
                if l:
                    act.wait_ge(nb_ready, ML * 2 * it + 2 * (l - 1) + p + 1)
                for b in range(GB):
                    act.activation(e_s[:, b], us[:, 0, b], ACT.Exp, scale=1.0 / TEMPER,
                                   bias=nb[:, b:b + 1] if l else 0.0,
                                   accum_out=esum[p][:, b:b + 1]).then_inc(e_ready, 1)

            def take_transposed(it, l, p):
                c = ML * 2 * it + 2 * (l - 1) + p
                act.wait_ge(et_ready, c + 1)
                act.activation(e_t[:], us[:, 1], ACT.Copy).then_inc(et_taken, 1)

            def take_attention(v):
                act.wait_ge(au_ready, v + 1)
                act.activation(a_hi[:], au[:], ACT.Copy).then_inc(ah_ready, 1)

            def norm(it, l, p, v):
                act.wait_ge(nm_ready, v + 1)
                after(act, t2_ready, 2 * it + (p if l == L - 1 else 0))
                for b in range(GB):
                    i = act.activation(tn[:, b], cn[:, b], ACT.Identity, scale=rr[:, b:b + 1], bias=nm[:, b:b + 1])
                i.then_inc(tn_ready, 1)

            def keep_x(it, p, v):
                act.wait_ge(tp_ready, v + 1)
                after(act, y_ready, 2 * it + p - 1)
                act.activation(xres[p][:], xin[p][:], ACT.Copy).then_inc(xin_free[p], 1)

            def output(it, p):
                act.wait_ge(ynm_ready, 2 * it + p + 1)
                act.wait_ge(stored[p], base + 16 * it + 16)
                for b in range(GB):
                    i = act.activation(o[p][:, b], y[p][:, b], ACT.Identity, scale=yr[p][:, b:b + 1], bias=ynm[p][:, b:b + 1])
                i.then_inc(o_ready, 1)

            def half(it, k, has_prev, has_next):
                v = n * it + k
                pi, pl, pp = prev_of(it, k)
                ni, nl, np_ = next_of(it, k)
                exps(it, k // 2, k % 2, v)
                urgent = has_next and nl > 0
                if not urgent:
                    take_hi(0, v)
                if k // 2 and not urgent:
                    take_transposed(it, k // 2, k % 2)
                if has_prev:
                    norm(pi, pl, pp, v - 1)
                if urgent:
                    take_hi(0, v)
                take_hi(1, v)
                if k // 2 and urgent:
                    take_transposed(it, k // 2, k % 2)
                take_hi(2, v)
                if k != 2:
                    take_attention(v)
                if (k == 3):
                    take_hi(3, v)
                scale_bias(k // 2, k % 2, v)
                if not (k == 3):
                    take_hi(3, v)
                if k == 2:
                    take_attention(v)
                if has_next:
                    open_visit(nl, v + 1)
                take_self(0, k % 2, v)
                if has_next:
                    open_hi(np_, v + 1)
                take_self(1, k % 2, v)
                if k < 2:
                    keep_x(it, k, v)
                if k < 2 and not first(it):
                    output(it - 1, k)
                if first(it) and k % 2 == 0 and k // 2 < L - 1:
                    split_weights(k // 2 + 1)

            def last():
                norm(NIT - 1, L - 1, 1, n * NIT - 1)
                output(NIT - 1, 0)
                output(NIT - 1, 1)

            open_visit(0, 0)
            open_hi(0, 0)
            split_weights(0)
            act.wait_ge(c_loaded, 16 * CONSTS)
            halves(act, L, half, last)

        @block.vector
        def _(dve):
            dve.memset(v_hi[:, :, :, H:HE].bitcast(F32), 1.0).then_inc(dconst, 1)
            dve.memset(v_lo[:, :, :, H:HE].bitcast(F32), 0.0).then_inc(dconst, 1)

            def split_weights(l):
                for w in range(3 * l, 3 * l + 3):
                    dve.wait_ge(w_hi_done, w + 1)
                    dve.tensor_tensor(w_lo[:, w], raw[:, w], w_hi[:, w].bitcast(F32), ALU.subtract).then_inc(w_ready, 1)

            def adjacency_diagonal(it, l, p):
                if l == 0:
                    dve.wait_ge(mask_ready, 2 * it + p + 1)
                    for b in range(GB):
                        dve.tensor_tensor_reduce(junk_adj[:, b], adjin[p][:, b], ident[:], 1.0, 0.0, ALU.mult, ALU.add,
                                                 adj_d[p][:, b:b + 1]).then_inc(adjd_ready, 1)

            def open_visit(p, v):
                dve.wait_ge(hh_ready, v + 1)
                dve.tensor_tensor(h_lo[p][:], h_f[:], h_hi[p][:].bitcast(F32), ALU.subtract).then_inc(h_ready, 1)

            def row_max(it, l, p, v):
                c = ML * 2 * it + 2 * (l - 1) + p
                dve.wait_ge(us_ready, v + 1)
                dve.tensor_reduce(mx[:], us[:, 0], AX_X, ALU.max).then_inc(mx_ready, 1)
                dve.wait_ge(mx_ready, c + 1)
                dve.tensor_scalar(nb[:], mx[:], -1.0 / TEMPER, None, ALU.mult).then_inc(nb_ready, 1)

            def diagonal(it, p, v):
                dve.wait_ge(e_ready, GB * (v + 1))
                for b in range(GB):
                    dve.tensor_tensor_reduce(junk[:, b], e_s[:, b], ident[:], 1.0, 0.0, ALU.mult, ALU.add,
                                             diag[:, b:b + 1]).then_inc(diag_ready, 1)
                dve.wait_ge(diag_ready, GB * (v + 1))
                dve.wait_ge(adjd_ready, GB * (2 * it + p + 1))
                dve.tensor_tensor(dself[p][:], diag[:], adj_d[p][:], ALU.mult).then_inc(d_ready, 1)

            def take_f32(j, l, v):
                dve.wait_ge(pj_ready, JOBS * v + j + 1)
                dve.tensor_tensor(v_f[:, j // 2, j % 2], pj[:, j % RING, 0:H], v_bias[:, 3 * l + j % 2],
                                  ALU.add).then_inc(f32_taken, 1)

            def take_lo(j, v):
                dve.wait_ge(hi_ready, LO_JOBS * v + j + 1)
                dve.tensor_tensor(v_lo[:, j // 2, j % 2, 0:H], v_f[:, j // 2, j % 2],
                                  v_hi[:, j // 2, j % 2, 0:H].bitcast(F32), ALU.subtract).then_inc(lo_ready, 1)

            def take_attention(v):
                dve.wait_ge(ah_ready, v + 1)
                dve.tensor_tensor(a_lo[:], au[:], a_hi[:].bitcast(F32), ALU.subtract).then_inc(a_ready, 1)

            def close_sums(p, v):
                dve.wait_ge(cx_ready, v + 1)
                dve.scalar_tensor_tensor(part[:].unsqueeze(2), esum[p][:].unsqueeze(2), 1e-10, cx[:, :, H:H + 1],
                                         ALU.mult, ALU.add).then_inc(part_ready, 1)
                after(dve, tn_ready, v)
                for b in range(GB):
                    dve.wait_ge(own_ready, GB * v + b + 1)
                    dve.tensor_tensor(cn[:, b], cx[:, b, 0:H], own[:, b], ALU.add).then_inc(cn_ready, 1)
                dve.wait_ge(part_ready, v + 1)
                dve.tensor_tensor(den[:], part[:], dself[p][:], ALU.add).then_inc(den_ready, 1)
                dve.wait_ge(den_ready, v + 1)
                dve.scalar_tensor_tensor(dd[:], den[:], 1e-12, den[:], ALU.mult, ALU.mult).then_inc(dd_ready, 1)

            def close_stats(v):
                for b in range(GB):
                    dve.wait_ge(cn_ready, GB * v + b + 1)
                    dve.bn_stats(stats[:, b], cn[:, b]).then_inc(st_ready, 1)

            def close_variance(v):
                dve.wait_ge(st_ready, GB * (v + 1))
                dve.sem_inc(dve_gate, 1)
                for b in range(GB):
                    dve.bn_aggr(mv[:, b], stats[:, b]).then_inc(mv_ready, 1)
                dve.wait_ge(mv_ready, GB * (v + 1))
                dve.wait_ge(dd_ready, v + 1)
                dve.tensor_tensor(vs[:].unsqueeze(2), mv[:, :, 1:2], dd[:].unsqueeze(2), ALU.add).then_inc(vs_ready, 1)

            def shift(v):
                dve.wait_ge(rr_ready, v + 1)
                dve.scalar_tensor_tensor(nm[:].unsqueeze(2), mv[:, :, 0:1], -1.0, rr[:].unsqueeze(2), ALU.mult,
                                         ALU.mult).then_inc(nm_ready, 1)

            def residual(it, p):
                g = 2 * it + p
                after(dve, o_ready, g - 1)
                dve.wait_ge(xin_free[p], it + 1)
                dve.wait_ge(t3_ready, g + 1)
                dve.scalar_tensor_tensor(y[p][:], t3[:], 0.0, xres[p][:], ALU.max, ALU.add).then_inc(y_ready, 1)

            def out_stats(it, p):
                dve.wait_ge(y_ready, 2 * it + p + 1)
                for b in range(GB):
                    dve.bn_stats(ystats[:, b], y[p][:, b]).then_inc(yst_ready, 1)

            def out_variance(it, p):
                g = 2 * it + p
                dve.wait_ge(yst_ready, GB * (g + 1))
                dve.sem_inc(dve_gate, 1)
                for b in range(GB):
                    dve.bn_aggr(ymv[:, b], ystats[:, b]).then_inc(ymv_ready, 1)
                dve.wait_ge(ymv_ready, GB * (g + 1))
                dve.tensor_scalar(yv[:].unsqueeze(2), ymv[:, :, 1:2], 1e-5, None, ALU.add).then_inc(yv_ready, 1)

            def out_shift(it, p):
                g = 2 * it + p
                dve.wait_ge(yr_ready, g + 1)
                dve.scalar_tensor_tensor(ynm[p][:].unsqueeze(2), ymv[:, :, 0:1], -1.0, yr[p][:].unsqueeze(2), ALU.mult,
                                         ALU.mult).then_inc(ynm_ready, 1)

            def half(it, k, has_prev, has_next):
                v = n * it + k
                l, p = k // 2, k % 2
                pi, pl, pp = prev_of(it, k)
                ni, nl, np_ = next_of(it, k)
                done = k < 2 and not first(it)
                if has_prev:
                    close_sums(pp, v - 1)
                    close_stats(v - 1)
                take_f32(0, l, v)
                if has_prev:
                    close_variance(v - 1)
                if l:
                    row_max(it, l, p, v)
                if done:
                    out_stats(it - 1, k)
                if has_prev:
                    shift(v - 1)
                diagonal(it, p, v)
                take_f32(1, l, v)
                if done:
                    out_variance(it - 1, k)
                take_f32(2, l, v)
                take_lo(0, v)
                take_lo(1, v)
                take_f32(3, l, v)
                take_lo(2, v)
                take_attention(v)
                take_lo(3, v)
                if done:
                    out_shift(it - 1, k)
                if has_next:
                    open_visit(np_, v + 1)
                if has_prev and pl == L - 1:
                    residual(pi, pp)
                if has_next:
                    adjacency_diagonal(ni, nl, np_)
                if first(it) and k % 2 == 0 and l < L - 1:
                    split_weights(l + 1)

            def last():
                close_sums(1, n * NIT - 1)
                close_stats(n * NIT - 1)
                close_variance(n * NIT - 1)
                shift(n * NIT - 1)
                out_stats(NIT - 1, 0)
                out_variance(NIT - 1, 0)
                out_shift(NIT - 1, 0)
                g = 2 * NIT - 1
                dve.wait_ge(tn_ready, n * NIT)
                dve.wait_ge(t3_ready, g)
                dve.tensor_tensor(t2[:], tn[:], g_row[:].unsqueeze(1).broadcast_to([P, GB, H]), ALU.mult).then_inc(t2_ready, 1)
                dve.wait_ge(t2_ready, g + 1)
                dve.tensor_tensor(t3[:], t2[:], b_row[:].unsqueeze(1).broadcast_to([P, GB, H]), ALU.add).then_inc(t3_ready, 1)
                residual(NIT - 1, 1)
                out_stats(NIT - 1, 1)
                out_variance(NIT - 1, 1)
                out_shift(NIT - 1, 1)

            adjacency_diagonal(0, 0, 0)
            open_visit(0, 0)
            split_weights(0)
            dve.wait_ge(c_loaded, 16 * CONSTS)
            halves(dve, L, half, last)

        @block.tensor
        def _(pe):
            def open_visit(it, l, p, v):
                if l == 0:
                    pe.wait_ge(x_loaded[p], base + 16 * it + 16)
                    src = xin[p]
                else:
                    pe.wait_ge(tn_ready, v - 1)
                    src = tn
                for b in range(GB):
                    for c in range(KC):
                        i = pe.transpose(tp[:, b, c * P:(c + 1) * P], src[:, b, c * P:(c + 1) * P], ident[:])
                i.then_inc(tp_ready, 1)

            def scores(v):
                pe.wait_ge(f_ready, v + 1)
                after(pe, e_ready, GB * v)
                for b in range(GB):
                    for c in range(KC):
                        i = pe.matmul(us[:, 0, b], h_f[:, c, b], h_f[:, c, b], start=(c == 0), stop=(c == KC - 1))
                i.then_inc(us_ready, 1)

            def transpose_exps(it, l, p, v):
                pe.wait_ge(e_ready, GB * (v + 1))
                after(pe, et_taken, ML * 2 * it + 2 * (l - 1) + p)
                for b in range(GB):
                    i = pe.transpose(us[:, 1, b], e_s[:, b], ident[:])
                i.then_inc(et_ready, 1)

            def project(j, it, l, p, v):
                if j == 0:
                    pe.wait_ge(h_ready, v + 1)
                if j in (1, 2):
                    after(pe, self_taken, GB * (v - 1) + j)
                else:
                    after(pe, f32_taken, LO_JOBS * v + (j - RING + 1 if j else 0))
                b, s = (j // 2, j % 2) if j < LO_JOBS else (j - LO_JOBS, 2)
                if first(it):
                    pe.wait_ge(w_ready, 3 * l + s + 1)
                w = 3 * l + s
                split_product(
                    pe, pj[:, j % RING, 0:H], [h_hi[p][:, c, b] for c in range(KC)], [h_lo[p][:, c, b] for c in range(KC)],
                    [w_hi[:, w, c] for c in range(KC)], [w_lo[:, w, c] for c in range(KC)]).then_inc(pj_ready, 1)

            def attend(v):
                after(pe, cn_ready, GB * v)
                pe.wait_ge(a_ready, v + 1)
                if first(v):
                    pe.wait_ge(dconst, 2)
                for b in range(GB):
                    pe.wait_ge(lo_ready, LO_JOBS * v + 2 * (b + 1))
                    i = split_product(pe, cx[:, b, 0:HE], [a_hi[:, b, s] for s in range(2)], [a_lo[:, b, s] for s in range(2)],
                                      [v_hi[:, b, s] for s in range(2)], [v_lo[:, b, s] for s in range(2)])
                i.then_inc(cx_ready, 1)

            def half(it, k, has_prev, has_next):
                v = n * it + k
                l, p = k // 2, k % 2
                ni, nl, np_ = next_of(it, k)
                scores(v)
                project(0, it, l, p, v)
                project(1, it, l, p, v)
                project(2, it, l, p, v)
                if l:
                    transpose_exps(it, l, p, v)
                project(3, it, l, p, v)
                if has_next:
                    open_visit(ni, nl, np_, v + 1)
                for j in range(4, JOBS):
                    project(j, it, l, p, v)
                attend(v)

            open_visit(0, 0, 0, 0)
            halves(pe, L, half, lambda: None)


def mha_phase(nc, x_in, adj, b_v, b_o, shared, next_weights, next_adj, x_out):
    n = 2
    HEADS = 12
    D = H // HEADS
    R = P // D
    SCALE = float(H) ** -0.5
    HJ = HEADS // 3
    with ExitStack() as ctx:
        m = Memory(nc, ctx, "mh_")
        raw, ident, mhalf_c = shared.raw, shared.ident, shared.mhalf_c
        w_count = list(shared.loads)
        w_hi = m.sb("w_hi", [4, KC, H], F32R)
        w_lo = m.sb("w_lo", [4, KC, H], F32R)
        bv_row = m.sb("bv_row", [H])
        bo_row = m.sb("bo_row", [H])
        xin, adjin, o = shared.xin, shared.adjin, shared.o
        x_loaded, adj_loaded, stored = shared.x_loaded, shared.adj_loaded, shared.stored
        base = shared.enter()
        xres = [m.sb(f"xres{p}", [GB, H]) for p in range(2)]
        h_f = m.sb("h_f", [KC, GB, S])
        h_hi = m.sb("h_hi", [KC, GB, S], F32R)
        h_lo = m.sb("h_lo", [KC, GB, S], F32R)
        qk = m.sb("qk", [KC, 2, GB, S])
        v_s = [m.sb(f"v_s{p}", [GB, H]) for p in range(2)]
        a_s = [m.sb(f"a_s{b}", [HEADS, S]) for b in range(GB)]
        e_s = [m.sb(f"e_s{b}", [HEADS, S]) for b in range(GB)]
        mx = [m.sb(f"mx{b}", [HEADS]) for b in range(GB)]
        mn = [m.sb(f"mn{b}", [HEADS]) for b in range(GB)]
        nb = [m.sb(f"nb{b}", [HEADS]) for b in range(GB)]
        zero = [m.sb(f"zero{b}", [HEADS]) for b in range(GB)]
        pad = [m.sb(f"pad{b}", [HEADS]) for b in range(GB)]
        keep = [m.sb(f"keep{b}", [HEADS]) for b in range(GB)]
        esum = [m.sb(f"esum{b}", [HEADS]) for b in range(GB)]
        rec = m.sb("rec", [HEADS])
        rd = [m.sb(f"rd{b}", [HEADS]) for b in range(GB)]
        at = m.sb("at", [HEADS, S])
        o_hi = m.sb("o_hi", [KC, S], F32R)
        o_lo = m.sb("o_lo", [KC, S], F32R)
        y = m.sb("y", [GB, H])
        ystats = m.sb("ystats", [GB, BN])
        ymv = m.sb("ymv", [GB, 2])
        yv = m.sb("yv", [GB])
        yr = m.sb("yr", [GB])

        ra = m.ps("ra", [2, 512])
        rb = m.ps("rb", [2, 512])
        sc = m.ps("sc", [R, 512])

        c_loaded = m.sem("c_loaded")
        w_hi_done = m.sem("w_hi_done")
        w_ready = m.sem("w_ready")
        dve_gate = m.sem("dve_gate")
        xin_free = [m.sem(f"xin_free{p}") for p in range(2)]
        tp_ready = m.sem("tp_ready")
        f_ready = m.sem("f_ready")
        hh_ready = m.sem("hh_ready")
        h_ready = m.sem("h_ready")
        qk_done = m.sem("qk_done")
        qk_taken = m.sem("qk_taken")
        v_done = m.sem("v_done")
        v_taken = m.sem("v_taken")
        sc_ready = m.sem("sc_ready")
        a_ready = m.sem("a_ready")
        mx_ready = m.sem("mx_ready")
        nb_ready = m.sem("nb_ready")
        mn_ready = m.sem("mn_ready")
        zero_ready = m.sem("zero_ready")
        pad_ready = m.sem("pad_ready")
        keep_ready = m.sem("keep_ready")
        e_ready = m.sem("e_ready")
        rec_ready = m.sem("rec_ready")
        rd_ready = m.sem("rd_ready")
        p_ready = m.sem("p_ready")
        et_done = m.sem("et_done")
        et_taken = m.sem("et_taken")
        av_done = m.sem("av_done")
        oh_ready = m.sem("oh_ready")
        av_taken = m.sem("av_taken")
        wo_done = m.sem("wo_done")
        wo_taken = m.sem("wo_taken")
        yst_ready = m.sem("yst_ready")
        ymv_ready = m.sem("ymv_ready")
        yv_ready = m.sem("yv_ready")
        yr_ready = m.sem("yr_ready")
        o_ready = m.sem("o_ready")

        block = ctx.enter_context(nc.Block())

        def a_bank(job, k):
            return ra[:, (job + k) % 2, :]

        def e_bank(i):
            return rb[:, (i if i < 3 else i + 1) % 2, :]

        def v_bank():
            return rb[:, 1, :]

        def prev_of(it, k):
            return (it, 0) if k else (it - 1, 1)

        def next_of(it, k):
            return (it, 1) if k == 0 else (it + 1, 0)

        @block.sync
        def _(sp):

            def load_x(it, p, x=x_in, at=None):
                after(sp, xin_free[p], it)
                at = (2 * it + p) * GB if at is None else at
                sp.dma_start(xin[p][:], x[bass.ds(at, GB)].rearrange("b s h -> s b h")).then_inc(x_loaded[p], 16)

            def load_adj(it, p, a=adj, at=None):
                after(sp, a_ready, GB * R * (2 * it + p - 1))
                at = (2 * it + p) * GB if at is None else at
                sp.dma_start(adjin[p][:], a[bass.ds(at, GB)].rearrange("b s t -> s b t")).then_inc(adj_loaded[p], 16)

            def store(it, p):
                sp.wait_ge(o_ready, 2 * it + p + 1)
                g = (2 * it + p) * GB
                sp.dma_start(x_out[bass.ds(g, GB)].rearrange("b s h -> s b h"), o[p][:]).then_inc(stored[p], 16)

            sp.dma_start(bv_row[:], b_v.partition_broadcast(P)).then_inc(c_loaded, 16)
            sp.dma_start(bo_row[:], b_o.partition_broadcast(P)).then_inc(c_loaded, 16)
            for p in range(2):
                load_x(1, p)
                load_adj(1, p)
            sp.wait_ge(w_ready, 4)
            shared.load(sp, next_weights)
            with sp.Fori(1, NIT - 1) as it:
                for p in range(2):
                    load_x(it + 1, p)
                    store(it - 1, p)
                    load_adj(it + 1, p)
            for p in range(2):
                sp.wait_ge(stored[p], base + 32)
                load_x(NIT, p, x_out, GB * p)
                store(NIT - 2, p)
                load_adj(NIT, p, next_adj, GB * p)
            for p in range(2):
                store(NIT - 1, p)

        @block.gpsimd
        def _(pool):
            def normalise(b, v):
                pool.wait_ge(rd_ready, GB * v + b + 1)
                for i in range(3):
                    heads = slice(HJ * i, HJ * (i + 1))
                    pool.tensor_tensor(a_s[b][:, heads], e_s[b][:, heads],
                                       rd[b][:, heads].unsqueeze(2).broadcast_to([P, HJ, S]), ALU.mult).then_inc(p_ready, 1)

            def out_norm(v):
                pool.wait_ge(yv_ready, v + 1)
                pool.tensor_tensor(yr[:], yv[:], mhalf_c[:], ALU.pow).then_inc(yr_ready, 1)

            def half(it, k, has_prev, has_next):
                v = n * it + k
                if has_prev:
                    normalise(0, v - 1)
                if not first(it):
                    out_norm(v - 2)
                if has_prev:
                    normalise(1, v - 1)

            def last():
                v = n * NIT - 1
                normalise(0, v)
                out_norm(v - 1)
                normalise(1, v)
                out_norm(v)

            halves(pool, 1, half, last)

        @block.scalar
        def _(act):
            def split_weights(*slots):
                for w in slots:
                    act.wait_ge(shared.loaded[w], 16 * w_count[w])
                    act.activation(w_hi[:, w], raw[:, w], ACT.Copy).then_inc(w_hi_done, 1)

            def open_visit(b, v, k):
                act.wait_ge(tp_ready, GB * v + b + 1)
                after(act, h_ready, GB * (v - 1) + b + 1)
                act.activation(h_f[:, :, b, :], a_bank(5 + 2 * b, k)[:, 0:H].rearrange("p (c s) -> p c s", c=KC),
                               ACT.Copy).then_inc(f_ready, 1)

            def take_qk(c, k, v):
                act.wait_ge(qk_done, KC * v + c + 1)
                act.activation(qk[:, c], a_bank(c, k).rearrange("p (w b s) -> p w b s", w=2, b=GB),
                               ACT.Copy).then_inc(qk_taken, 1)

            def take_e(b, parts, v):
                for i in parts:
                    act.wait_ge(et_done, 3 * (GB * v + b) + i + 1)
                    act.activation(at[:, HJ * i:HJ * (i + 1)], e_bank(3 * b + i).rearrange("p (h s) -> p h s", h=HJ),
                                   ACT.Copy).then_inc(et_taken, 1)

            def take_o(b, k, v):
                act.wait_ge(av_done, GB * v + b + 1)
                act.activation(o_hi[:], a_bank(3 + 3 * b, k)[:, 0:H].rearrange("p (c s) -> p c s", c=KC),
                               ACT.Copy).then_inc(oh_ready, 1)

            def exps(part, b, v):
                if part == 0:
                    act.wait_ge(nb_ready, GB * v + b + 1)
                for h in range(HJ * part, HJ * (part + 1)):
                    act.activation(e_s[b][:, h], a_s[b][:, h], ACT.Exp, bias=nb[b][:, h:h + 1],
                                   accum_out=esum[b][:, h:h + 1]).then_inc(e_ready, 1)

            def half(it, k, has_prev, has_next):
                v = n * it + k
                take_qk(0, k, v)
                take_qk(1, k, v)
                if has_prev:
                    take_e(0, (0, 1), v - 1)
                    exps(0, 1, v - 1)
                take_qk(2, k, v)
                if has_prev:
                    take_e(0, (2,), v - 1)
                    exps(1, 1, v - 1)
                    exps(2, 1, v - 1)
                    take_o(0, k, v - 1)
                    take_e(1, (0, 1, 2), v - 1)
                if has_next:
                    open_visit(0, v + 1, k)
                exps(0, 0, v)
                if has_prev:
                    take_o(1, k, v - 1)
                if has_next:
                    open_visit(1, v + 1, k)
                exps(1, 0, v)
                exps(2, 0, v)

            def last():
                v = n * NIT - 1
                exps(0, 1, v)
                take_e(0, (0, 1, 2), v)
                exps(1, 1, v)
                exps(2, 1, v)
                take_o(0, 0, v)
                take_e(1, (0, 1, 2), v)
                take_o(1, 0, v)

            for b in range(GB):
                open_visit(b, 0, -1)
            split_weights(0, 1, 2, 3)
            halves(act, 1, half, last)

        @block.vector
        def _(dve):

            def open_visit(b, v):
                dve.wait_ge(f_ready, GB * v + b + 1)
                dve.tensor_copy(h_hi[:, :, b], h_f[:, :, b]).then_inc(hh_ready, 1)
                dve.wait_ge(hh_ready, GB * v + b + 1)
                dve.tensor_tensor(h_lo[:, :, b], h_f[:, :, b], h_hi[:, :, b].bitcast(F32), ALU.subtract).then_inc(h_ready, 1)

            def keep_x(it, p, v):
                dve.wait_ge(x_loaded[p], base + 16 * it + 16)
                dve.wait_ge(tp_ready, GB * (v + 1))
                dve.tensor_tensor(xres[p][:], xin[p][:], bo_row[:].unsqueeze(1).broadcast_to([P, GB, H]),
                                  ALU.add).then_inc(xin_free[p], 1)

            def take_v(b, p, v):
                dve.wait_ge(v_done, GB * v + b + 1)
                dve.tensor_tensor(v_s[p][:, b], v_bank()[:, 0:H], bv_row[:], ALU.add).then_inc(v_taken, 1)

            def scale_scores(it, b, p, v):
                dve.wait_ge(adj_loaded[p], base + 16 * it + 16)
                dve.wait_ge(sc_ready, GB * v + b + 1)
                for r in range(R):
                    dve.scalar_tensor_tensor(a_s[b][:, KC * r:KC * (r + 1)], sc[:, r, 0:KC * S].rearrange("p (c s) -> p c s", c=KC),
                                             SCALE, adjin[p][:, b].unsqueeze(1).broadcast_to([P, KC, S]),
                                             ALU.mult, ALU.add).then_inc(a_ready, 1)

            def find_max(b, v):
                dve.wait_ge(a_ready, R * (GB * v + b + 1))
                dve.tensor_reduce(mx[b][:], a_s[b][:], AX_X, ALU.max).then_inc(mx_ready, 1)
                dve.wait_ge(mx_ready, GB * v + b + 1)
                dve.tensor_scalar(nb[b][:], mx[b][:], -1.0, None, ALU.mult).then_inc(nb_ready, 1)

            def find_pads(b, v):
                u = GB * v + b
                dve.tensor_reduce(mn[b][:], a_s[b][:], AX_X, ALU.min).then_inc(mn_ready, 1)
                dve.wait_ge(mn_ready, u + 1)
                dve.tensor_scalar(zero[b][:], mn[b][:], 0.0, None, ALU.is_equal).then_inc(zero_ready, 1)
                dve.wait_ge(zero_ready, u + 1)
                dve.scalar_tensor_tensor(pad[b][:], mx[b][:], 0.0, zero[b][:], ALU.is_equal, ALU.mult).then_inc(pad_ready, 1)
                dve.wait_ge(pad_ready, u + 1)
                dve.tensor_scalar(keep[b][:], pad[b][:], -1.0, 1.0, ALU.mult, ALU.add).then_inc(keep_ready, 1)

            def sums(b, v):
                u = GB * v + b
                dve.wait_ge(e_ready, HEADS * (u + 1))
                dve.reciprocal(rec[:], esum[b][:]).then_inc(rec_ready, 1)
                dve.wait_ge(rec_ready, u + 1)
                dve.wait_ge(keep_ready, u + 1)
                dve.tensor_tensor(rd[b][:], rec[:], keep[b][:], ALU.mult).then_inc(rd_ready, 1)

            def take_o(b, k, v):
                dve.wait_ge(oh_ready, GB * v + b + 1)
                dve.tensor_tensor(o_lo[:], a_bank(3 + 3 * b, k)[:, 0:H].rearrange("p (c s) -> p c s", c=KC),
                                  o_hi[:].bitcast(F32), ALU.subtract).then_inc(av_taken, 1)

            def add_x(it, b, p, k, v):
                u = GB * v + b
                dve.wait_ge(wo_done, u + 1)
                dve.wait_ge(xin_free[p], it + 1)
                dve.tensor_tensor(y[:, b], a_bank(4 + 4 * b, k)[:, 0:H], xres[p][:, b], ALU.add).then_inc(wo_taken, 1)

            def out_stats(b, v):
                u = GB * v + b
                dve.wait_ge(wo_taken, u + 1)
                dve.bn_stats(ystats[:, b], y[:, b]).then_inc(yst_ready, 1)
                dve.wait_ge(yst_ready, u + 1)
                dve.sem_inc(dve_gate, 1)
                dve.bn_aggr(ymv[:, b], ystats[:, b]).then_inc(ymv_ready, 1)

            def variance(v):
                dve.wait_ge(ymv_ready, GB * (v + 1))
                dve.tensor_scalar(yv[:].unsqueeze(2), ymv[:, :, 1:2], 1e-5, None, ALU.add).then_inc(yv_ready, 1)

            def output(it, p):
                g = 2 * it + p
                dve.wait_ge(yr_ready, g + 1)
                dve.wait_ge(stored[p], base + 16 * it + 16)
                for b in range(GB):
                    i = dve.tensor_scalar(o[p][:, b], y[:, b], ymv[:, b, 0:1], yr[:, b:b + 1], ALU.subtract, ALU.mult)
                i.then_inc(o_ready, 1)

            def half(it, k, has_prev, has_next):
                v = n * it + k
                pi, pp = prev_of(it, k)
                ni, np_ = next_of(it, k)
                if has_prev:
                    find_pads(1, v - 1)
                if not first(it):
                    output(it - 1, k)
                take_v(0, k, v)
                if has_prev:
                    sums(1, v - 1)
                    take_o(0, k, v - 1)
                scale_scores(it, 0, k, v)
                find_max(0, v)
                if has_prev:
                    add_x(pi, 0, pp, k, v - 1)
                    out_stats(0, v - 1)
                take_v(1, k, v)
                if has_next:
                    open_visit(0, v + 1)
                if has_prev:
                    take_o(1, k, v - 1)
                if has_next:
                    open_visit(1, v + 1)
                find_pads(0, v)
                sums(0, v)
                if has_prev:
                    add_x(pi, 1, pp, k, v - 1)
                scale_scores(it, 1, k, v)
                find_max(1, v)
                if has_prev:
                    out_stats(1, v - 1)
                    variance(v - 1)
                if has_next:
                    keep_x(ni, np_, v + 1)

            def last():
                v = n * NIT - 1
                find_pads(1, v)
                output(NIT - 1, 0)
                sums(1, v)
                take_o(0, 0, v)
                add_x(NIT - 1, 0, 1, 0, v)
                out_stats(0, v)
                take_o(1, 0, v)
                add_x(NIT - 1, 1, 1, 0, v)
                out_stats(1, v)
                variance(v)
                output(NIT - 1, 1)

            for b in range(GB):
                open_visit(b, 0)
            for w in range(4):
                dve.wait_ge(w_hi_done, w + 1)
                dve.tensor_tensor(w_lo[:, w], raw[:, w], w_hi[:, w].bitcast(F32), ALU.subtract).then_inc(w_ready, 1)
            dve.wait_ge(c_loaded, 16 * 2)
            keep_x(0, 0, 0)
            halves(dve, 1, half, last)

        @block.tensor
        def _(pe):
            def open_visit(it, b, p, v, k):
                if b == 0:
                    pe.wait_ge(x_loaded[p], base + 16 * it + 16)
                    after(pe, qk_taken, KC * v)
                    after(pe, av_taken, GB * (v - 2) + 1)
                else:
                    pe.wait_ge(f_ready, GB * v + 1)
                for c in range(KC):
                    i = pe.transpose(a_bank(5 + 2 * b, k)[:, c * P:(c + 1) * P], xin[p][:, b, c * P:(c + 1) * P], ident[:])
                i.then_inc(tp_ready, 1)

            def project_qk(c, k, v):
                if first(v):
                    pe.wait_ge(w_ready, 2)
                if c == 0:
                    pe.wait_ge(h_ready, GB * (v + 1))
                elif c == 1:
                    after(pe, wo_taken, GB * (v - 1))
                else:
                    pe.wait_ge(qk_taken, KC * v + 1)
                for w in range(2):
                    i = split_product(
                        pe, a_bank(c, k)[:, w * GB * S:(w + 1) * GB * S],
                        [w_hi[:, w, i, c * P:(c + 1) * P] for i in range(KC)],
                        [w_lo[:, w, i, c * P:(c + 1) * P] for i in range(KC)],
                        [h_hi[:, i].rearrange("p b s -> p (b s)") for i in range(KC)],
                        [h_lo[:, i].rearrange("p b s -> p (b s)") for i in range(KC)])
                i.then_inc(qk_done, 1)

            def project_v(b, v, has_prev):
                if has_prev:
                    pe.wait_ge(et_taken, 6 * (v - 1) + 3 * b + 2)
                else:
                    after(pe, v_taken, GB * v + b)
                if first(v):
                    pe.wait_ge(w_ready, 3)
                split_product(pe, v_bank()[:, 0:H], [h_hi[:, c, b] for c in range(KC)], [h_lo[:, c, b] for c in range(KC)],
                              [w_hi[:, 2, c] for c in range(KC)], [w_lo[:, 2, c] for c in range(KC)]).then_inc(v_done, 1)

            def scores(b, v):
                pe.wait_ge(qk_taken, KC * (v + 1))
                after(pe, a_ready, R * (GB * v + b))
                for c in range(KC):
                    for r in range(R):
                        q = slice(D * r, D * (r + 1))
                        i = pe.matmul(sc[:, r, c * S:(c + 1) * S], qk[q, c, 0, b], qk[q, c, 1, b], start=True, stop=True)
                i.then_inc(sc_ready, 1)

            def transpose_attention(b, parts, v, projects):
                for i in parts:
                    pe.wait_ge(p_ready, 3 * (GB * v + b) + i + 1)
                    if (b, i) == (0, 0):
                        after(pe, et_taken, 6 * v)
                    elif (b, i) == (0, 1):
                        pe.wait_ge(v_taken, GB * (v + 1))
                    elif (b, i) == (1, 1) and projects:
                        pe.wait_ge(v_taken, GB * (v + 1) + 1)
                    else:
                        pe.wait_ge(et_taken, 6 * v + 3 * b + i - (1 if b == 0 or i != 0 else 0))
                    for h in range(HJ):
                        t = pe.transpose(e_bank(3 * b + i)[:, h * S:(h + 1) * S], a_s[b][:, HJ * i + h], ident[:])
                    t.then_inc(et_done, 1)

            def attend(b, p, k, v, projects):
                pe.wait_ge(et_taken, 6 * v + 3 * b + 3)
                if b == 0:
                    if projects:
                        pe.wait_ge(qk_taken, KC * (v + 1) + 2)
                    else:
                        after(pe, wo_taken, GB * v)
                        after(pe, av_taken, GB * v)
                else:
                    pe.wait_ge(wo_taken, GB * v + 1)
                out = a_bank(3 + 3 * b, k)
                for c in range(KC):
                    for r in range(R):
                        h = R * c + r
                        i = pe.matmul(out[D * r:D * (r + 1), c * S:(c + 1) * S], v_s[p][:, b, h * D:(h + 1) * D],
                                      at[:, KC * r + c], start=True, stop=True)
                i.then_inc(av_done, 1)

            def project_out(b, k, v, projects):
                pe.wait_ge(av_taken, GB * v + b + 1)
                if first(v):
                    pe.wait_ge(w_ready, 4)
                if b == 0 and projects:
                    pe.wait_ge(qk_taken, KC * (v + 2))
                split_product(pe, a_bank(4 + 4 * b, k)[:, 0:H], [o_hi[:, c] for c in range(KC)], [o_lo[:, c] for c in range(KC)],
                              [w_hi[:, 3, c] for c in range(KC)], [w_lo[:, 3, c] for c in range(KC)]).then_inc(wo_done, 1)

            def half(it, k, has_prev, has_next):
                v = n * it + k
                pi, pp = prev_of(it, k)
                ni, np_ = next_of(it, k)
                project_qk(0, k, v)
                project_qk(1, k, v)
                if has_prev:
                    transpose_attention(0, (0, 1), v - 1, True)
                project_qk(2, k, v)
                if has_prev:
                    transpose_attention(0, (2,), v - 1, True)
                project_v(0, v, has_prev)
                if has_prev:
                    attend(0, pp, k, v - 1, True)
                scores(0, v)
                if has_prev:
                    project_out(0, k, v - 1, True)
                    transpose_attention(1, (0, 1), v - 1, True)
                if has_next:
                    open_visit(ni, 0, np_, v + 1, k)
                if has_prev:
                    transpose_attention(1, (2,), v - 1, True)
                project_v(1, v, has_prev)
                if has_prev:
                    attend(1, pp, k, v - 1, True)
                if has_next:
                    open_visit(ni, 1, np_, v + 1, k)
                scores(1, v)
                if has_prev:
                    project_out(1, k, v - 1, True)

            def last():
                v = n * NIT - 1
                transpose_attention(0, (0, 1, 2), v, False)
                attend(0, 1, 0, v, False)
                project_out(0, 0, v, False)
                transpose_attention(1, (0, 1, 2), v, False)
                attend(1, 1, 0, v, False)
                project_out(1, 0, v, False)

            for b in range(GB):
                open_visit(0, b, 0, 0, -1)
            halves(pe, 1, half, last)


def build(nc, a):
    x1, x2, x3 = (nc.dram_tensor(f"x_{i}", (B, S, H), F32).ap() for i in (1, 2, 3))
    adj_t = nc.dram_tensor("adj_t", (B, S, S), F32).ap()
    w0 = [a[f"L0_gnn_W_{side}"][i] for i in range(2) for side in ("left", "right", "lin")]
    w1 = [a[f"L1_gnn_W{side}"][i] for i in range(2) for side in ("l", "r", "s")]
    w2 = [a[f"L2_gnn_W{side}"] for side in ("q", "k", "v", "o")]
    w3 = [a[f"L3_gnn_W_{side}"][0] for side in ("left", "right", "self")]
    with ExitStack() as ctx:
        shared = set_up(nc, ctx)
        gat_phase(nc, a["x"], a["adj"], a["L0_gnn_b_lin"], a["L0_gnn_ln_a"], a["L0_gnn_ln_b"],
                  a["L0_gnn_ln_a_cols"], a["L0_gnn_ln_b_cols"], shared, w0, w1, adj_t, x1, adj_t)
        digcn_phase(nc, x1, adj_t, a["L1_gnn_bl"], a["L1_gnn_bs"], a["L1_gnn_br"], a["L1_gnn_ln_w"], a["L1_gnn_ln_b"],
                    a["L1_gnn_ln_w_cols"], a["L1_gnn_ln_b_cols"], shared, w2, a["adj"], x2)
        mha_phase(nc, x2, a["adj"], a["L2_gnn_bv"], a["L2_gnn_bo"], shared, w3, adj_t, x3)
        digcn_phase(nc, x3, adj_t, a["L3_gnn_b_left"], a["L3_gnn_b_self"], a["L3_gnn_b_right"], a["L3_gnn_gamma"],
                    a["L3_gnn_beta"], a["L3_gnn_gamma_cols"], a["L3_gnn_beta_cols"], shared, [], None, a["out"])


_TURNED = ["L0_gnn_W_lin", "L1_gnn_Wl", "L1_gnn_Ws", "L1_gnn_Wr", "L2_gnn_Wq", "L2_gnn_Wk", "L2_gnn_Wv", "L2_gnn_Wo",
           "L3_gnn_W_left", "L3_gnn_W_self", "L3_gnn_W_right"]
_COLUMNS = ["L0_gnn_ln_a", "L0_gnn_ln_b", "L1_gnn_ln_w", "L1_gnn_ln_b", "L3_gnn_gamma", "L3_gnn_beta"]


def kernel(**inputs):
    import numpy as _np
    import concourse.bacc as _bacc
    from concourse import mybir as _mybir
    from concourse.bass_utils import run_bass_kernel_spmd as _run

    nc = _bacc.Bacc("TRN2", target_bir_lowering=False, num_devices=1)
    host = {}
    for name, value in inputs.items():
        value = _np.asarray(value)
        if name in _TURNED:
            value = value.swapaxes(-1, -2)
        if name.startswith("L3_"):
            value = value[None]
        host[name] = value
        if name in _COLUMNS:
            host[name + "_cols"] = value.reshape(-1, KC, P).swapaxes(1, 2)
    arrays, aps = {}, {}
    for name, value in host.items():
        value = _np.ascontiguousarray(value)
        arrays[f"in_{name}"] = value
        aps[name] = nc.dram_tensor(f"in_{name}", value.shape, _mybir.dt.from_np(value.dtype), kind="ExternalInput").ap()
    aps["out"] = nc.dram_tensor("out_x", (B, S, H), F32, kind="ExternalOutput").ap()
    build(nc, aps)
    return _run(nc, [arrays], core_ids=[0]).results[0]["out_x"]
```
